# Optimizing a Trainium2 kernel written in Bass

```python
import numpy as np
import jax
import jax.numpy as jnp

def _softmax(x, axis=-1):
    return jax.nn.softmax(x, axis=axis)

def _gelu(x):
    return jax.nn.gelu(x, approximate=True)

def _silu(x):
    return jax.nn.silu(x)

def _sigmoid(x):
    return jax.nn.sigmoid(x)

def _layernorm(x, axis=-1, eps=1e-05):
    m = jnp.mean(x, axis=axis, keepdims=True)
    v = jnp.var(x, axis=axis, keepdims=True)
    return (x - m) / jnp.sqrt(v + eps)

def _scatter_add(tgt, idx, src, axis=0):
    return tgt.at[idx].add(src)

def _segment_sum(src, seg, n):
    return jax.ops.segment_sum(src, seg, n)
kernel_name = 'mk_adaln_d4_jaxref_r8_7465a9'

def setup_inputs(seed: int=0):
    np.random.seed(seed)
    _w = jnp.asarray

    def _L0_attn_setup():
        import jax, jax.numpy as jnp
        import numpy as np
        B, S, D = (8, 256, 128)
        key = jax.random.key(seed)
        k1, k2, k3, k4 = jax.random.split(key, 4)
        return {'hidden_states': jax.random.normal(k1, (B, S, D), dtype=jnp.float32), 'w_dec_attn': jax.random.normal(k2, (D, D), dtype=jnp.float32), 'w_out': jax.random.normal(k3, (D, 2 * D), dtype=jnp.float32) * 0.02, 'b_out': jnp.zeros((D,), dtype=jnp.float32)}
    _L0_attn_in = _L0_attn_setup()

    def _L0_ffn_setup():
        import jax, jax.numpy as jnp
        import numpy as np
        D = 128
        E = 8
        K = 2
        NUM_ITER = 2
        DT = 0.1
        H = 64
        CTX = 2 * D

        def _gelu(t):
            return jax.nn.gelu(t, approximate=False)

        def _inl(ctrl, x, v, mu):
            alpha_raw, beta_raw, gate_raw = jnp.split(ctrl, 3, axis=-1)
            alpha = jax.nn.sigmoid(alpha_raw)
            beta = jax.nn.softplus(beta_raw)
            gate = jax.nn.sigmoid(gate_raw)
            error = x - mu
            v_next = alpha * v - beta * error
            x_next = x + DT * gate * v_next
            return (x_next, v_next)
        key = jax.random.key(seed)
        ks = jax.random.split(key, 20)
        s = 0.02
        inp = {'x': jax.random.normal(ks[0], (4, 512, D), jnp.float32), 'w_r1': jax.random.normal(ks[1], (D, D // 4), jnp.float32) * s, 'b_r1': jnp.zeros((D // 4,), jnp.float32), 'w_r2': jax.random.normal(ks[2], (D // 4, E), jnp.float32) * s, 'b_r2': jnp.zeros((E,), jnp.float32), 'w_h1': jax.random.normal(ks[3], (D, D // 4), jnp.float32) * s, 'b_h1': jnp.zeros((D // 4,), jnp.float32), 'w_h2': jax.random.normal(ks[4], (D // 4, 1), jnp.float32) * s, 'b_h2': jnp.zeros((1,), jnp.float32), 'expert_w1': jax.random.normal(ks[5], (E, CTX, H), jnp.float32) * s, 'expert_b1': jnp.zeros((E, H), jnp.float32), 'expert_w2': jax.random.normal(ks[6], (E, H, 3 * D), jnp.float32) * s, 'expert_b2': jnp.zeros((E, 3 * D), jnp.float32), 'w_s1': jax.random.normal(ks[7], (CTX, H), jnp.float32) * s, 'b_s1': jnp.zeros((H,), jnp.float32), 'w_s2': jax.random.normal(ks[8], (H, 3 * D), jnp.float32) * s, 'b_s2': jnp.zeros((3 * D,), jnp.float32), 'shared_weight': jnp.asarray(0.5, jnp.float32), 'w_f1': jax.random.normal(ks[9], (D, 2 * D), jnp.float32) * s, 'b_f1': jnp.zeros((2 * D,), jnp.float32), 'w_f2': jax.random.normal(ks[10], (2 * D, D), jnp.float32) * s, 'b_f2': jnp.zeros((D,), jnp.float32), 'integration_weight': jnp.full((D,), 0.5, jnp.float32), 'mu': jnp.zeros((D,), jnp.float32)}
        return inp
    _L0_ffn_in = _L0_ffn_setup()
    _L0_c = _w((lambda *s: np.random.randn(*s).astype(np.float32) * 0.05)(1, 128))
    _L0_wmod = _w((lambda *s: np.random.randn(*s).astype(np.float32) * 0.05)(128, 6 * 128) * 128 ** (-0.5))

    def _L1_attn_setup():
        import jax, jax.numpy as jnp
        import numpy as np
        HEADS = 8
        BLOCK = 32
        key = jax.random.key(seed)
        ks = jax.random.split(key, 4)
        b, n, d, f = (4, 512, 128, 128)
        x = jax.random.normal(ks[0], (b, n, d), dtype=jnp.float32)
        w_qkv = jax.random.normal(ks[1], (3 * d, d), dtype=jnp.float32) * d ** (-0.5)
        w_out = jax.random.normal(ks[2], (d, d), dtype=jnp.float32) * d ** (-0.5)
        b_out = jnp.zeros((d,), dtype=jnp.float32)
        proj = jax.random.normal(ks[3], (HEADS, d // HEADS, f), dtype=jnp.float32) * (d // HEADS) ** (-0.5)
        return {'x': x, 'w_qkv': w_qkv, 'w_out': w_out, 'b_out': b_out, 'proj': proj}
    _L1_attn_in = _L1_attn_setup()

    def _L1_ffn_setup():
        import jax, jax.numpy as jnp
        import numpy as np
        MODEL_DIM = 128
        HIDDEN = 256
        NUM_GROUPS = 2
        EXPERTS_PER_GP = 4
        NUM_EXPERTS = NUM_GROUPS * EXPERTS_PER_GP
        TOP_K = 2
        B, T = (2, 256)

        def _swiglu(x):
            a, b = jnp.split(x, 2, axis=-1)
            return jax.nn.silu(a) * b
        key = jax.random.key(seed)
        ks = jax.random.split(key, 7)
        s = 0.02
        return {'x': jax.random.normal(ks[0], (B, T, MODEL_DIM), jnp.float32), 'w_in': jax.random.normal(ks[1], (HIDDEN * 2, MODEL_DIM), jnp.float32) * s, 'w_out': jax.random.normal(ks[2], (MODEL_DIM, HIDDEN), jnp.float32) * s, 'w1': jax.random.normal(ks[3], (HIDDEN * 2, MODEL_DIM), jnp.float32) * s, 'w2': jax.random.normal(ks[4], (NUM_EXPERTS, MODEL_DIM, HIDDEN), jnp.float32) * s, 'wg': jax.random.normal(ks[5], (NUM_GROUPS, MODEL_DIM), jnp.float32) * s, 'we': jax.random.normal(ks[6], (NUM_EXPERTS, MODEL_DIM), jnp.float32) * s, 'gb': jnp.zeros((NUM_GROUPS,), jnp.float32), 'eb': jnp.zeros((NUM_EXPERTS,), jnp.float32)}
    _L1_ffn_in = _L1_ffn_setup()
    _L1_c = _w((lambda *s: np.random.randn(*s).astype(np.float32) * 0.05)(1, 128))
    _L1_wmod = _w((lambda *s: np.random.randn(*s).astype(np.float32) * 0.05)(128, 6 * 128) * 128 ** (-0.5))

    def _L2_attn_setup():
        import jax, jax.numpy as jnp
        import numpy as np
        EPS = 1e-05

        def xpos_rotate(x, offset=0, conjugate=False):
            b, s, h, dh = x.shape
            expoent = jnp.arange(0, dh, 2, dtype=jnp.float32) / dh
            angle = 10.0 ** (-4.0 * expoent)
            if conjugate:
                angle = -angle
            pos = jnp.arange(offset, s + offset, dtype=jnp.float32)
            nangle = pos[:, None] * angle[None, :]
            sin = jnp.sin(nangle)[None, :, None, :]
            cos = jnp.cos(nangle)[None, :, None, :]
            x0 = x[..., 0::2]
            x1 = x[..., 1::2]
            rot = jnp.stack([x0 * cos - x1 * sin, x0 * sin + x1 * cos], axis=-1)
            return rot.reshape(b, s, h, dh)

        def decay_mask(nseq, scale):
            idx = jnp.arange(nseq)
            diff = idx[:, None] - idx[None, :]
            mask = (diff >= 0).astype(scale.dtype)
            diff_c = jnp.maximum(diff, 0).astype(scale.dtype)
            logd = diff_c[None, :, :] * jnp.log(scale)[:, None, None]
            return jnp.exp(logd) * mask[None, :, :]

        def group_norm(R, gamma, beta, nheads):
            b, s, d = R.shape
            dh = d // nheads
            Rg = R.reshape(b, s, nheads, dh)
            mu = jnp.mean(Rg, axis=-1, keepdims=True)
            var = jnp.var(Rg, axis=-1, keepdims=True)
            Rn = (Rg - mu) * jax.lax.rsqrt(var + EPS)
            Rn = Rn * gamma.reshape(1, 1, nheads, dh) + beta.reshape(1, 1, nheads, dh)
            return Rn.reshape(b, s, d)
        key = jax.random.key(seed)
        ks = jax.random.split(key, 7)
        b, s, d, h = (2, 256, 128, 16)
        dh = d // h
        x = jax.random.normal(ks[0], (b, s, d), dtype=jnp.float32)
        std_qkv = float(np.sqrt(2.0 / (dh + d)))
        std_o = float(np.sqrt(2.0 / (d + d)))
        WQ = jax.random.normal(ks[1], (h, dh, d), dtype=jnp.float32) * std_qkv
        WK = jax.random.normal(ks[2], (h, dh, d), dtype=jnp.float32) * std_qkv
        WV = jax.random.normal(ks[3], (h, dh, d), dtype=jnp.float32) * std_qkv
        WO = jax.random.normal(ks[4], (d, d), dtype=jnp.float32) * std_o
        gamma = jnp.ones((d,), dtype=jnp.float32)
        beta = jnp.zeros((d,), dtype=jnp.float32)
        return {'x': x, 'WQ': WQ, 'WK': WK, 'WV': WV, 'WO': WO, 'gamma': gamma, 'beta': beta}
    _L2_attn_in = _L2_attn_setup()

    def _L2_ffn_setup():
        import jax, jax.numpy as jnp
        import numpy as np
        B, S, H = (4, 256, 128)
        E, K, INTER = (16, 2, 64)
        ALPHA, LIMIT = (1.702, 7.0)
        key = jax.random.key(seed)
        ks = jax.random.split(key, 6)
        return {'hidden_states': jax.random.normal(ks[0], (B, S, H), jnp.float32), 'router_weight': jax.random.normal(ks[1], (H, E), jnp.float32) * 0.02, 'gate_up_proj': jax.random.normal(ks[2], (E, H, 2 * INTER), jnp.float32) * 0.02, 'gate_up_proj_bias': jax.random.normal(ks[3], (E, 2 * INTER), jnp.float32) * 0.02, 'down_proj': jax.random.normal(ks[4], (E, INTER, H), jnp.float32) * 0.02, 'down_proj_bias': jax.random.normal(ks[5], (E, H), jnp.float32) * 0.02}
    _L2_ffn_in = _L2_ffn_setup()
    _L2_c = _w((lambda *s: np.random.randn(*s).astype(np.float32) * 0.05)(1, 128))
    _L2_wmod = _w((lambda *s: np.random.randn(*s).astype(np.float32) * 0.05)(128, 6 * 128) * 128 ** (-0.5))

    def _L3_attn_setup():
        import jax, jax.numpy as jnp
        import numpy as np
        D_MODEL = 128
        D_STATE = 16
        BATCH, SEQ = (2, 256)
        key = jax.random.key(seed)
        ks = jax.random.split(key, 16)
        D, N = (D_MODEL, D_STATE)
        s = 1.0 / np.sqrt(D)
        inp = {'x': jax.random.normal(ks[0], (BATCH, SEQ, D), dtype=jnp.float32), 'Wz': jax.random.normal(ks[1], (D, D), dtype=jnp.float32) * s, 'bz': jnp.zeros((D,), dtype=jnp.float32), 'Wx': jax.random.normal(ks[2], (D, D), dtype=jnp.float32) * s, 'bx': jnp.zeros((D,), dtype=jnp.float32), 'WB': jax.random.normal(ks[3], (D, N), dtype=jnp.float32) * s, 'bB': jnp.zeros((N,), dtype=jnp.float32), 'WC': jax.random.normal(ks[4], (D, N), dtype=jnp.float32) * s, 'bC': jnp.zeros((N,), dtype=jnp.float32), 'Wdt': jax.random.normal(ks[5], (D, D), dtype=jnp.float32) * s, 'bdt': jnp.zeros((D,), dtype=jnp.float32), 'A_log': jnp.log(jnp.broadcast_to(jnp.arange(1, N + 1, dtype=jnp.float32), (D, N))), 'Wout': jax.random.normal(ks[6], (D, D), dtype=jnp.float32) * s, 'bout': jnp.zeros((D,), dtype=jnp.float32)}
        return inp
    _L3_attn_in = _L3_attn_setup()

    def _L3_ffn_setup():
        import jax, jax.numpy as jnp
        import numpy as np
        TOP_K = 2
        key = jax.random.key(seed)
        ks = jax.random.split(key, 5)
        B, T, D, F, E = (4, 256, 128, 512, 8)
        s = 0.02
        return {'x': jax.random.normal(ks[0], (B, T, D), jnp.float32), 'gate_w': jax.random.normal(ks[1], (D, E), jnp.float32) * s, 'w1': jax.random.normal(ks[2], (E, D, F), jnp.float32) * s, 'w3': jax.random.normal(ks[3], (E, D, F), jnp.float32) * s, 'w2': jax.random.normal(ks[4], (E, F, D), jnp.float32) * s}
    _L3_ffn_in = _L3_ffn_setup()
    _L3_c = _w((lambda *s: np.random.randn(*s).astype(np.float32) * 0.05)(1, 128))
    _L3_wmod = _w((lambda *s: np.random.randn(*s).astype(np.float32) * 0.05)(128, 6 * 128) * 128 ** (-0.5))
    _d = {'L0_attn_hidden_states': _L0_attn_in['hidden_states'], 'L0_attn_w_dec_attn': _L0_attn_in['w_dec_attn'], 'L0_attn_w_out': _L0_attn_in['w_out'], 'L0_attn_b_out': _L0_attn_in['b_out'], 'L0_ffn_w_r1': _L0_ffn_in['w_r1'], 'L0_ffn_b_r1': _L0_ffn_in['b_r1'], 'L0_ffn_w_r2': _L0_ffn_in['w_r2'], 'L0_ffn_b_r2': _L0_ffn_in['b_r2'], 'L0_ffn_w_h1': _L0_ffn_in['w_h1'], 'L0_ffn_b_h1': _L0_ffn_in['b_h1'], 'L0_ffn_w_h2': _L0_ffn_in['w_h2'], 'L0_ffn_b_h2': _L0_ffn_in['b_h2'], 'L0_ffn_expert_w1': _L0_ffn_in['expert_w1'], 'L0_ffn_expert_b1': _L0_ffn_in['expert_b1'], 'L0_ffn_expert_w2': _L0_ffn_in['expert_w2'], 'L0_ffn_expert_b2': _L0_ffn_in['expert_b2'], 'L0_ffn_w_s1': _L0_ffn_in['w_s1'], 'L0_ffn_b_s1': _L0_ffn_in['b_s1'], 'L0_ffn_w_s2': _L0_ffn_in['w_s2'], 'L0_ffn_b_s2': _L0_ffn_in['b_s2'], 'L0_ffn_shared_weight': _L0_ffn_in['shared_weight'], 'L0_ffn_w_f1': _L0_ffn_in['w_f1'], 'L0_ffn_b_f1': _L0_ffn_in['b_f1'], 'L0_ffn_w_f2': _L0_ffn_in['w_f2'], 'L0_ffn_b_f2': _L0_ffn_in['b_f2'], 'L0_ffn_integration_weight': _L0_ffn_in['integration_weight'], 'L0_ffn_mu': _L0_ffn_in['mu'], 'L0_c': _L0_c, 'L0_wmod': _L0_wmod, 'L1_attn_w_qkv': _L1_attn_in['w_qkv'], 'L1_attn_w_out': _L1_attn_in['w_out'], 'L1_attn_b_out': _L1_attn_in['b_out'], 'L1_attn_proj': _L1_attn_in['proj'], 'L1_ffn_w_in': _L1_ffn_in['w_in'], 'L1_ffn_w_out': _L1_ffn_in['w_out'], 'L1_ffn_w1': _L1_ffn_in['w1'], 'L1_ffn_w2': _L1_ffn_in['w2'], 'L1_ffn_wg': _L1_ffn_in['wg'], 'L1_ffn_we': _L1_ffn_in['we'], 'L1_ffn_gb': _L1_ffn_in['gb'], 'L1_ffn_eb': _L1_ffn_in['eb'], 'L1_c': _L1_c, 'L1_wmod': _L1_wmod, 'L2_attn_WQ': _L2_attn_in['WQ'], 'L2_attn_WK': _L2_attn_in['WK'], 'L2_attn_WV': _L2_attn_in['WV'], 'L2_attn_WO': _L2_attn_in['WO'], 'L2_attn_gamma': _L2_attn_in['gamma'], 'L2_attn_beta': _L2_attn_in['beta'], 'L2_ffn_router_weight': _L2_ffn_in['router_weight'], 'L2_ffn_gate_up_proj': _L2_ffn_in['gate_up_proj'], 'L2_ffn_gate_up_proj_bias': _L2_ffn_in['gate_up_proj_bias'], 'L2_ffn_down_proj': _L2_ffn_in['down_proj'], 'L2_ffn_down_proj_bias': _L2_ffn_in['down_proj_bias'], 'L2_c': _L2_c, 'L2_wmod': _L2_wmod, 'L3_attn_Wz': _L3_attn_in['Wz'], 'L3_attn_bz': _L3_attn_in['bz'], 'L3_attn_Wx': _L3_attn_in['Wx'], 'L3_attn_bx': _L3_attn_in['bx'], 'L3_attn_WB': _L3_attn_in['WB'], 'L3_attn_bB': _L3_attn_in['bB'], 'L3_attn_WC': _L3_attn_in['WC'], 'L3_attn_bC': _L3_attn_in['bC'], 'L3_attn_Wdt': _L3_attn_in['Wdt'], 'L3_attn_bdt': _L3_attn_in['bdt'], 'L3_attn_A_log': _L3_attn_in['A_log'], 'L3_attn_Wout': _L3_attn_in['Wout'], 'L3_attn_bout': _L3_attn_in['bout'], 'L3_ffn_gate_w': _L3_ffn_in['gate_w'], 'L3_ffn_w1': _L3_ffn_in['w1'], 'L3_ffn_w3': _L3_ffn_in['w3'], 'L3_ffn_w2': _L3_ffn_in['w2'], 'L3_c': _L3_c, 'L3_wmod': _L3_wmod}
    _x0 = _d['L0_attn_hidden_states']
    _d['L0_attn_hidden_states'] = jax.random.normal(jax.random.fold_in(jax.random.key(seed), 1), (1, 2048, 128), dtype=_x0.dtype)
    del _x0
    return _d

def reference(L0_attn_hidden_states, L0_attn_w_dec_attn, L0_attn_w_out, L0_attn_b_out, L0_ffn_w_r1, L0_ffn_b_r1, L0_ffn_w_r2, L0_ffn_b_r2, L0_ffn_w_h1, L0_ffn_b_h1, L0_ffn_w_h2, L0_ffn_b_h2, L0_ffn_expert_w1, L0_ffn_expert_b1, L0_ffn_expert_w2, L0_ffn_expert_b2, L0_ffn_w_s1, L0_ffn_b_s1, L0_ffn_w_s2, L0_ffn_b_s2, L0_ffn_shared_weight, L0_ffn_w_f1, L0_ffn_b_f1, L0_ffn_w_f2, L0_ffn_b_f2, L0_ffn_integration_weight, L0_ffn_mu, L0_c, L0_wmod, L1_attn_w_qkv, L1_attn_w_out, L1_attn_b_out, L1_attn_proj, L1_ffn_w_in, L1_ffn_w_out, L1_ffn_w1, L1_ffn_w2, L1_ffn_wg, L1_ffn_we, L1_ffn_gb, L1_ffn_eb, L1_c, L1_wmod, L2_attn_WQ, L2_attn_WK, L2_attn_WV, L2_attn_WO, L2_attn_gamma, L2_attn_beta, L2_ffn_router_weight, L2_ffn_gate_up_proj, L2_ffn_gate_up_proj_bias, L2_ffn_down_proj, L2_ffn_down_proj_bias, L2_c, L2_wmod, L3_attn_Wz, L3_attn_bz, L3_attn_Wx, L3_attn_bx, L3_attn_WB, L3_attn_bB, L3_attn_WC, L3_attn_bC, L3_attn_Wdt, L3_attn_bdt, L3_attn_A_log, L3_attn_Wout, L3_attn_bout, L3_ffn_gate_w, L3_ffn_w1, L3_ffn_w3, L3_ffn_w2, L3_c, L3_wmod):

    def _L0_attn_ref(hidden_states, w_dec_attn, w_out, b_out):
        import jax, jax.numpy as jnp
        import numpy as np
        B, S, D = (8, 256, 128)
        b, s, d = hidden_states.shape
        q = hidden_states @ w_dec_attn
        scores = jnp.einsum('bid,bjd->bij', q, hidden_states)
        i_idx = jnp.arange(s)[:, None]
        j_idx = jnp.arange(s)[None, :]
        mask = j_idx < i_idx
        mask = mask.at[0, 0].set(True)
        attn = jax.nn.softmax(jnp.where(mask, scores, -jnp.inf), axis=-1)
        context = jnp.einsum('bij,bjd->bid', attn, hidden_states)
        combined = jnp.concatenate([hidden_states, context], axis=-1)
        out = jnp.tanh(combined @ w_out.T + b_out)
        return out

    def _L0_ffn_ref(x, w_r1, b_r1, w_r2, b_r2, w_h1, b_h1, w_h2, b_h2, expert_w1, expert_b1, expert_w2, expert_b2, w_s1, b_s1, w_s2, b_s2, shared_weight, w_f1, b_f1, w_f2, b_f2, integration_weight, mu):
        import jax, jax.numpy as jnp
        import numpy as np
        D = 128
        E = 8
        K = 2
        NUM_ITER = 2
        DT = 0.1
        H = 64
        CTX = 2 * D

        def _gelu(t):
            return jax.nn.gelu(t, approximate=False)

        def _inl(ctrl, x, v, mu):
            alpha_raw, beta_raw, gate_raw = jnp.split(ctrl, 3, axis=-1)
            alpha = jax.nn.sigmoid(alpha_raw)
            beta = jax.nn.softplus(beta_raw)
            gate = jax.nn.sigmoid(gate_raw)
            error = x - mu
            v_next = alpha * v - beta * error
            x_next = x + DT * gate * v_next
            return (x_next, v_next)
        B, N, Dm = x.shape
        xf = x.reshape(B * N, Dm)
        logits = _gelu(xf @ w_r1 + b_r1) @ w_r2 + b_r2
        probs = jax.nn.softmax(logits, axis=-1)
        top_p, top_i = jax.lax.top_k(probs, K)
        top_p = top_p / jnp.sum(top_p, axis=-1, keepdims=True)
        flat_idx = top_i.reshape(-1)
        flat_w = top_p.reshape(-1, 1)
        v = jnp.zeros_like(xf)
        integrated = xf
        for _ in range(NUM_ITER):
            ctx = jnp.concatenate([integrated, v], axis=-1)
            shared_ctrl = _gelu(ctx @ w_s1 + b_s1) @ w_s2 + b_s2
            x_shared, v_shared = _inl(shared_ctrl, integrated, v, mu)
            sw = jax.nn.sigmoid(shared_weight)
            ctx_e = jnp.repeat(ctx, K, axis=0)
            x_e = jnp.repeat(integrated, K, axis=0)
            v_e = jnp.repeat(v, K, axis=0)
            w1 = expert_w1[flat_idx]
            b1 = expert_b1[flat_idx]
            w2 = expert_w2[flat_idx]
            b2 = expert_b2[flat_idx]
            hidden = _gelu(jnp.einsum('tc,tch->th', ctx_e, w1) + b1)
            ctrl = jnp.einsum('th,tho->to', hidden, w2) + b2
            x_r, v_r = _inl(ctrl, x_e, v_e, mu)
            x_r = (x_r * flat_w).reshape(B * N, K, Dm).sum(axis=1)
            v_r = (v_r * flat_w).reshape(B * N, K, Dm).sum(axis=1)
            x_next = sw * x_shared + (1.0 - sw) * x_r
            v_next = sw * v_shared + (1.0 - sw) * v_r
            halt = jax.nn.sigmoid(_gelu(x_next @ w_h1 + b_h1) @ w_h2 + b_h2)
            refined = _gelu(x_next @ w_f1 + b_f1) @ w_f2 + b_f2
            integrated = integrated + halt * refined * integration_weight
            v = v_next
        return integrated.reshape(B, N, Dm)

    def _L1_attn_ref(x, w_qkv, w_out, b_out, proj):
        import jax, jax.numpy as jnp
        import numpy as np
        HEADS = 8
        BLOCK = 32
        b, n, d = x.shape
        h = HEADS
        hd = d // h
        nb = n // BLOCK
        qkv = x @ w_qkv.T
        q, k, v = jnp.split(qkv, 3, axis=-1)

        def to_blocks(t):
            return t.reshape(b, n, h, hd).transpose(0, 2, 1, 3).reshape(b, h, nb, BLOCK, hd)
        q, k, v = (to_blocks(q), to_blocks(k), to_blocks(v))
        qp = jax.nn.elu(jnp.einsum('bhcsd,hdf->bhcsf', q, proj)) + 1.0
        kp = jax.nn.elu(jnp.einsum('bhcsd,hdf->bhcsf', k, proj)) + 1.0
        kv = jnp.einsum('bhcsf,bhcsd->bhcfd', kp, v)
        num = jnp.einsum('bhcsf,bhcfd->bhcsd', qp, kv)
        ksum = kp.sum(axis=3)
        z = 1.0 / (jnp.einsum('bhcsf,bhcf->bhcs', qp, ksum) + 1e-08)
        out = num * z[..., None]
        out = out.reshape(b, h, n, hd).transpose(0, 2, 1, 3).reshape(b, n, d)
        return out @ w_out.T + b_out

    def _L1_ffn_ref(x, w_in, w_out, w1, w2, wg, we, gb, eb):
        import jax, jax.numpy as jnp
        import numpy as np
        MODEL_DIM = 128
        HIDDEN = 256
        NUM_GROUPS = 2
        EXPERTS_PER_GP = 4
        NUM_EXPERTS = NUM_GROUPS * EXPERTS_PER_GP
        TOP_K = 2
        B, T = (2, 256)

        def _swiglu(x):
            a, b = jnp.split(x, 2, axis=-1)
            return jax.nn.silu(a) * b
        Bs, Ts, C = x.shape
        S = Bs * Ts
        flat = x.reshape(S, C)
        shared = _swiglu(flat @ w_in.T) @ w_out.T
        g_probs = jax.nn.softmax(flat @ wg.T + gb, axis=-1)
        g_idx = jnp.argmax(g_probs, axis=-1)
        e_logits = flat @ we.T + eb
        egid = jnp.arange(NUM_EXPERTS) // EXPERTS_PER_GP
        masked = jnp.where(g_idx[:, None] == egid[None, :], e_logits, -jnp.inf)
        e_probs = jax.nn.softmax(masked, axis=-1)
        g_prob = jnp.take_along_axis(g_probs, g_idx[:, None], axis=1)
        p_expert = e_probs * g_prob
        topv, topi = jax.lax.top_k(p_expert, TOP_K)
        w_se = jnp.zeros((S, NUM_EXPERTS), x.dtype).at[jnp.arange(S)[:, None], topi].add(topv)
        h = _swiglu(flat @ w1.T)
        routed = jnp.zeros_like(shared)
        for e in range(NUM_EXPERTS):
            routed = routed + h * w_se[:, e:e + 1] @ w2[e].T
        return (shared + routed).reshape(Bs, Ts, C)

    def _L2_attn_ref(x, WQ, WK, WV, WO, gamma, beta):
        import jax, jax.numpy as jnp
        import numpy as np
        EPS = 1e-05

        def xpos_rotate(x, offset=0, conjugate=False):
            b, s, h, dh = x.shape
            expoent = jnp.arange(0, dh, 2, dtype=jnp.float32) / dh
            angle = 10.0 ** (-4.0 * expoent)
            if conjugate:
                angle = -angle
            pos = jnp.arange(offset, s + offset, dtype=jnp.float32)
            nangle = pos[:, None] * angle[None, :]
            sin = jnp.sin(nangle)[None, :, None, :]
            cos = jnp.cos(nangle)[None, :, None, :]
            x0 = x[..., 0::2]
            x1 = x[..., 1::2]
            rot = jnp.stack([x0 * cos - x1 * sin, x0 * sin + x1 * cos], axis=-1)
            return rot.reshape(b, s, h, dh)

        def decay_mask(nseq, scale):
            idx = jnp.arange(nseq)
            diff = idx[:, None] - idx[None, :]
            mask = (diff >= 0).astype(scale.dtype)
            diff_c = jnp.maximum(diff, 0).astype(scale.dtype)
            logd = diff_c[None, :, :] * jnp.log(scale)[:, None, None]
            return jnp.exp(logd) * mask[None, :, :]

        def group_norm(R, gamma, beta, nheads):
            b, s, d = R.shape
            dh = d // nheads
            Rg = R.reshape(b, s, nheads, dh)
            mu = jnp.mean(Rg, axis=-1, keepdims=True)
            var = jnp.var(Rg, axis=-1, keepdims=True)
            Rn = (Rg - mu) * jax.lax.rsqrt(var + EPS)
            Rn = Rn * gamma.reshape(1, 1, nheads, dh) + beta.reshape(1, 1, nheads, dh)
            return Rn.reshape(b, s, d)
        b, s, d = x.shape
        h, dh, _ = WQ.shape
        Q = jnp.einsum('bsd,hud->bshu', x, WQ)
        K = jnp.einsum('bsd,hud->bshu', x, WK)
        V = jnp.einsum('bsd,hud->bshu', x, WV)
        Q = xpos_rotate(Q)
        K = xpos_rotate(K)
        QK = jnp.einsum('bihd,bjhd->bhij', Q, K)
        scale = 1.0 - 2.0 ** (-5.0 - jnp.arange(h, dtype=jnp.float32))
        D = decay_mask(s, scale)
        QKD = QK * D[None]
        R = jnp.einsum('bhij,bjhd->bihd', QKD, V)
        R = R.reshape(b, s, d)
        R = group_norm(R, gamma, beta, h)
        y = R @ WO
        return y

    def _L2_ffn_ref(hidden_states, router_weight, gate_up_proj, gate_up_proj_bias, down_proj, down_proj_bias):
        import jax, jax.numpy as jnp
        import numpy as np
        B, S, H = (4, 256, 128)
        E, K, INTER = (16, 2, 64)
        ALPHA, LIMIT = (1.702, 7.0)
        b, s, h = hidden_states.shape
        x = hidden_states.reshape(-1, h)
        logits = x @ router_weight
        topk_w, topk_i = jax.lax.top_k(logits, K)
        topk_w = jax.nn.softmax(topk_w, axis=-1)
        one_hot = (topk_i[..., None] == jnp.arange(E)[None, None, :]).astype(topk_w.dtype)
        scores = jnp.einsum('tk,tke->te', topk_w, one_hot)
        gu = jnp.einsum('th,ehf->tef', x, gate_up_proj) + gate_up_proj_bias
        gate = gu[..., ::2]
        up = gu[..., 1::2]
        gate = jnp.minimum(gate, LIMIT)
        up = jnp.clip(up, -LIMIT, LIMIT)
        glu = gate * jax.nn.sigmoid(gate * ALPHA)
        act = (up + 1.0) * glu
        out = jnp.einsum('tei,eih,te->th', act, down_proj, scores)
        out = out + jnp.einsum('te,eh->th', scores, down_proj_bias)
        return out.reshape(b, s, h)

    def _L3_attn_ref(x, Wz, bz, Wx, bx, WB, bB, WC, bC, Wdt, bdt, A_log, Wout, bout):
        import jax, jax.numpy as jnp
        import numpy as np
        D_MODEL = 128
        D_STATE = 16
        BATCH, SEQ = (2, 256)
        z = jax.nn.sigmoid(x @ Wz + bz)
        x_ssm = x @ Wx + bx
        Bm = x @ WB + bB
        C = x @ WC + bC
        dt = jax.nn.softplus(x @ Wdt + bdt)
        A = -jnp.exp(A_log)
        A_bar = jnp.exp(dt[..., None] * A[None, None])
        x_db = x_ssm[..., None] * (dt[..., None] * Bm[..., None, :])

        def combine(c1, c2):
            a1, b1 = c1
            a2, b2 = c2
            return (a2 * a1, a2 * b1 + b2)
        _, h = jax.lax.associative_scan(combine, (A_bar, x_db), axis=1)
        y_ssm = jnp.einsum('bldn,bln->bld', h, C)
        y = y_ssm * z
        return y @ Wout + bout

    def _L3_ffn_ref(x, gate_w, w1, w3, w2):
        import jax, jax.numpy as jnp
        import numpy as np
        TOP_K = 2
        logits = jnp.einsum('btd,de->bte', x, gate_w)
        probs = jax.nn.softmax(logits, axis=-1)
        expert_weights, expert_indices = jax.lax.top_k(probs, TOP_K)
        expert_weights = expert_weights / expert_weights.sum(-1, keepdims=True)
        E = w1.shape[0]
        out = jnp.zeros_like(x)
        for i in range(E):
            wi = jnp.where(expert_indices == i, expert_weights, 0.0).sum(-1)
            h = jax.nn.silu(jnp.einsum('btd,df->btf', x, w1[i])) * jnp.einsum('btd,df->btf', x, w3[i])
            out = out + jnp.einsum('btf,fd->btd', h, w2[i]) * wi[..., None]
        return out
    x = L0_attn_hidden_states
    mod = (_silu(L0_c) @ L0_wmod).reshape(L0_c.shape[0], 6, 1, -1)
    sa, ca, ga, sb, cb, gb = (mod[:, 0], mod[:, 1], mod[:, 2], mod[:, 3], mod[:, 4], mod[:, 5])
    ga = (2 * (ga >= 0) - 1) * jnp.maximum(jnp.abs(ga), 0.25)
    gb = (2 * (gb >= 0) - 1) * jnp.maximum(jnp.abs(gb), 0.25)
    h = _layernorm(x, axis=-1) * (1 + ca) + sa
    x = x + ga * _L0_attn_ref(h, L0_attn_w_dec_attn, L0_attn_w_out, L0_attn_b_out)
    h = _layernorm(x, axis=-1) * (1 + cb) + sb
    x = x + gb * _L0_ffn_ref(h, L0_ffn_w_r1, L0_ffn_b_r1, L0_ffn_w_r2, L0_ffn_b_r2, L0_ffn_w_h1, L0_ffn_b_h1, L0_ffn_w_h2, L0_ffn_b_h2, L0_ffn_expert_w1, L0_ffn_expert_b1, L0_ffn_expert_w2, L0_ffn_expert_b2, L0_ffn_w_s1, L0_ffn_b_s1, L0_ffn_w_s2, L0_ffn_b_s2, L0_ffn_shared_weight, L0_ffn_w_f1, L0_ffn_b_f1, L0_ffn_w_f2, L0_ffn_b_f2, L0_ffn_integration_weight, L0_ffn_mu)
    mod = (_silu(L1_c) @ L1_wmod).reshape(L1_c.shape[0], 6, 1, -1)
    sa, ca, ga, sb, cb, gb = (mod[:, 0], mod[:, 1], mod[:, 2], mod[:, 3], mod[:, 4], mod[:, 5])
    ga = (2 * (ga >= 0) - 1) * jnp.maximum(jnp.abs(ga), 0.25)
    gb = (2 * (gb >= 0) - 1) * jnp.maximum(jnp.abs(gb), 0.25)
    h = _layernorm(x, axis=-1) * (1 + ca) + sa
    x = x + ga * _L1_attn_ref(h, L1_attn_w_qkv, L1_attn_w_out, L1_attn_b_out, L1_attn_proj)
    h = _layernorm(x, axis=-1) * (1 + cb) + sb
    x = x + gb * _L1_ffn_ref(h, L1_ffn_w_in, L1_ffn_w_out, L1_ffn_w1, L1_ffn_w2, L1_ffn_wg, L1_ffn_we, L1_ffn_gb, L1_ffn_eb)
    mod = (_silu(L2_c) @ L2_wmod).reshape(L2_c.shape[0], 6, 1, -1)
    sa, ca, ga, sb, cb, gb = (mod[:, 0], mod[:, 1], mod[:, 2], mod[:, 3], mod[:, 4], mod[:, 5])
    ga = (2 * (ga >= 0) - 1) * jnp.maximum(jnp.abs(ga), 0.25)
    gb = (2 * (gb >= 0) - 1) * jnp.maximum(jnp.abs(gb), 0.25)
    h = _layernorm(x, axis=-1) * (1 + ca) + sa
    x = x + ga * _L2_attn_ref(h, L2_attn_WQ, L2_attn_WK, L2_attn_WV, L2_attn_WO, L2_attn_gamma, L2_attn_beta)
    h = _layernorm(x, axis=-1) * (1 + cb) + sb
    x = x + gb * _L2_ffn_ref(h, L2_ffn_router_weight, L2_ffn_gate_up_proj, L2_ffn_gate_up_proj_bias, L2_ffn_down_proj, L2_ffn_down_proj_bias)
    mod = (_silu(L3_c) @ L3_wmod).reshape(L3_c.shape[0], 6, 1, -1)
    sa, ca, ga, sb, cb, gb = (mod[:, 0], mod[:, 1], mod[:, 2], mod[:, 3], mod[:, 4], mod[:, 5])
    ga = (2 * (ga >= 0) - 1) * jnp.maximum(jnp.abs(ga), 0.25)
    gb = (2 * (gb >= 0) - 1) * jnp.maximum(jnp.abs(gb), 0.25)
    h = _layernorm(x, axis=-1) * (1 + ca) + sa
    x = x + ga * _L3_attn_ref(h, L3_attn_Wz, L3_attn_bz, L3_attn_Wx, L3_attn_bx, L3_attn_WB, L3_attn_bB, L3_attn_WC, L3_attn_bC, L3_attn_Wdt, L3_attn_bdt, L3_attn_A_log, L3_attn_Wout, L3_attn_bout)
    h = _layernorm(x, axis=-1) * (1 + cb) + sb
    x = x + gb * _L3_ffn_ref(h, L3_ffn_gate_w, L3_ffn_w1, L3_ffn_w3, L3_ffn_w2)
    return x

_drawn_inputs = setup_inputs


def setup_inputs(seed=0):
    import zlib

    import numpy as np

    out = dict(_drawn_inputs(seed))
    spreads = {'L0_attn_b_out': (0.0, 0.29),
     'L0_ffn_b_r1': (0.0, 0.8),
     'L0_ffn_b_r2': (0.0, 0.8),
     'L0_ffn_b_h1': (0.0, 0.8),
     'L0_ffn_expert_b1': (0.0, 0.8),
     'L0_ffn_expert_b2': (0.0, 0.8),
     'L0_ffn_b_s1': (0.0, 0.8),
     'L0_ffn_b_s2': (0.0, 0.8),
     'L0_ffn_b_f1': (0.0, 0.8),
     'L0_ffn_b_f2': (0.0, 0.474),
     'L0_ffn_integration_weight': (0.5, 0.6),
     'L0_ffn_mu': (0.0, 0.8),
     'L1_attn_b_out': (0.0, 0.1),
     'L1_ffn_gb': (0.0, 0.8),
     'L1_ffn_eb': (0.0, 0.8),
     'L2_attn_gamma': (1.0, 0.2),
     'L2_attn_beta': (0.0, 0.268),
     'L3_attn_bz': (0.0, 0.392),
     'L3_attn_bx': (0.0, 0.1),
     'L3_attn_bB': (0.0, 0.1),
     'L3_attn_bC': (0.0, 0.1),
     'L3_attn_bdt': (0.0, 0.316),
     'L3_attn_bout': (0.0, 0.374)}
    factors = {'L0_ffn_w_r1': 8.0,
     'L0_ffn_w_r2': 8.0,
     'L0_ffn_w_h1': 8.0,
     'L0_ffn_w_h2': 8.0,
     'L0_ffn_expert_w1': 8.0,
     'L0_ffn_expert_w2': 8.0,
     'L0_ffn_w_s1': 8.0,
     'L0_ffn_w_s2': 8.0,
     'L0_ffn_w_f1': 8.0,
     'L0_ffn_w_f2': 8.0,
     'L1_attn_proj': 8.0,
     'L1_ffn_w_in': 8.0,
     'L1_ffn_w_out': 8.0,
     'L1_ffn_w1': 8.0,
     'L1_ffn_w2': 8.0,
     'L1_ffn_wg': 8.0,
     'L1_ffn_we': 8.0,
     'L2_ffn_router_weight': 8.0,
     'L2_ffn_gate_up_proj': 8.0,
     'L2_ffn_gate_up_proj_bias': 8.0,
     'L2_ffn_down_proj': 8.0,
     'L2_ffn_down_proj_bias': 8.0,
     'L3_ffn_gate_w': 8.0,
     'L3_ffn_w1': 8.0,
     'L3_ffn_w3': 8.0,
     'L3_ffn_w2': 8.0}
    for name, (base, spread) in spreads.items():
        noise = np.random.default_rng([zlib.crc32(name.encode()), seed]).standard_normal(out[name].shape)
        drawn = base * np.exp(spread * noise) if base else spread * noise
        out[name] = jnp.asarray(drawn.astype(out[name].dtype))
    for name, factor in factors.items():
        out[name] = (out[name] * factor).astype(out[name].dtype)
    return out
```

```python
import numpy as np
import concourse.bass as bass
from concourse import mybir

F32 = mybir.dt.float32
BF16 = mybir.dt.bfloat16
U32 = mybir.dt.uint32
ALU = mybir.AluOpType
ACT = mybir.ActivationFunctionType
AX = mybir.AxisListType

S, D, NT, NC, W = 2048, 128, 16, 4, 512
SPEC = [
    ("c0", [("ident", 128), ("mask", 128), ("mask0", 128), ("block", 128), ("iota", 16), ("ind", 16), ("ccol", 4)]),
    ("a0", [("wdec", 128), ("w1o", 128), ("w2o", 128), ("brow0", 128)]),
    ("f0", [("wr1", 32), ("br1", 1), ("wr2", 8), ("br2", 8), ("wh1", 32), ("bh1", 1), ("wh2", 1), ("bh2", 1),
            ("ew1", 1024), ("eb1", 4), ("ew2", 1536), ("eb2a", 384), ("eb2b", 384), ("ws1", 128), ("bs1", 1),
            ("ws2", 384), ("sw", 1), ("wf1", 256), ("bf1", 2), ("wf2", 256), ("bf2", 1), ("iw", 1), ("mu", 1)]),
    ("l1", [("wv1", 128), ("wo1", 128), ("bo1", 128), ("win", 512), ("wou", 256), ("w11", 512), ("w21", 2048),
            ("wge", 10), ("bge", 10)]),
    ("l2", [("wq", 128), ("wqs", 128), ("wk", 128), ("wks", 128), ("wvr", 1024), ("wo2", 128), ("gam", 1), ("bet", 1),
            ("rw", 16), ("gup", 2048), ("gb", 8), ("ub", 8), ("dwn", 1024), ("dbn", 128)]),
    ("l3", [("wz", 128), ("bz", 1), ("wx", 128), ("bx", 1), ("wbc", 32), ("bbc", 32), ("wdt", 128), ("bdt", 1),
            ("alog", 16), ("wo3", 128), ("bo3", 128), ("gw", 8)]),
]
TEMP = [("wmod", 4 * 768), ("wqkv", 24 * 128), ("proj", 8 * 128)]
GROUP_COLS = {g: sum(n for _, n in items) for g, items in SPEC}
NG = {"L0A": 0, "L0F": 1, "L1A": 2, "L1F": 3, "L2A": 4, "L2F": 5, "L3A": 6, "L3F": 7}


class Tok:

    def __init__(self, key, n, t):
        self.key, self.n, self.t = key, n, t


class Buf:

    def __init__(self, ap, w=()):
        self.ap, self.w = ap, list(w)


class Op:
    def __init__(self, alts, deps):
        self.alts, self.deps = alts, deps


class Queues:

    ENG = ["PE", "ACT", "DVE", "POOL", "SP"]

    def __init__(self):
        self.items = {e: [] for e in self.ENG}
        self.count = {}
        self.known = {e: {} for e in self.ENG}
        self.free = {e: 0.0 for e in self.ENG}
        self.tset = None

    def start(self, alt, deps):
        eng, _, _, tset, _ = alt
        t = max([self.free[eng]] + [d.t + 60 for d in deps])
        if eng == "ACT" and tset and self.tset not in tset:
            t += 1300
        return t

    def emit(self, alt, deps):
        eng, fn, cost, tset, dma = alt
        t = self.start(alt, deps)
        if eng == "ACT" and tset and self.tset not in tset:
            self.tset = tset[0]
        need = {}
        for d in deps:
            if self.known[eng].get(d.key, 0) < d.n:
                need[d.key] = max(need.get(d.key, 0), d.n)
        self.known[eng].update(need)
        key, by = (dma, 16) if dma else (eng, 1)
        self.count[key] = self.count.get(key, 0) + by
        self.items[eng].append((sorted(need.items()), fn, key, by))
        self.free[eng] = t + (50 if dma else cost)
        return Tok(key, self.count[key], t + cost)


class Slots:
    def __init__(self, bufs):
        self.bufs, self.promised, self.n, self.line = list(bufs), 0, len(bufs), []

    def take(self, k):
        self.bufs.sort(key=lambda b: max([x.t for x in b.w], default=0))
        out, self.bufs = self.bufs[:k], self.bufs[k:]
        return out

    def give(self, b, toks):
        b.w = list(toks)
        self.bufs.append(b)


def run(queues, streams):
    live = []
    for pri, g in enumerate(streams):
        live.append([pri, g, next(g, None)])
    live = [s for s in live if s[2] is not None]
    while live:
        best = None
        for s in live:
            req = s[2]
            if isinstance(req, Op):
                for alt in req.alts:
                    t = queues.start(alt, req.deps)
                    k = (t, s[0], t + alt[2])
                    if best is None or k[0] < best[0][0] - 1 or (abs(k[0] - best[0][0]) <= 1 and (k[1], k[2]) < best[0][1:]):
                        best = (k, s, alt)
            else:
                got = None
                if req[0] == "take" and len(req[1].bufs) >= req[2]:
                    got = req[1].take(req[2])
                elif req[0] == "reserve":
                    if s not in req[1].line:
                        req[1].line.append(s)
                    if req[1].line[0] is s and req[1].n - req[1].promised >= req[2]:
                        req[1].line.pop(0)
                        req[1].promised += req[2]
                        got = True
                elif req[0] == "until" and req[1]():
                    got = True
                if got is not None:
                    best = (None, s, got)
                    break
        assert best is not None, ("stuck", [(s[0], s[2][0], s[2][2:]) for s in live])
        k, s, what = best
        val = what if k is None else queues.emit(what, s[2].deps)
        try:
            s[2] = s[1].send(val)
        except StopIteration:
            live.remove(s)


SETS = {"Gelu": ("gelu",), "Tanh": ("exp", "gelu"), "Exp": ("exp", "lnexp"), "Ln": ("lnexp",), "Sqrt": ("sqrt",)}


def width(ap):
    n = 1
    for k in ap.shape[1:]:
        n *= k
    return n


def build(nc, x_d, cs_d, w3_d, pk, temps, out_d):
    from contextlib import ExitStack
    ctx = ExitStack()
    with ctx:
        def sb(name, shape, dt=F32):
            return ctx.enter_context(nc.sbuf_tensor(name, shape, dt))

        Q = Queues()
        G = {g: sb("g_" + g, [128, n]) for g, n in GROUP_COLS.items()}
        V = {}
        for g, items in SPEC:
            at = 0
            for name, n in items:
                V[name] = G[g][:, at:at + n]
                at += n

        xs = sb("xs", [128, NT, D])
        early = sb("early", [128, 4 * S])
        hT0 = early[:, 0:S]
        Vp = early[:, S:2 * S].rearrange("p (n d) -> p n d", n=NT)
        S_buf = [early[:, 2 * S:3 * S], early[:, 3 * S:4 * S]]
        mask_sb = sb("maskb", [128, 8, W], BF16)
        vext = [sb(f"vext{i}", [128, 4, 8, 17]) for i in range(2)]
        NTILE = 35
        tiles = sb("tiles", [128, NTILE * W])
        CQ = sb("CQ", [128, 16, 128])
        GR = sb("GR", [128, 8, 128])
        mc = sb("mc", [128, 24])
        pc = sb("pc", [128, 64])
        Acol = sb("Acol", [128, 16])
        brow2 = sb("brow2", [128, 128])
        identb = sb("identb", [128, 128], BF16)
        oneb = sb("oneb", [128, W], BF16)
        zerob = sb("zerob", [128, W], BF16)
        gwt = sb("gwt", [128, 128])
        carry2 = sb("carry2", [128, NC, 8])
        carry3 = sb("carry3", [128, NC, 16])
        sm = [sb(f"sm{c}", [128, 620]) for c in range(NC)]
        smu = [sb(f"smu{c}", [128, 32], U32) for c in range(NC)]
        ohb_sb = sb("ohb", [128, W], BF16)

        psum = [ctx.enter_context(nc.psum_tensor(f"ps{i}", [128, W], F32)) for i in range(8)]

        PS = Slots([Buf(p[:, :]) for p in psum])
        TL = Slots([Buf(tiles[:, i * W:(i + 1) * W]) for i in range(NTILE)])
        SR = Slots([Buf(s) for s in S_buf])
        MK = Slots([Buf(mask_sb[:, :, :])])
        R3 = Slots([])
        VX = Slots([Buf(v[:, :, :, :]) for v in vext])

        def PEop(fn, cost, deps):
            return Op([("PE", fn, cost, None, None)], deps)

        def MM(chains, deps, passes=4, zero=True):
            cost = 0
            for out, prods in chains:
                cost += sum(passes * width(r) / 2.4 + 3 for _, r in prods)

            def fn(e):
                for out, prods in chains:
                    for i, (l, r) in enumerate(prods):
                        last = e.matmul(out, l, r, start=(i == 0), stop=(i == len(prods) - 1))
                return last
            return PEop(fn, cost, deps)

        def MMadd(prods, deps, stop=False, start=False):
            cost = sum(4 * width(r) / 2.4 + 3 for _, _, r in prods)

            def fn(e):
                for i, (o, l, r) in enumerate(prods):
                    last = e.matmul(o, l, r, start=start and i == 0, stop=stop and i == len(prods) - 1)
                return last
            return PEop(fn, cost, deps)

        def TR(pairs, deps):
            def fn(e):
                for o, i in pairs:
                    last = e.transpose(o, i, V["ident"])
                return last
            return PEop(fn, len(pairs) * 107, deps)

        def AC(out, in_, func, deps, bias=0.0, scale=1.0, accum=None):
            f = getattr_act(func)

            def fn(e):
                if accum is not None:
                    return e.activation(out, in_, f, bias=bias, scale=scale, accum_out=accum)
                return e.activation(out, in_, f, bias=bias, scale=scale)
            cost = 70 + width(out) / 1.2 + 93 * (sum(not isinstance(x, float) for x in (bias, scale)) + (accum is not None))
            return Op([("ACT", fn, cost, SETS.get(func), None)], deps)

        def vec(fn, out, deps, eng, n=None, rate=1.0):
            n = n or width(out)
            c = {"DVE": 68 + rate * n / 0.96, "POOL": 120 + n * (3.5 if rate < 1 else 2.15)}
            return Op([(g, fn, c[g], None, None) for g in eng], deps)

        def TS(out, a, s1, s2, op0, op1, deps, eng=("DVE",), rate=1.0):
            if op1 is None:
                return vec(lambda e: e.tensor_scalar(out, a, s1, None, op0), out, deps, eng, rate=rate)
            return vec(lambda e: e.tensor_scalar(out, a, s1, s2, op0, op1), out, deps, eng, rate=rate)

        def TT(out, a, b, op, deps, eng=("DVE",)):
            return vec(lambda e: e.tensor_tensor(out, a, b, op), out, deps, eng)

        def STT(out, a, s, b, op0, op1, deps):
            return vec(lambda e: e.scalar_tensor_tensor(out=out, in0=a, scalar=s, in1=b, op0=op0, op1=op1),
                       out, deps, ("DVE",))

        def CP(out, a, deps, eng=("DVE",)):
            return vec(lambda e: e.tensor_copy(out, a), out, deps, eng)

        def EV(out, a, deps):
            return Op([("ACT", lambda e: e.activation(out, a, ACT.Copy), 60 + width(out) / 1.2, None, None),
                       ("DVE", lambda e: e.tensor_copy(out, a), 68 + width(out) / 0.96, None, None)], deps)

        def RED(out, a, op, deps, negate=False):
            return vec(lambda e: e.tensor_reduce(out, a, AX.X, op, negate=negate), a, deps, ("DVE",))

        def many(fns, n, deps, eng=("DVE",)):
            def fn(e):
                for f in fns:
                    last = f(e)
                return last
            return Op([(g, fn, len(fns) * (70 if g == "DVE" else 120) + n * (1.04 if g == "DVE" else 2.0), None, None)
                       for g in eng], deps)

        def DMA(out, in_, key, deps, size):
            return Op([("SP", lambda e: e.dma_start(out, in_), 2000 + size / 180.0, None, key)], deps)

        BOTH = ("DVE", "POOL")
        take = lambda pool, k=1: ("take", pool, k)

        load = {}
        done = {}
        xt = [None] * NC
        hTt, Vt = [None] * NC, [None] * NC
        L0A_last = []
        c2t, c3t = {}, {}

        def tile4(b):
            return b.rearrange("p (t n) -> p t n", t=4)

        def tl(ap, i):
            return ap[:, i * 128:(i + 1) * 128]

        tbase = {}
        at = 0
        for name, n in TEMP:
            tbase[name] = (at, n)
            at += n
        NTEMP = -(-at // W)
        wmod = tiles[:, 0:3072].rearrange("p (l n) -> p l n", l=4)
        wqkv = tiles[0:16, 3072:6144].rearrange("p (h n) -> p h n", h=24)
        proj = tiles[0:16, 6144:7168].rearrange("p (h n) -> p h n", h=8)

        def loads():
            tmp = TL.take(NTEMP)
            xv = x_d.rearrange("a (n p) d -> p (a n) d", p=128)
            load["c0"] = yield DMA(G["c0"][:, :], pk["c0"], "d_c0", [], 128 * 4 * GROUP_COLS["c0"])
            xt[0] = [(yield DMA(xs[:, 0:4, :], xv[:, 0:4, :], "d_x0", [], 1 << 18))]
            load["wmod"] = yield DMA(tiles[:, 0:3072], temps["wmod"], "d_wmod", [], 128 * 4 * 3072)
            load["a0"] = yield DMA(G["a0"][:, :], pk["a0"], "d_a0", [], 128 * 4 * GROUP_COLS["a0"])
            for c in range(1, NC):
                xt[c] = [(yield DMA(xs[:, 4 * c:4 * c + 4, :], xv[:, 4 * c:4 * c + 4, :], f"d_x{c}", [], 1 << 18))]
            load["f0"] = yield DMA(G["f0"][:, :], pk["f0"], "d_f0", [], 128 * 4 * GROUP_COLS["f0"])
            a = yield DMA(tiles[0:16, 3072:6144], temps["wqkv"], "d_wqkv", [], 16 * 4 * 3072)
            b = yield DMA(tiles[0:16, 6144:7168], temps["proj"], "d_proj", [], 16 * 4 * 1024)
            load["qkv"] = [a, b]
            for g in ("l1", "l2", "l3"):
                load[g] = yield DMA(G[g][:, :], pk[g], "d_" + g, [], 128 * 4 * GROUP_COLS[g])
            load["tmp"] = tmp

        def prep():
            yield ("until", lambda: "wmod" in load)
            lc, lw = load["c0"], load["wmod"]
            a = yield CP(identb[:, :], V["ident"], [lc])
            done["identb"] = a
            a = yield vec(lambda e: e.memset(oneb[:, :], 1.0), oneb[:, :], [], ("DVE",))
            done["oneb"] = a
            a = yield vec(lambda e: e.memset(zerob[:, :], 0.0), zerob[:, :], [], ("DVE",))
            done["zerob"] = a
            done["vones"] = []
            for v in vext:
                a = yield vec(lambda e, v=v: e.memset(v[:, :, :, 16:17], 1.0), v[:, :, :, 16], [], ("POOL",))
                done["vones"].append(a)
            a = yield vec(lambda e: e.memset(pc[:, 0:1], -0.5), pc[:, 0:1], [], ("POOL",))
            done["half"] = a
            a = yield AC(pc[:, 4:8], V["ccol"], "Tanh", [lc], scale=0.5)
            a = yield STT(pc[:, 8:12], pc[:, 4:8], 1.0, V["ccol"], ALU.add, ALU.mult, [a])
            a = yield TS(pc[:, 12:16], pc[:, 8:12], 0.5, None, ALU.mult, None, [a])
            sc = pc[:, 12:16]
            (b,) = yield take(PS)
            t = yield MM([(b.ap[:, 6 * l + s:6 * l + s + 1], [(wmod[:, l, 128 * s:128 * s + 128], sc[:, l:l + 1])])
                          for l in range(4) for s in range(6)], [a, lw] + b.w)
            t2 = yield CP(mc[:, :], b.ap[:, 0:24], [t])
            mc3 = mc[:, :].rearrange("p (l s) -> p l s", l=4)
            t3 = yield TS(mc3[:, :, 1:5:3], mc3[:, :, 1:5:3], 1.0, None, ALU.add, None, [t2])
            done["mc"] = t3
            t4 = yield TS(pc[:, 16:17], mc[:, 5:6], 0.0, 2.0, ALU.is_ge, ALU.mult, [t3])
            t5 = yield STT(pc[:, 17:18], pc[:, 16:17], -1.0, mc[:, 5:6], ALU.add, ALU.mult, [t4])
            t5 = yield TS(pc[:, 17:18], pc[:, 17:18], 0.25, None, ALU.max, None, [t5])
            done["gcol"] = yield STT(pc[:, 18:19], pc[:, 16:17], -1.0, pc[:, 17:18], ALU.add, ALU.mult, [t4, t5])
            PS.give(b, [t2])
            bs = yield take(PS, 2)
            for k, seg in enumerate((2, 5)):
                ch = [(tl(bs[k].ap, l), [(sc[:, l:l + 1].broadcast_to([128, 128]), wmod[:, l, 128 * seg:128 * seg + 128])])
                      for l in range(4)]
                t = yield MM(ch, [a, lw] + bs[k].w)
                ge = GR[:, 4 * k:4 * k + 4, :]
                (m,) = yield take(TL)
                t2 = yield TS(ge, tile4(bs[k].ap), 0.0, 2.0, ALU.is_ge, ALU.mult, [t])
                t3 = yield STT(tile4(m.ap), ge, -1.0, tile4(bs[k].ap), ALU.add, ALU.mult, [t2] + m.w)
                t3 = yield TS(m.ap, m.ap, 0.25, None, ALU.max, None, [t3])
                t4 = yield STT(ge, ge, -1.0, tile4(m.ap), ALU.add, ALU.mult, [t3])
                TL.give(m, [t4])
                PS.give(bs[k], [t2, t3])
                done["G%d" % k] = t4
            tw = [t]
            GA = lambda l: GR[:, l, :]
            GB = lambda l: GR[:, 4 + l, :]
            ga, gb = done["G0"], done["G1"]
            yield ("until", lambda: "f0" in load)
            lf = load["f0"]
            a = yield AC(pc[:, 20:21], V["sw"], "Tanh", [lf], scale=0.5)
            t1 = yield TS(pc[:, 21:22], pc[:, 20:21], 0.5, 0.5, ALU.mult, ALU.add, [a])
            t2 = yield TS(pc[:, 22:23], pc[:, 20:21], -0.5, 0.5, ALU.mult, ALU.add, [a])
            t3 = yield TS(pc[:, 23:24], pc[:, 20:21], -0.5, -0.5, ALU.mult, ALU.add, [a])
            t4 = yield TS(pc[:, 24:25], V["bh2"], 0.5, None, ALU.mult, None, [lf])
            t5 = yield TS(pc[:, 25:26], V["iw"], 0.5, None, ALU.mult, None, [lf])
            done["f0c"] = [t1, t2, t3, t4, t5]
            yield ("until", lambda: "tmp" in load)
            ts = []
            for k in range(2):
                for half in range(2):
                    (b,) = yield take(PS)
                    t = yield MM([(tl(b.ap, j), [(wqkv[:, 8 * k + 4 * half + j, :], proj[:, 4 * half + j, :])])
                                  for j in range(4)], load["qkv"] + b.w)
                    o = 8 * k + 4 * half
                    t2 = yield CP(CQ[:, o:o + 4, :], tile4(b.ap), [t])
                    PS.give(b, [t2])
                    ts.append(t2)
                    tw.append(t)
            done["CQ"] = ts
            for b in load["tmp"]:
                TL.give(b, tw)
            l1 = load["l1"]
            a = yield TT(V["wo1"], V["wo1"], GA(1), ALU.mult, [l1, ga], BOTH)
            b = yield TT(V["bo1"], V["bo1"], GA(1), ALU.mult, [l1, ga], BOTH)
            done["L1A"] = [a, b]
            h1 = yield TS(gwt[:, :], GB(1), 0.5, None, ALU.mult, None, [gb], BOTH)
            w = V["wou"].rearrange("p (k n) -> p k n", k=2)
            a = yield TT(w, w, gwt[:, :].unsqueeze(1).broadcast_to([128, 2, 128]), ALU.mult, [l1, h1], BOTH)
            w = V["w21"].rearrange("p (k n) -> p k n", k=16)
            b = yield TT(w, w, gwt[:, :].unsqueeze(1).broadcast_to([128, 16, 128]), ALU.mult, [l1, h1], ("POOL",))
            done["L1F"] = [a, b]
            l2 = load["l2"]
            (p,) = yield take(PS)
            t = yield MM([(p.ap[:, 0:128], [(V["bet"].broadcast_to([128, 128]), V["wo2"])])], [l2] + p.w)
            t2 = yield TT(brow2[:, :], p.ap[:, 0:128], GA(2), ALU.mult, [t, ga])
            PS.give(p, [t2])
            t3 = yield STT(V["wo2"], V["wo2"], V["gam"], GA(2), ALU.mult, ALU.mult, [l2, t, ga])
            done["L2A"] = [t2, t3]
            h2 = yield TS(gwt[:, :], GB(2), 0.5, None, ALU.mult, None, [gb, a, b])
            w = V["dwn"].rearrange("p (k n) -> p k n", k=8)
            a = yield TT(w, w, gwt[:, :].unsqueeze(1).broadcast_to([128, 8, 128]), ALU.mult, [l2, h2], ("POOL",))
            b = yield TT(V["dbn"][0:16, :], V["dbn"][0:16, :], GR[0:16, 6, :], ALU.mult, [l2, gb])
            c = yield TS(V["ub"], V["ub"], 1.0, None, ALU.add, None, [l2], BOTH)
            done["L2F"] = [a, b, c]
            l3 = load["l3"]
            t1 = yield AC(Acol[:, :], V["alog"], "Exp", [l3])
            t2 = yield TS(Acol[:, :], Acol[:, :], -1.0, None, ALU.mult, None, [t1])
            t3 = yield TS(V["wo3"], V["wo3"], 0.5, None, ALU.mult, None, [l3], BOTH)
            t3 = yield TT(V["wo3"], V["wo3"], GA(3), ALU.mult, [t3, ga], BOTH)
            t4 = yield TT(V["bo3"], V["bo3"], GA(3), ALU.mult, [l3, ga], BOTH)
            t5 = yield TS(V["bz"], V["bz"], 0.5, None, ALU.mult, None, [l3], BOTH)
            done["L3A"] = [t2, t3, t4, t5]
            t6 = yield TS(GB(3), GB(3), 0.5, None, ALU.mult, None, [gb], BOTH)
            done["L3F"] = [t6, l3]

        ring = {}

        def stream3():
            yield ("until", lambda: "l3" in load)
            for c in range(NC):
                for e in range(8):
                    (b,) = yield take(R3)
                    t = yield DMA(b.ap, w3_d[e], b.sem, b.w, 128 * 4 * 1536)
                    ring[c, e] = (b, t)

        def norm(c, k, deps):
            l, half = divmod(k, 2)
            st = sm[c][:, 0:24].rearrange("p (t n) -> p t n", t=4)
            mv = sm[c][:, 24:32].rearrange("p (t n) -> p t n", t=4)
            rs = sm[c][:, 32:36]
            a = yield many([lambda e, i=i: e.bn_stats(st[:, i, :], xs[:, 4 * c + i, :]) for i in range(4)], 512, xt[c])
            a = yield many([lambda e, i=i: e.bn_aggr(mv[:, i, :], st[:, i, :]) for i in range(4)], 104, [a])
            b = yield TS(rs, mv[:, :, 1], 1e-5, None, ALU.add, None, [a], ("POOL",))
            b = yield TT(rs, rs, pc[:, 0:1].broadcast_to([128, 4]), ALU.pow, [b, done["half"]], ("POOL",))
            (xn,) = yield take(TL)
            t = yield many([lambda e, i=i: e.tensor_scalar(tl(xn.ap, i), xs[:, 4 * c + i, :], mv[:, i, 0:1], rs[:, i:i + 1],
                                                           ALU.subtract, ALU.mult) for i in range(4)], 512, [b] + xn.w)
            (p,) = yield take(PS)
            t2 = yield TR([(tl(p.ap, i), tl(xn.ap, i)) for i in range(4)], [t, load["c0"]] + p.w)
            TL.give(xn, [t2])
            if deps is None:
                dst, w = hT0[:, c * W:(c + 1) * W], []
                h = Buf(dst)
            else:
                (h,) = yield take(TL)
                dst, w = h.ap, h.w
            o = 6 * l + 3 * half
            t3 = yield AC(dst, p.ap, "Identity", [t2, done["mc"]] + w, bias=mc[:, o:o + 1], scale=mc[:, o + 1:o + 2])
            PS.give(p, [t3])
            return h, t3, t

        def topk(c, E, lg, t):
            s = sm[c]
            mx = s[:, 100:132].rearrange("p (t n) -> p t n", t=4)
            ix = smu[c][:, :].rearrange("p (t n) -> p t n", t=4)
            ixf = s[:, 132:140].rearrange("p (t n) -> p t n", t=4)
            w = s[:, 140:148].rearrange("p (s t) -> p s t", s=2)
            oh = s[:, 160:160 + 8 * E].rearrange("p (t s n) -> p t s n", t=4, s=2)
            a = yield many([lambda e, i=i: e.max(mx[:, i, :], lg[:, i, :]) for i in range(4)], 4 * E, [t])
            b = yield many([lambda e, i=i: e.max_index(ix[:, i, :], mx[:, i, :], lg[:, i, :]) for i in range(4)], 8 * E, [a])
            b = yield CP(ixf, ix[:, :, 0:2], [b])
            io = V["iota"][:, 0:E].unsqueeze(1).broadcast_to([128, 4, E])
            o0 = yield TT(oh[:, :, 0, :], io, ixf[:, :, 0:1].broadcast_to([128, 4, E]), ALU.is_equal, [b])
            o1 = yield TT(oh[:, :, 1, :], io, ixf[:, :, 1:2].broadcast_to([128, 4, E]), ALU.is_equal, [b])
            a = yield TT(w[:, 1, :], mx[:, :, 1], mx[:, :, 0], ALU.subtract, [a])
            a = yield AC(w[:, 1, :], w[:, 1, :], "Exp", [a])
            d = yield TS(w[:, 0, :], w[:, 1, :], 1.0, None, ALU.add, None, [a])
            d = yield vec(lambda e: e.reciprocal(w[:, 0, :], w[:, 0, :]), w[:, 0, :], [d], ("DVE",))
            d = yield TT(w[:, 1, :], w[:, 1, :], w[:, 0, :], ALU.mult, [d])
            return oh, w, [o0, o1, d]

        def weights(c, E, oh, w, ts):
            s = sm[c]
            se = s[:, 300:300 + 4 * E].rearrange("p (t n) -> p t n", t=4)
            s2 = s[:, 364:364 + 4 * E].rearrange("p (t n) -> p t n", t=4)
            a = yield TT(se, oh[:, :, 0, :], w[:, 0, :].unsqueeze(2).broadcast_to([128, 4, E]), ALU.mult, ts)
            b = yield TT(s2, oh[:, :, 1, :], w[:, 1, :].unsqueeze(2).broadcast_to([128, 4, E]), ALU.mult, ts)
            a = yield TT(se, se, s2, ALU.add, [a, b])
            return se, a

        def project_out(c, a, t, w, ws):
            (p,) = yield take(PS)
            t2 = yield MM([(tl(p.ap, i), [(tl(a, i), w)]) for i in range(4)], t + ws + p.w)
            xc = xs[:, 4 * c:4 * c + 4, :]
            t3 = yield TT(xc, tile4(p.ap), xc, ALU.add, [t2] + xt[c])
            PS.give(p, [t3])
            xt[c] = [t3]
            return t2

        def turned(src, t):
            (p,) = yield take(PS)
            t2 = yield TR([(tl(p.ap, i), tl(src.ap, i)) for i in range(4)], t + p.w)
            TL.give(src, [t2])
            (o,) = yield take(TL)
            t3 = yield EV(o.ap, p.ap, [t2] + o.w)
            PS.give(p, [t3])
            return o, t3

        def bias_rows(c, row, t):
            xc = xs[:, 4 * c:4 * c + 4, :]
            a = yield TT(xc, xc, row.unsqueeze(1).broadcast_to([128, 4, 128]), ALU.add, t + xt[c], ("POOL",))
            xt[c] = [a]

        def L0A(c):
            yield ("reserve", TL, 6)
            yield ("until", lambda: xt[c] is not None and "a0" in load and "mc" in done and "half" in done)
            h, th, _ = yield from norm(c, 0, None)
            hTt[c] = th
            h = h.ap
            wd = load["a0"]
            p = yield take(PS, 3)
            t1 = yield MM([(p[0].ap, [(V["wdec"], h)])], [th, wd] + p[0].w)
            (qT,) = yield take(TL)
            tq = yield EV(qT.ap, p[0].ap, [t1] + qT.w)
            t2 = yield MM([(tl(p[1].ap, i), [(tl(h, i), V["w2o"])]) for i in range(4)], p[1].w + [th, wd])
            Vt[c] = yield EV(Vp[:, 4 * c:4 * c + 4, :], tile4(p[1].ap), [t2])
            t3 = yield MM([(tl(p[2].ap, i), [(tl(h, i), V["w1o"])]) for i in range(4)], p[2].w + [th, wd])
            (Bt,) = yield take(TL)
            tB = yield TT(tile4(Bt.ap), tile4(p[2].ap), V["brow0"].unsqueeze(1).broadcast_to([128, 4, 128]), ALU.add, [t3] + Bt.w)
            PS.give(p[0], [tq])
            PS.give(p[1], [Vt[c]])
            PS.give(p[2], [tB])
            yield ("until", lambda: all(Vt[k] is not None for k in range(c)))
            s = sm[c]
            outs = []
            for i in range(4):
                (R,) = yield take(SR)
                rw = R.w
                mx = s[:, 40:48]
                parts = []
                for kb in range(c + 1):
                    n = W if kb < c else (i + 1) * 128
                    (p,) = yield take(PS)
                    t = yield MM([(p.ap[:, 0:n], [(tl(qT.ap, i), hT0[:, kb * W:kb * W + n])])], [tq, hTt[kb]] + p.w)
                    free = []
                    m = n if kb < c else n - 128
                    if m:
                        a = yield vec(lambda e, o=R.ap[:, kb * W:kb * W + m], q=p.ap[:, 0:m], z=mx[:, kb:kb + 1]:
                                      e.tensor_scalar(o, q, 0.0, -3.0e38, ALU.add, ALU.max, accum_out=z),
                                      p.ap[:, 0:m], [t] + rw, ("DVE",))
                        free.append(a)
                        parts.append(a)
                    if kb == c:
                        dg = R.ap[:, kb * W + m:kb * W + n]
                        a = yield TT(dg, p.ap[:, m:n], V["mask0" if c == 0 and i == 0 else "mask"], ALU.add, [t] + rw)
                        free.append(a)
                        a = yield RED(mx[:, 5:6], dg, ALU.max, [a])
                        parts.append(a)
                        if not m:
                            a = yield CP(mx[:, kb:kb + 1], mx[:, 5:6], [a])
                            parts.append(a)
                    PS.give(p, free)
                n = c * W + (i + 1) * 128
                nk = n // 128
                a = yield CP(mx[:, c + 1:c + 2], mx[:, 5:6], parts) if c < 4 else None
                a = yield RED(s[:, 48:49], mx[:, 0:c + 2], ALU.max, parts + [a], negate=True)
                te = yield AC(R.ap[:, 0:n], R.ap[:, 0:n], "Exp", parts + [a], bias=s[:, 48:49], accum=s[:, 49:50])
                tr = yield vec(lambda e: e.reciprocal(s[:, 50:51], s[:, 49:50]), s[:, 50:51], [te], ("DVE",))
                last = []
                (O,) = yield take(PS)
                tw = O.w
                o = O.ap[:, 0:128]
                for j0 in range(0, nk, 4):
                    js = range(j0, min(j0 + 4, nk))
                    (p,) = yield take(PS)
                    t = yield TR([(tl(p.ap, j - j0), tl(R.ap, j)) for j in js], [te] + p.w)
                    (PT,) = yield take(TL)
                    t2 = yield EV(PT.ap[:, 0:128 * len(js)], p.ap[:, 0:128 * len(js)], [t] + PT.w)
                    PS.give(p, [t2])
                    pr = [(tl(PT.ap, j - j0), Vp[:, j, :]) for j in js]

                    def fn(e, pr=pr, first=j0 == 0, fin=js[-1] == nk - 1, o=o):
                        for q, (a, b) in enumerate(pr):
                            x = e.matmul(o, a, b, start=first and q == 0, stop=fin and q == len(pr) - 1)
                        return x
                    t3 = yield PEop(fn, len(pr) * 216, [t2] + [Vt[j // 4] for j in js] + tw)
                    TL.give(PT, [t3])
                    last = [t3]
                SR.give(R, [t, te])
                a = yield STT(tl(Bt.ap, i), o, s[:, 50:51], tl(Bt.ap, i), ALU.mult, ALU.add, last + [tr, tB])
                outs.append(a)
                PS.give(O, [a])
            TL.give(qT, last)
            a = yield AC(Bt.ap, Bt.ap, "Tanh", outs)
            a = yield TT(tile4(Bt.ap), tile4(Bt.ap), GR[:, 0, :].unsqueeze(1).broadcast_to([128, 4, 128]), ALU.mult,
                         [a, done["G0"]], BOTH)
            xc = xs[:, 4 * c:4 * c + 4, :]
            a = yield TT(xc, xc, tile4(Bt.ap), ALU.add, [a] + xt[c], BOTH)
            TL.give(Bt, [a])
            xt[c] = [a]
            TL.promised -= 6
            L0A_last.append(last + outs)
            if len(L0A_last) == NC:
                after = [t for ts in L0A_last for t in ts]
                for i in range(3):
                    R3.give(Buf(early[:, 3 * i * W:3 * (i + 1) * W]), after)
                    R3.bufs[-1].sem = f"r3_{i}"
                for i in range(9, 16):
                    TL.give(Buf(early[:, i * W:(i + 1) * W]), after)
                TL.n += 7

        def L0F(c):
            yield ("reserve", TL, 18)
            (mk,) = yield take(MK)
            yield ("until", lambda: "f0c" in done and "identb" in done and "gcol" in done)
            lf = load["f0"]
            fc = done["f0c"]
            I, tI, _ = yield from norm(c, 1, [])
            s = sm[c]
            (p,) = yield take(PS)
            t = yield MM([(p.ap[0:32, :], [(V["wr1"], I.ap)])], [tI, lf] + p.w)
            (g,) = yield take(TL)
            t = yield AC(g.ap[0:32, :], p.ap[0:32, :], "Gelu", [t] + g.w, bias=V["br1"][0:32, :])
            PS.give(p, [t])
            (p,) = yield take(PS)
            t = yield MM([(p.ap[:, 8 * i:8 * i + 8], [(tl(g.ap[0:32, :], i), V["wr2"][0:32, :])]) for i in range(4)], [t] + p.w)
            TL.give(g, [t])
            lg = s[:, 52:84].rearrange("p (t n) -> p t n", t=4)
            t = yield TT(lg, p.ap[:, 0:32].rearrange("p (t n) -> p t n", t=4),
                         V["br2"].unsqueeze(1).broadcast_to([128, 4, 8]), ALU.add, [t])
            PS.give(p, [t])
            oh, w, ts = yield from topk(c, 8, lg, t)
            uw = s[:, 148:156].rearrange("p (s t) -> p s t", s=2)
            tu = yield TS(uw, w, pc[:, 22:23], None, ALU.mult, None, ts + fc)
            (p,) = yield take(PS)
            t = yield TR([(tl(p.ap[0:16, :], i), s[:, 160 + 16 * i:176 + 16 * i]) for i in range(4)], ts + p.w)
            (oT,) = yield take(TL)
            toT = yield EV(oT.ap[0:16, :], p.ap[0:16, :], [t] + oT.w)
            tob = yield EV(ohb_sb[0:16, :], p.ap[0:16, :], [toT] + mk.w)
            PS.give(p, [toT, tob])
            tm = {}
            for k in range(2):
                for m in range(4):
                    (p,) = yield take(PS)
                    sel = [identb[0:16, 8 * k + 2 * m + q:8 * k + 2 * m + q + 1].broadcast_to([16, 64]) for q in range(2)]
                    t = yield MM([(p.ap[64 * q:64 * q + 64, :], [(sel[q], ohb_sb[0:16, :])]) for q in range(2)],
                                 [tob, done["identb"]] + p.w, passes=1)
                    tm[k, m] = yield EV(mk.ap[:, 4 * k + m, :], p.ap, [t] + mk.w)
                    PS.give(p, [tm[k, m]])
            tohb = t
            U, tU = [], []
            for k in range(2):
                (p,) = yield take(PS)
                t = yield TR([(tl(p.ap, i), uw[:, k, i:i + 1].broadcast_to([128, 128])) for i in range(4)], [tu] + p.w)
                (u,) = yield take(TL)
                t = yield EV(u.ap, p.ap, [t] + u.w)
                PS.give(p, [t])
                U.append(u)
                tU.append(t)
            eb = [V["eb2a"][0:16, :], V["eb2b"][0:16, :]]
            v, tv = None, []
            ew1 = V["ew1"].rearrange("p (k m n) -> p k m n", k=2, m=4)
            ew2 = V["ew2"].rearrange("p (m n) -> p m n", m=4)
            ws1 = V["ws1"].rearrange("p (k n) -> p k n", k=2)
            wf1 = V["wf1"].rearrange("p (k n) -> p k n", k=2)
            wf2 = V["wf2"].rearrange("p (k n) -> p k n", k=2)
            lastmask = []
            for it in range(2):
                g, tg = [], []
                for m in range(4):
                    (p,) = yield take(PS)
                    t = yield MM([(p.ap, [(ew1[:, 0, m, :], I.ap)] + ([(ew1[:, 1, m, :], v.ap)] if it else []))],
                                 [tI, lf] + tv + p.w)
                    (b,) = yield take(TL)
                    t = yield AC(b.ap, p.ap, "Gelu", [t] + b.w, bias=V["eb1"][:, m:m + 1])
                    PS.give(p, [t])
                    g.append(b)
                    tg.append(t)
                (p,) = yield take(PS)
                t = yield MM([(p.ap[0:64, :], [(ws1[:, 0, :], I.ap)] + ([(ws1[:, 1, :], v.ap)] if it else []))],
                             [tI, lf] + tv + p.w)
                (gs,) = yield take(TL)
                t1 = yield AC(gs.ap[0:64, :], p.ap[0:64, :], "Gelu", [t] + gs.w, bias=V["bs1"][0:64, :])
                PS.give(p, [t1])
                t2 = yield vec(lambda e, gs=gs: e.memset(gs.ap[64:65, :], 1.0), gs.ap, gs.w, ("DVE",), rate=0.5)
                tgs = [t1, t2]
                (err,) = yield take(TL)
                terr = yield TS(err.ap, I.ap, V["mu"], None, ALU.subtract, None, [tI, lf] + err.w, BOTH, rate=0.5)
                vacc = xacc = None
                gfree = [[] for _ in range(4)]
                for k in range(-1, 2):
                    ps = yield take(PS, 3 if it else 2)
                    cols = (0, 1, 2) if it else (1, 2)
                    if k < 0:
                        tp = []
                        for q, cc in zip(ps, cols):
                            t = yield MM([(q.ap, [(V["ws2"][0:65, 128 * cc:128 * cc + 128], gs.ap[0:65, :])])], tgs + [lf] + q.w)
                            tp.append(t)
                        TL.give(gs, tp)
                    else:
                        for q, cc in zip(ps, cols):
                            t = yield MMadd([(q.ap, eb[k][:, 128 * cc:128 * cc + 128], oT.ap[0:16, :])], [toT, lf] + q.w, start=True)
                        for m in range(4):
                            (gm,) = yield take(TL)
                            t = yield TT(gm.ap, g[m].ap, mk.ap[:, 4 * k + m, :], ALU.mult, [tg[m], tm[k, m]] + gm.w, BOTH)
                            gfree[m].append(t)
                            lastmask = lastmask[-7:] + [t]
                            t = yield MMadd([(q.ap, ew2[:, m, 128 * cc:128 * cc + 128], gm.ap) for q, cc in zip(ps, cols)], [t, lf], stop=False) \
                                if m < 3 else PEop(
                                    lambda e, ps=ps, cols=cols, gm=gm: [e.matmul(q.ap, ew2[:, 3, 128 * cc:128 * cc + 128], gm.ap, start=False, stop=True)
                                                                        for q, cc in zip(ps, cols)][-1], 2560, [t, lf])
                            TL.give(gm, [t])
                        tp = [t] * len(ps)
                        if k == 1:
                            for m in range(4):
                                TL.give(g[m], gfree[m])
                    pb, pg = ps[-2], ps[-1]
                    tpb, tpg = tp[-2], tp[-1]
                    if it:
                        (T,) = yield take(TL)
                        ta = yield AC(T.ap, ps[0].ap, "Tanh", [tp[0]] + T.w, scale=0.5)
                        PS.give(ps[0], [ta])
                    (Gt,) = yield take(TL)
                    tgt = yield AC(Gt.ap, pg.ap, "Tanh", [tpg] + Gt.w, scale=0.5)
                    PS.give(pg, [tgt])
                    (A,) = yield take(TL)
                    t = yield AC(A.ap, pb.ap, "Abs", [tpb] + A.w)
                    t = yield AC(A.ap, A.ap, "Exp", [t], scale=-1.0)
                    t = yield AC(A.ap, A.ap, "Ln", [t], bias=1.0)
                    t = yield STT(A.ap, pb.ap, 0.0, A.ap, ALU.max, ALU.add, [t])
                    PS.give(pb, [t])
                    t = yield TT(A.ap, A.ap, err.ap, ALU.mult, [t, terr], BOTH)
                    ter = t
                    if it:
                        ta = yield STT(T.ap, T.ap, 1.0, v.ap, ALU.add, ALU.mult, [ta] + tv)
                        tvr = ta
                        t = yield STT(A.ap, T.ap, 0.5, A.ap, ALU.mult, ALU.subtract, [ta, t])
                        TL.give(T, [t])
                        if k < 0:
                            t = yield TS(A.ap, A.ap, pc[:, 21:22], None, ALU.mult, None, [t] + fc, BOTH, rate=0.5)
                        else:
                            t = yield TT(A.ap, A.ap, U[k].ap, ALU.mult, [t, tU[k]], BOTH)
                    elif k < 0:
                        t = yield TS(A.ap, A.ap, pc[:, 23:24], None, ALU.mult, None, [t] + fc, BOTH, rate=0.5)
                    else:
                        t = yield STT(A.ap, A.ap, -1.0, U[k].ap, ALU.mult, ALU.mult, [t, tU[k]])
                    tA = t
                    t = yield STT(Gt.ap, Gt.ap, 1.0, A.ap, ALU.add, ALU.mult, [tgt, tA])
                    if k < 0:
                        vacc, xacc, tva, txa = A, Gt, [tA, t], [t]
                    else:
                        a = yield TT(vacc.ap, vacc.ap, A.ap, ALU.add, [tA, t] + tva, BOTH)
                        b = yield TT(xacc.ap, xacc.ap, Gt.ap, ALU.add, [t] + txa, BOTH)
                        TL.give(A, [a])
                        TL.give(Gt, [b])
                        tva, txa = [a], [b]
                TL.give(err, [ter])
                if it:
                    TL.give(v, [tvr])
                    TL.give(vacc, tva)
                v, tv = vacc, tva
                t = yield STT(xacc.ap, xacc.ap, 0.05, I.ap, ALU.mult, ALU.add, txa + [tI])
                xn, tx = xacc, t
                (p,) = yield take(PS)
                t = yield MM([(p.ap[0:32, :], [(V["wh1"], xn.ap)])], [tx, lf] + p.w)
                (gh,) = yield take(TL)
                t = yield AC(gh.ap[0:32, :], p.ap[0:32, :], "Gelu", [t] + gh.w, bias=V["bh1"][0:32, :])
                PS.give(p, [t])
                f, tf = [], []
                for m in range(2):
                    (p,) = yield take(PS)
                    a = yield MM([(p.ap, [(wf1[:, m, :], xn.ap)])], [tx, lf] + p.w)
                    (b,) = yield take(TL)
                    a2 = yield AC(b.ap, p.ap, "Gelu", [a] + b.w, bias=V["bf1"][:, m:m + 1])
                    PS.give(p, [a2])
                    f.append(b)
                    tf.append(a2)
                TL.give(xn, [a])
                ps = yield take(PS, 2)
                t = yield MM([(ps[0].ap, [(V["wh2"][0:32, :].broadcast_to([32, 128]), gh.ap[0:32, :])])], [t] + ps[0].w)
                (th_,) = yield take(TL)
                t2 = yield AC(th_.ap, ps[0].ap, "Tanh", [t] + th_.w + fc, bias=pc[:, 24:25], scale=0.5)
                TL.give(gh, [t])
                t = yield MM([(ps[1].ap, [(wf2[:, m, :], f[m].ap) for m in range(2)])], tf + ps[1].w)
                for b in f:
                    TL.give(b, [t])
                (r,) = yield take(TL)
                t3 = yield TS(r.ap, ps[1].ap, V["bf2"], pc[:, 25:26], ALU.add, ALU.mult, [t] + r.w + fc)
                PS.give(ps[0], [t2])
                PS.give(ps[1], [t3])
                t = yield STT(r.ap, th_.ap, 1.0, r.ap, ALU.add, ALU.mult, [t2, t3])
                TL.give(th_, [t])
                tI = yield TT(I.ap, I.ap, r.ap, ALU.add, [t, tI, a, tx], BOTH)
                TL.give(r, [tI])
            MK.give(mk, lastmask + [tohb])
            TL.give(oT, [tp[-1]])
            for u in U:
                TL.give(u, [tA])
            t = yield TS(I.ap, I.ap, pc[:, 18:19], None, ALU.mult, None, [tI, done["gcol"]], BOTH, rate=0.5)
            (p,) = yield take(PS)
            t = yield TR([(tl(p.ap, i), tl(I.ap, i)) for i in range(4)], [t] + p.w)
            TL.give(I, [t])
            xc = xs[:, 4 * c:4 * c + 4, :]
            t = yield TT(xc, tile4(p.ap), xc, ALU.add, [t] + xt[c])
            PS.give(p, [t])
            xt[c] = [t]
            TL.promised -= 18

        def L1A(c):
            yield ("reserve", TL, 6)
            yield ("until", lambda: "L1A" in done and "CQ" in done)
            l1 = load["l1"]
            h, th, tx = yield from norm(c, 2, [])
            yield from bias_rows(c, V["bo1"], done["L1A"] + [tx])
            (vx,) = yield take(VX)
            (p,) = yield take(PS)
            t = yield MM([(tl(p.ap, i), [(tl(h.ap, i), V["wv1"])]) for i in range(4)], [th, l1] + p.w)
            tv = [(yield EV(vx.ap[:, :, :, 0:16], p.ap.rearrange("p (t h n) -> p t h n", t=4, h=8), [t] + vx.w))]
            PS.give(p, tv)
            nd = yield take(PS, 2)
            tnd = []
            for hd in range(8):
                maps = []
                for k in range(2):
                    (p,) = yield take(PS)

                    t = yield MM([(p.ap, [(CQ[:, 8 * k + hd, :], h.ap)])], [th] + done["CQ"] + p.w)
                    (E,) = yield take(TL)
                    if k:
                        t2 = yield TS(E.ap, p.ap, 0.0, None, ALU.min, None, [t] + E.w)
                        t2 = yield AC(E.ap, E.ap, "Exp", [t2])
                    else:
                        t2 = yield AC(E.ap, p.ap, "Relu", [t] + E.w, scale=-1.0)
                        t2 = yield AC(E.ap, E.ap, "Exp", [t2], scale=-1.0)
                    t2 = yield STT(E.ap, p.ap, 1.0, E.ap, ALU.add, ALU.max, [t2])
                    PS.give(p, [t2])
                    maps.append((E, t2))
                (qf, tq), (kf, tk) = maps
                (p,) = yield take(PS)
                t = yield MM([(tl(p.ap, i), [(tl(kf.ap, i), tl(qf.ap, i))]) for i in range(4)], [tq, tk] + p.w)
                TL.give(qf, [t])
                TL.give(kf, [t])
                (B,) = yield take(TL)
                t = yield TT(tile4(B.ap), tile4(p.ap), V["block"].unsqueeze(1).broadcast_to([128, 4, 128]), ALU.mult, [t] + B.w)
                PS.give(p, [t])
                t = yield MM([(nd[i // 2].ap[:, (i % 2) * 136 + 17 * hd:(i % 2) * 136 + 17 * hd + 17],
                               [(tl(B.ap, i), vx.ap[:, i, hd, :])]) for i in range(4)],
                             [t] + tv + done["vones"] + nd[0].w + nd[1].w)
                TL.give(B, [t])
                tnd = [t]
            TL.give(h, tnd)
            VX.give(vx, tnd)
            (o,) = yield take(TL)
            to = []
            for j in range(2):
                z = sm[c][:, 500 + 16 * j:516 + 16 * j].rearrange("p (t n) -> p t n", t=2)
                v4 = nd[j].ap[:, 0:272].rearrange("p (t n k) -> p t n k", t=2, n=8)
                a = yield TS(z, v4[:, :, :, 16], 1e-8, None, ALU.add, None, tnd)
                a = yield vec(lambda e, z=z: e.reciprocal(z, z), z, [a], ("DVE",))
                for i in range(2):
                    b = yield TT(tl(o.ap, 2 * j + i).rearrange("p (n k) -> p n k", n=8), v4[:, i, :, 0:16],
                                 z[:, i, :].unsqueeze(2).broadcast_to([128, 8, 16]), ALU.mult, [a] + o.w)
                    to.append(b)
                PS.give(nd[j], to[-2:])
            oT, t = yield from turned(o, to)
            t = yield from project_out(c, oT.ap, [t], V["wo1"], done["L1A"])
            TL.give(oT, [t])
            TL.promised -= 6

        def L1F(c):
            yield ("reserve", TL, 7)
            yield ("until", lambda: "L1F" in done)
            l1 = load["l1"]
            h, th, tx = yield from norm(c, 3, [])
            s = sm[c]
            (p,) = yield take(PS)
            t = yield MM([(p.ap[:, 10 * i:10 * i + 10], [(tl(h.ap, i), V["wge"])]) for i in range(4)], [th, l1] + p.w)
            lg = s[:, 52:92].rearrange("p (t n) -> p t n", t=4)
            t = yield TT(lg, p.ap[:, 0:40].rearrange("p (t n) -> p t n", t=4),
                         V["bge"].unsqueeze(1).broadcast_to([128, 4, 10]), ALU.add, [t])
            PS.give(p, [t])
            pen = s[:, 92:100].rearrange("p (t n) -> p t n", t=4)
            gd = s[:, 440:444]
            a = yield TT(gd, lg[:, :, 1], lg[:, :, 0], ALU.subtract, [t])
            b0 = yield TT(pen[:, :, 0], lg[:, :, 1], lg[:, :, 0], ALU.is_gt, [t])
            b1 = yield TS(pen[:, :, 1], pen[:, :, 0], 1.0e30, -1.0e30, ALU.mult, ALU.add, [b0])
            b0 = yield TS(pen[:, :, 0], pen[:, :, 0], -1.0e30, None, ALU.mult, None, [b0, b1])
            gp = s[:, 444:448]
            a = yield AC(gd, gd, "Abs", [a])
            a = yield AC(gd, gd, "Exp", [a], scale=-1.0)
            em = s[:, 448:480].rearrange("p (t n) -> p t n", t=4)
            te = yield TT(s[:, 448:480].rearrange("p (t a n) -> p t a n", t=4, a=2),
                          lg[:, :, 2:10].rearrange("p t (a n) -> p t a n", a=2),
                          pen.unsqueeze(3).broadcast_to([128, 4, 2, 4]), ALU.add, [t, b0, b1])
            oh, w, ts = yield from topk(c, 8, em, te)
            mx = s[:, 100:132].rearrange("p (t n) -> p t n", t=4)
            pe = s[:, 300:332].rearrange("p (t n) -> p t n", t=4)
            t = yield TT(pe, em, mx[:, :, 0:1].broadcast_to([128, 4, 8]), ALU.subtract, ts)
            t = yield AC(s[:, 300:332], s[:, 300:332], "Exp", [t])
            den = s[:, 484:488]
            d = yield RED(den, pe, ALU.add, [t])
            d = yield STT(den, gd, 1.0, den, ALU.add, ALU.mult, [d, a])
            d = yield vec(lambda e: e.reciprocal(den, den), den, [d], ("DVE",))
            b = yield TT(oh[:, :, 0, :], oh[:, :, 0, :], oh[:, :, 1, :], ALU.add, ts)
            t = yield TT(pe, pe, oh[:, :, 0, :], ALU.mult, [t, b, d])
            tse = yield TT(pe, pe, den.unsqueeze(2).broadcast_to([128, 4, 8]), ALU.mult, [t, d])

            def swiglu(wt):
                out = []
                for j in range(2):
                    ps = yield take(PS, 2)
                    t1 = yield MM([(ps[0].ap, [(wt[:, 128 * j:128 * j + 128], h.ap)])], [th, l1] + ps[0].w)
                    t2 = yield MM([(ps[1].ap, [(wt[:, 256 + 128 * j:384 + 128 * j], h.ap)])], [th, l1] + ps[1].w)
                    (T,) = yield take(TL)
                    a = yield AC(T.ap, ps[0].ap, "Tanh", [t1] + T.w, scale=0.5)
                    a = yield STT(T.ap, T.ap, 1.0, ps[0].ap, ALU.add, ALU.mult, [a])
                    PS.give(ps[0], [a])
                    a = yield TT(T.ap, T.ap, ps[1].ap, ALU.mult, [a, t2])
                    PS.give(ps[1], [a])
                    out.append((T, a))
                return out, t2

            sh, _ = yield from swiglu(V["win"])
            hh, t2 = yield from swiglu(V["w11"])
            TL.give(h, [t2])
            wou = V["wou"].rearrange("p (k n) -> p k n", k=2)
            w21 = V["w21"].rearrange("p (k n) -> p k n", k=2)
            wt = done["L1F"]
            (p,) = yield take(PS)
            t = yield MM([(tl(p.ap, i), [(tl(sh[k][0].ap, i), wou[:, k, :]) for k in range(2)]) for i in range(4)],
                         [sh[0][1], sh[1][1]] + wt + p.w)
            TL.give(sh[0][0], [t])
            TL.give(sh[1][0], [t])
            xc = xs[:, 4 * c:4 * c + 4, :]
            t = yield TT(xc, tile4(p.ap), xc, ALU.add, [t] + xt[c])
            PS.give(p, [t])
            fin = []
            for i in range(4):
                xi = xs[:, 4 * c + i, :]
                tx = t
                for half in range(2):
                    (p,) = yield take(PS)
                    t3 = yield MM([(p.ap, [(tl(hh[k][0].ap, i), w21[:, k, 512 * half:512 * half + 512]) for k in range(2)])],
                                  [hh[0][1], hh[1][1]] + wt + p.w)
                    for e in range(4):
                        tx = yield STT(xi, tl(p.ap, e), pe[:, i, 4 * half + e:4 * half + e + 1], xi, ALU.mult, ALU.add,
                                       [t3, tse, tx])
                    PS.give(p, [tx])
                fin.append(tx)
            TL.give(hh[0][0], [t3])
            TL.give(hh[1][0], [t3])
            xt[c] = fin
            TL.promised -= 7

        def L2A(c):
            yield ("reserve", TL, 9)
            yield ("until", lambda: "L2A" in done)
            l2 = load["l2"]
            cs = yield take(TL, 2)
            tc = []
            for k in range(2):
                a = yield DMA(cs[k].ap, cs_d[k, :, c * W:(c + 1) * W], f"d_cs{c}{k}", cs[k].w, 1 << 18)
                tc.append(a)
            h, th, tx = yield from norm(c, 4, [])
            yield from bias_rows(c, brow2[:, :], done["L2A"] + [tx])
            qk = []
            for a, b in (("wk", "wks"), ("wq", "wqs")):
                ps = yield take(PS, 2)
                t1 = yield MM([(ps[0].ap, [(V[a], h.ap)])], [th, l2] + ps[0].w)
                t2 = yield MM([(ps[1].ap, [(V[b], h.ap)])], [th, l2] + ps[1].w)
                (r, r2) = yield take(TL, 2)
                t1 = yield TT(r.ap, ps[0].ap, cs[0].ap, ALU.mult, [t1, tc[0]] + r.w)
                t2 = yield TT(r2.ap, ps[1].ap, cs[1].ap, ALU.mult, [t2, tc[1]] + r2.w)
                PS.give(ps[0], [t1])
                PS.give(ps[1], [t2])
                t = yield TT(r.ap, r.ap, r2.ap, ALU.add, [t1, t2], BOTH)
                TL.give(r2, [t])
                qk.append((r, t))
            TL.give(cs[0], [t1])
            TL.give(cs[1], [t2])
            (kT, tk), (qT, tq) = qk
            (R,) = yield take(PS)
            for e in range(8):
                (p,) = yield take(PS)
                t = yield MM([(p.ap, [(V["wvr"][:, 128 * e:128 * e + 128], h.ap)])], [th, l2] + p.w)
                tvv = t
                (kv,) = yield take(TL)
                t = yield TT(kv.ap, p.ap, kT.ap, ALU.mult, [t, tk] + kv.w)
                tkl = t
                PS.give(p, [t])
                if c:
                    yield ("until", lambda: (c - 1, e) in c2t)
                init, wi = (carry2[:, c - 1, e:e + 1], [c2t[c - 1, e]]) if c else (0.0, [])
                (st,) = yield take(TL)
                t = yield vec(lambda en, st=st, kv=kv, init=init: en.tensor_tensor_scan(
                    st.ap, decay.broadcast_to([128, W]), kv.ap, init, ALU.mult, ALU.add),
                    st.ap, [t, l2] + wi + st.w, ("DVE",), rate=2.0)
                TL.give(kv, [t])
                c2t[c, e] = yield CP(carry2[:, c, e:e + 1], st.ap[:, W - 1:W], [t], ("POOL",))
                t = yield TT(st.ap, st.ap, qT.ap, ALU.mult, [t, tq, c2t[c, e]], BOTH)
                tql = t
                t = yield MM([(tl(R.ap, i).rearrange("p (h e) -> p h e", e=8)[:, :, e], [(tl(st.ap, i), V["ind"])])
                              for i in range(4)], [t] + R.w)
                TL.give(st, [t])
            TL.give(h, [tvv])
            TL.give(kT, [tkl])
            TL.give(qT, [tql])
            s = sm[c]
            nm, vs = s[:, 490:554], s[:, 554:618]
            R3d = R.ap.rearrange("p (g n) -> p g n", n=8)
            a = yield RED(nm, R3d, ALU.add, [t])
            a = yield TS(nm, nm, -0.125, None, ALU.mult, None, [a])
            (xc, sq) = yield take(TL, 2)
            x3 = xc.ap.rearrange("p (g n) -> p g n", n=8)
            t = yield TT(x3, R3d, nm.unsqueeze(2).broadcast_to([128, 64, 8]), ALU.add, [a] + xc.w)
            PS.give(R, [t])
            b = yield TT(sq.ap, xc.ap, xc.ap, ALU.mult, [t] + sq.w, BOTH)
            b = yield RED(vs, sq.ap.rearrange("p (g n) -> p g n", n=8), ALU.add, [b])
            TL.give(sq, [b])
            b = yield TS(vs, vs, 0.125, 1e-5, ALU.mult, ALU.add, [b])
            b = yield AC(vs, vs, "Sqrt", [b])
            b = yield vec(lambda e: e.reciprocal(vs, vs), vs, [b], ("DVE",), rate=8)
            t = yield TT(x3, x3, vs.unsqueeze(2).broadcast_to([128, 64, 8]), ALU.mult, [t, b], BOTH)
            oT, t = yield from turned(xc, [t])
            t = yield from project_out(c, oT.ap, [t], V["wo2"], done["L2A"])
            TL.give(oT, [t])
            TL.promised -= 9

        def L2F(c):
            yield ("reserve", TL, 8)
            yield ("until", lambda: "L2F" in done)
            l2 = load["l2"]
            h, th, tx = yield from norm(c, 5, [])
            s = sm[c]
            (p,) = yield take(PS)
            t = yield MM([(p.ap[:, 16 * i:16 * i + 16], [(tl(h.ap, i), V["rw"])]) for i in range(4)], [th, l2] + p.w)
            lg = s[:, 500:564].rearrange("p (t n) -> p t n", t=4)
            t = yield CP(lg, p.ap[:, 0:64].rearrange("p (t n) -> p t n", t=4), [t])
            PS.give(p, [t])
            oh, w, ts = yield from topk(c, 16, lg, t)
            se, tse = yield from weights(c, 16, oh, w, ts)
            (p,) = yield take(PS)
            t = yield TR([(tl(p.ap[0:16, :], i), se[:, i, :]) for i in range(4)], [tse] + p.w)
            (sT,) = yield take(TL)
            tsT = yield EV(sT.ap[0:16, :], p.ap[0:16, :], [t] + sT.w)
            PS.give(p, [tsT])
            wt = done["L2F"]
            (Y,) = yield take(PS)

            def fn(e):
                e.matmul(Y.ap, zerob[0:1, 0:128], zerob[0:1, :], start=True, stop=False)
                for i in range(4):
                    x = e.matmul(tl(Y.ap, i), tl(sT.ap[0:16, :], i), V["dbn"][0:16, :], start=False, stop=False)
                return x
            t = yield PEop(fn, 1100, [tsT, done["zerob"]] + wt + Y.w)
            TL.give(sT, [t])
            gu = V["gup"].rearrange("p (e f a) -> p e f a", e=16, a=2)
            dw = V["dwn"].rearrange("p (k n) -> p k n", k=8)
            for m in range(8):
                ps = yield take(PS, 3)
                t1 = yield MM([(ps[0].ap, [(gu[:, 2 * m:2 * m + 2, :, 0], h.ap)])], [th, l2] + ps[0].w)
                t2 = yield MM([(ps[1].ap, [(gu[:, 2 * m:2 * m + 2, :, 1], h.ap)])], [th, l2] + ps[1].w)
                (g, T, u, x) = yield take(TL, 4)
                t3 = yield CP(x.ap.rearrange("p (t a n) -> p t a n", t=4, a=2),
                              se[:, :, 2 * m:2 * m + 2].unsqueeze(3).broadcast_to([128, 4, 2, 64]), [tse] + x.w, BOTH)
                t3 = yield TR([(tl(ps[2].ap, i), tl(x.ap, i)) for i in range(4)], [t3] + ps[2].w)
                TL.give(x, [t3])
                a = yield TS(g.ap, ps[0].ap, V["gb"][:, m:m + 1], 7.0, ALU.add, ALU.min, [t1, l2] + g.w)
                PS.give(ps[0], [a])
                b = yield AC(u.ap, ps[1].ap, "Identity", [t2] + wt + u.w, bias=V["ub"][:, m:m + 1])
                PS.give(ps[1], [b])
                b = yield TS(u.ap, u.ap, -6.0, 8.0, ALU.max, ALU.min, [b], BOTH, rate=0.5)
                a2 = yield AC(T.ap, g.ap, "Tanh", [a] + T.w, scale=0.851)
                b = yield TT(u.ap, u.ap, ps[2].ap, ALU.mult, [b, t3])
                PS.give(ps[2], [b])
                a = yield STT(g.ap, T.ap, 1.0, g.ap, ALU.add, ALU.mult, [a2])
                TL.give(T, [a])
                a = yield TT(g.ap, g.ap, u.ap, ALU.mult, [a, b], BOTH)
                TL.give(u, [a])
                t = yield MMadd([(tl(Y.ap, i), tl(g.ap, i), dw[:, m, :]) for i in range(4)], [a] + wt, stop=(m == 7))
                TL.give(g, [t])
            TL.give(h, [t2])
            xc = xs[:, 4 * c:4 * c + 4, :]
            t = yield TT(xc, tile4(Y.ap), xc, ALU.add, [t] + xt[c])
            PS.give(Y, [t])
            xt[c] = [t]
            TL.promised -= 8

        def L3A(c):
            yield ("reserve", TL, 8)
            yield ("until", lambda: "L3A" in done)
            l3 = load["l3"]
            wt = done["L3A"]
            h, th, tx = yield from norm(c, 6, [])
            yield from bias_rows(c, V["bo3"], wt + [tx])
            s = sm[c]
            (p,) = yield take(PS)
            t = yield MM([(p.ap[:, 32 * i:32 * i + 32], [(tl(h.ap, i), V["wbc"])]) for i in range(4)], [th, l3] + p.w)
            bc = s[:, 160:288].rearrange("p (t n) -> p t n", t=4)
            tbc = yield TT(bc, p.ap[:, 0:128].rearrange("p (t n) -> p t n", t=4),
                           V["bbc"].unsqueeze(1).broadcast_to([128, 4, 32]), ALU.add, [t])
            PS.give(p, [tbc])
            ps = yield take(PS, 3)
            t1 = yield MM([(ps[0].ap, [(V["wz"], h.ap)])], [th, l3] + ps[0].w)
            t2 = yield MM([(ps[1].ap, [(V["wdt"], h.ap)])], [th, l3] + ps[1].w)
            t3 = yield MM([(ps[2].ap, [(V["wx"], h.ap)])], [th, l3] + ps[2].w)
            TL.give(h, [t3])
            (tz, dt, dx) = yield take(TL, 3)
            tzt = yield AC(tz.ap, ps[0].ap, "Tanh", [t1] + wt + tz.w, bias=V["bz"], scale=0.5)
            PS.give(ps[0], [tzt])
            ab = yield AC(dt.ap, ps[1].ap, "Abs", [t2] + dt.w, bias=V["bdt"])
            a = yield AC(dt.ap, dt.ap, "Exp", [ab], scale=-1.0)
            a = yield AC(dt.ap, dt.ap, "Ln", [a], bias=1.0)
            b = yield TS(dx.ap, ps[1].ap, V["bdt"], 0.0, ALU.add, ALU.max, [ab] + dx.w)
            PS.give(ps[1], [b])
            tdt = yield TT(dt.ap, dt.ap, dx.ap, ALU.add, [a, b])
            tdx = yield STT(dx.ap, ps[2].ap, V["bx"], dt.ap, ALU.add, ALU.mult, [t3, tdt])
            PS.give(ps[2], [tdx])
            (Y,) = yield take(PS)
            for n in range(16):
                (A, db) = yield take(TL, 2)
                ta = yield AC(A.ap, dt.ap, "Exp", [tdt] + wt + A.w, scale=Acol[:, n:n + 1])
                (p,) = yield take(PS)
                t = yield TR([(tl(p.ap, i), bc[:, i, n:n + 1].broadcast_to([128, 128])) for i in range(4)], [tbc] + p.w)
                t = yield TT(db.ap, dx.ap, p.ap, ALU.mult, [t, tdx] + db.w)
                tdl = t
                PS.give(p, [t])
                if c:
                    yield ("until", lambda: (c - 1, n) in c3t)
                init, wi = (carry3[:, c - 1, n:n + 1], [c3t[c - 1, n]]) if c else (0.0, [])
                (H,) = yield take(TL)
                t = yield vec(lambda e, A=A, db=db, H=H, init=init: e.tensor_tensor_scan(H.ap, A.ap, db.ap, init, ALU.mult, ALU.add),
                              H.ap, [ta, t] + wi + H.w, ("DVE",), rate=2.0)
                TL.give(A, [t])
                TL.give(db, [t])
                c3t[c, n] = yield CP(carry3[:, c, n:n + 1], H.ap[:, W - 1:W], [t], ("POOL",))
                (p,) = yield take(PS)
                t2 = yield TR([(tl(p.ap, i), bc[:, i, 16 + n:17 + n].broadcast_to([128, 128])) for i in range(4)], [tbc] + p.w)
                t = yield TT(H.ap, H.ap, p.ap, ALU.mult, [t, t2, c3t[c, n]])
                PS.give(p, [t])
                t = yield MMadd([(Y.ap, V["ident"], H.ap)], [t] + Y.w, start=(n == 0), stop=(n == 15))
                TL.give(H, [t])
            TL.give(dt, [ta])
            TL.give(dx, [tdl])
            t = yield STT(tz.ap, tz.ap, 1.0, Y.ap, ALU.add, ALU.mult, [t, tzt])
            PS.give(Y, [t])
            t = yield from project_out(c, tz.ap, [t], V["wo3"], wt)
            TL.give(tz, [t])
            TL.promised -= 8

        def L3F(c):
            yield ("reserve", TL, 9)
            yield ("until", lambda: "L3F" in done)
            wt = done["L3F"]
            h, th, tx = yield from norm(c, 7, [])
            s = sm[c]
            (p,) = yield take(PS)
            t = yield MM([(p.ap[:, 8 * i:8 * i + 8], [(tl(h.ap, i), V["gw"])]) for i in range(4)], [th] + wt + p.w)
            lg = s[:, 52:84].rearrange("p (t n) -> p t n", t=4)
            t = yield CP(lg, p.ap[:, 0:32].rearrange("p (t n) -> p t n", t=4), [t])
            PS.give(p, [t])
            oh, w, ts = yield from topk(c, 8, lg, t)
            se, tse = yield from weights(c, 8, oh, w, ts)
            (acc,) = yield take(TL)
            tacc = [[] for _ in range(4)]
            for e in range(8):
                yield ("until", lambda: (c, e) in ring)
                rb, tr = ring[c, e]
                w1, w3 = rb.ap[:, 0:512], rb.ap[:, 512:1024]
                w2 = rb.ap[:, 1024:1536].rearrange("p (f n) -> p f n", f=4)
                hid, tH = [], []
                for f in range(4):
                    ps = yield take(PS, 2)
                    t1 = yield MM([(ps[0].ap, [(tl(w1, f), h.ap)])], [th, tr] + ps[0].w)
                    t2 = yield MM([(ps[1].ap, [(tl(w3, f), h.ap)])], [th, tr] + ps[1].w)
                    (T, u) = yield take(TL, 2)
                    a = yield AC(T.ap, ps[0].ap, "Tanh", [t1] + T.w, scale=0.5)
                    b = yield EV(u.ap, ps[1].ap, [t2] + u.w)
                    PS.give(ps[1], [b])
                    a = yield STT(T.ap, T.ap, 1.0, ps[0].ap, ALU.add, ALU.mult, [a])
                    PS.give(ps[0], [a])
                    a = yield TT(T.ap, T.ap, u.ap, ALU.mult, [a, b], BOTH)
                    TL.give(u, [a])
                    hid.append(T)
                    tH.append(a)
                (p,) = yield take(PS)
                t = yield MM([(tl(p.ap, i), [(tl(hid[f].ap, i), w2[:, f, :]) for f in range(4)]) for i in range(4)], tH + [tr] + p.w)
                R3.give(rb, [t])
                for q in hid:
                    TL.give(q, [t])
                free = []
                for i in range(4):
                    ai = tl(acc.ap, i)
                    if e == 0:
                        tacc[i] = yield TS(ai, tl(p.ap, i), se[:, i, e:e + 1], None, ALU.mult, None, [t, tse] + acc.w)
                    else:
                        tacc[i] = yield STT(ai, tl(p.ap, i), se[:, i, e:e + 1], ai, ALU.mult, ALU.add, [t, tse, tacc[i]])
                    free.append(tacc[i])
                PS.give(p, free)
            TL.give(h, [t2])
            a = yield TT(tile4(acc.ap), tile4(acc.ap), GR[:, 7, :].unsqueeze(1).broadcast_to([128, 4, 128]), ALU.mult, tacc + wt, BOTH)
            xc = xs[:, 4 * c:4 * c + 4, :]
            a = yield TT(xc, xc, tile4(acc.ap), ALU.add, [a] + xt[c], BOTH)
            TL.give(acc, [a])
            ov = out_d.rearrange("a (n p) d -> p (a n) d", p=128)
            yield DMA(ov[:, 4 * c:4 * c + 4, :], xc, "d_out", [a], 1 << 18)
            TL.promised -= 9

        decay = sb("decay_sb", [128, 1])

        def consts():
            load["decay"] = yield DMA(decay[:, :], pk["decay"], "d_decay", [], 512)

        def chunk(c):
            for layer in (L0A, L0F, L1A, L1F, L2A, L2F, L3A, L3F):
                if layer is L2A:
                    yield ("until", lambda: "decay" in load)
                yield from layer(c)

        run(Q, [chunk(c) for c in range(NC)] + [loads(), prep(), stream3(), consts()])

        sems = {k: ctx.enter_context(nc.semaphore("s_" + k)) for k in Q.count}
        block = ctx.enter_context(nc.Block())

        def play(name, eng):
            for waits, fn, key, by in Q.items[name]:
                for k, n in waits:
                    eng.wait_ge(sems[k], n)
                fn(eng).then_inc(sems[key], by)

        @block.sync
        def _(eng):
            play("SP", eng)
            eng.wait_ge(sems["d_out"], Q.count["d_out"])

        @block.tensor
        def _(eng):
            play("PE", eng)

        @block.scalar
        def _(eng):
            play("ACT", eng)

        @block.vector
        def _(eng):
            play("DVE", eng)

        @block.gpsimd
        def _(eng):
            play("POOL", eng)


FUNCS = {"Sqrt": ACT.Sqrt, "Relu": ACT.Relu, "Gelu": ACT.Gelu, "Tanh": ACT.Tanh, "Exp": ACT.Exp, "Ln": ACT.Ln, "Abs": ACT.Abs, "Identity": ACT.Identity}


def getattr_act(name):
    return FUNCS[name]


def _laid_out(d):
    f = np.float32
    col = lambda a: np.asarray(a, f).reshape(-1, 1)
    rows = lambda a: np.broadcast_to(np.asarray(a, f).reshape(1, -1), (128, np.asarray(a).size))
    A = {k: np.asarray(v) for k, v in d.items()}
    p = np.arange(128)
    out = {}
    out["ident"] = np.eye(128, dtype=f)
    out["mask"] = np.where(p[None, :] < p[:, None], 0.0, -1e30).astype(f)
    m0 = out["mask"].copy()
    m0[0, 0] = 0.0
    out["mask0"] = m0
    out["block"] = (p[None, :] // 32 == p[:, None] // 32).astype(f)
    out["iota"] = np.broadcast_to(np.arange(16, dtype=f), (128, 16))
    out["ind"] = (p[:, None] // 8 == np.arange(16)[None, :]).astype(f)
    out["ccol"] = np.concatenate([col(A[f"L{l}_c"]) for l in range(4)], 1)
    out["wdec"] = A["L0_attn_w_dec_attn"]
    out["w1o"] = A["L0_attn_w_out"][:, :128].T
    out["w2o"] = A["L0_attn_w_out"][:, 128:].T
    out["brow0"] = rows(A["L0_attn_b_out"])
    F = lambda n: A["L0_ffn_" + n]
    out["wr1"], out["br1"], out["wr2"], out["br2"] = F("w_r1"), col(F("b_r1")), F("w_r2"), rows(F("b_r2"))
    out["wh1"], out["bh1"], out["wh2"], out["bh2"] = F("w_h1"), col(F("b_h1")), F("w_h2"), np.broadcast_to(col(F("b_h2")), (128, 1))
    w = F("expert_w1").reshape(8, 2, 128, 64)
    out["ew1"] = w.transpose(2, 1, 0, 3).reshape(128, 1024)
    out["eb1"] = F("expert_b1").reshape(4, 128).T
    out["ew2"] = F("expert_w2").reshape(4, 128, 384).transpose(1, 0, 2).reshape(128, 1536)
    b2 = F("expert_b2")
    z = np.zeros((8, 384), f)
    out["eb2a"], out["eb2b"] = np.concatenate([b2, z]), np.concatenate([z, b2])
    out["ws1"] = F("w_s1").reshape(2, 128, 64).transpose(1, 0, 2).reshape(128, 128)
    out["bs1"] = col(F("b_s1"))
    out["ws2"] = np.concatenate([F("w_s2"), F("b_s2").reshape(1, 384)])
    out["sw"] = np.broadcast_to(col(F("shared_weight")), (128, 1))
    out["wf1"] = F("w_f1")
    out["bf1"] = F("b_f1").reshape(2, 128).T
    out["wf2"] = F("w_f2").reshape(2, 128, 128).transpose(1, 0, 2).reshape(128, 256)
    out["bf2"], out["iw"], out["mu"] = col(F("b_f2")), col(F("integration_weight")), col(F("mu"))
    wq = A["L1_attn_w_qkv"]
    out["wv1"] = wq[256:].T
    out["wo1"], out["bo1"] = A["L1_attn_w_out"].T, rows(A["L1_attn_b_out"])
    F = lambda n: A["L1_ffn_" + n]
    out["win"], out["w11"] = F("w_in").T, F("w1").T
    out["wou"] = F("w_out").T.reshape(2, 128, 128).transpose(1, 0, 2).reshape(128, 256)
    out["w21"] = F("w2").transpose(2, 0, 1).reshape(2, 128, 8, 128).transpose(1, 0, 2, 3).reshape(128, 2048)
    out["wge"] = np.concatenate([F("wg"), F("we")]).T
    out["bge"] = np.concatenate([rows(F("gb")), rows(F("eb"))], 1)
    F = lambda n: A["L2_attn_" + n]
    swap = p ^ 1
    for n, k in (("wq", "WQ"), ("wk", "WK")):
        m = F(k).reshape(128, 128)
        out[n], out[n + "s"] = m.T, m[swap].T
    out["wvr"] = np.repeat(F("WV").transpose(2, 1, 0).reshape(128, 128), 8, axis=1)
    out["wo2"] = F("WO")
    out["gam"], out["bet"] = col(F("gamma")), col(F("beta"))
    F = lambda n: A["L2_ffn_" + n]
    out["rw"] = F("router_weight")
    out["gup"] = F("gate_up_proj").transpose(1, 0, 2).reshape(128, 2048)
    gub = F("gate_up_proj_bias")
    out["gb"], out["ub"] = gub[:, 0::2].reshape(8, 128).T, gub[:, 1::2].reshape(8, 128).T
    out["dwn"] = F("down_proj").reshape(8, 128, 128).transpose(1, 0, 2).reshape(128, 1024)
    out["dbn"] = F("down_proj_bias")
    F = lambda n: A["L3_attn_" + n]
    out["wz"], out["bz"], out["wx"], out["bx"] = F("Wz"), col(F("bz")), F("Wx"), col(F("bx"))
    out["wbc"] = np.concatenate([F("WB"), F("WC")], 1)
    out["bbc"] = np.concatenate([rows(F("bB")), rows(F("bC"))], 1)
    out["wdt"], out["bdt"], out["alog"] = F("Wdt"), col(F("bdt")), F("A_log")
    out["wo3"], out["bo3"] = F("Wout"), rows(F("bout"))
    out["gw"] = A["L3_ffn_gate_w"]

    packs = {}
    for g, items in SPEC:
        cols = []
        for name, n in items:
            a = np.asarray(out[name], f)
            assert a.shape[1] == n, (name, a.shape, n)
            if a.shape[0] < 128:
                a = np.concatenate([a, np.zeros((128 - a.shape[0], n), f)])
            cols.append(a)
        packs["p_" + g] = np.ascontiguousarray(np.concatenate(cols, 1))
    packs["t_wmod"] = np.ascontiguousarray(np.concatenate([A[f"L{l}_wmod"] for l in range(4)], 1))
    packs["t_wqkv"] = np.ascontiguousarray(wq.reshape(24, 16, 128).transpose(1, 0, 2).reshape(16, 3072))
    packs["t_proj"] = np.ascontiguousarray(A["L1_attn_proj"].transpose(1, 0, 2).reshape(16, 1024))
    F = lambda n: A["L3_ffn_" + n]
    packs["w3"] = np.ascontiguousarray(np.concatenate(
        [F("w1"), F("w3"), F("w2").reshape(8, 4, 128, 128).transpose(0, 2, 1, 3).reshape(8, 128, 512)], 2))
    packs["x"] = np.ascontiguousarray(A["L0_attn_hidden_states"])
    ex = np.arange(0, 8, 2, dtype=f) / f(8)
    angle = (f(10.0) ** (f(-4.0) * ex)).astype(f)
    pos = np.arange(S, dtype=f)
    na = (pos[:, None] * angle[None, :]).astype(f)
    pair = (p % 8) // 2
    cosT = np.cos(na.astype(np.float64)).astype(f).T[pair]
    sinT = np.sin(na.astype(np.float64)).astype(f).T[pair]
    sinT = np.where((p % 2 == 0)[:, None], -sinT, sinT).astype(f)
    packs["cs"] = np.ascontiguousarray(np.stack([cosT, sinT]))
    packs["decay"] = np.ascontiguousarray((1.0 - 2.0 ** (-5.0 - (p // 8))).astype(f).reshape(128, 1))
    return packs


def kernel(**inputs):
    import concourse.bacc as _bacc
    from concourse.bass_utils import run_bass_kernel_spmd as _run

    nc = _bacc.Bacc("TRN2", target_bir_lowering=False, num_devices=1)
    arrays = _laid_out(inputs)
    ap = {k: nc.dram_tensor(k, a.shape, F32, kind="ExternalInput").ap() for k, a in arrays.items()}
    out = nc.dram_tensor("out", (1, S, D), F32, kind="ExternalOutput").ap()
    pk = {g: ap["p_" + g] for g, _ in SPEC}
    pk["decay"] = ap["decay"]
    build(nc, ap["x"], ap["cs"], ap["w3"], pk, {k: ap["t_" + k] for k in ("wmod", "wqkv", "proj")}, out)
    r = _run(nc, [arrays], core_ids=[0])
    return r.results[0]["out"]
```

```python
import numpy as np
import concourse.bass as bass
from concourse import mybir

F32 = mybir.dt.float32
BF16 = mybir.dt.bfloat16
U32 = mybir.dt.uint32
ALU = mybir.AluOpType
ACT = mybir.ActivationFunctionType
AX = mybir.AxisListType

S, D, NT, NC, W = 2048, 128, 16, 4, 512
NJ = (2 * W + 8 * 127) // 128
SPEC = [
    ("c0", [("ident", 128), ("mask", 128), ("mask0", 128), ("block", 128), ("iota", 16), ("ind", 16), ("ccol", 4), ("pio", 1), ("three", 32)]),
    ("a0", [("wdec", 128), ("w1o", 128), ("w2o", 128), ("brow0", 128)]),
    ("f0", [("wr1", 32), ("br1", 1), ("wr2", 8), ("br2", 8), ("wh1", 32), ("bh1", 1), ("wh2", 1), ("bh2", 1),
            ("ew1", 1024), ("eb1", 4), ("ew2", 1536), ("eb2a", 384), ("eb2b", 384), ("ws1", 128), ("bs1", 1),
            ("ws2", 384), ("sw", 1), ("wf1", 256), ("bf1", 2), ("wf2", 256), ("bf2", 1), ("iw", 1), ("mu", 1)]),
    ("l1", [("wv1", 128), ("wo1", 128), ("bo1", 128), ("win", 512), ("wou", 256), ("w11", 512), ("w21", 2048),
            ("wge", 10), ("bge", 10)]),
    ("l2", [("wq", 128), ("wqs", 128), ("wk", 128), ("wks", 128), ("wvr", 1024), ("wo2", 128), ("gam", 1), ("bet", 1),
            ("rw", 16), ("gup", 2048), ("gb", 8), ("ub", 8), ("dwn", 1024), ("dbn", 128)]),
    ("l3", [("wz", 128), ("bz", 1), ("wx", 128), ("bx", 1), ("wbc", 32), ("bbc", 32), ("wdt", 128), ("bdt", 1),
            ("alog", 16), ("wo3", 128), ("bo3", 128), ("gw", 8)]),
]
TEMP = [("wmod", 4 * 768), ("wqkv", 24 * 128), ("proj", 8 * 128)]
GROUP_COLS = {g: sum(n for _, n in items) for g, items in SPEC}
WIDE = {"L0A": 2, "mask": 2, "L0F": 2, "L1A": 5, "swiglu": 2, "routed": 4, "L2A": 6, "L2F": 4, "L3A": 5, "L3F": 2}
ROOM = {"L0A": 6, "L0F": 26, "L1A": 13, "L1F": 4, "L2A": 11, "L2F": 3, "L3A": 14, "L3F": 8}
RANK = [0.4, 5.7, 0.7, 4.2, 1.1, 1.9, 5.4, 5.5]
AGE = 0.1
LATER = 2
NEAR = 1


class Tok:

    def __init__(self, key, n, t):
        self.key, self.n, self.t, self.first = key, n, t, self


class Buf:

    def __init__(self, ap, w=()):
        self.ap, self.w, self.last = ap, list(w), False


class Op:
    def __init__(self, alts, deps, queued=None):
        self.alts, self.deps, self.queued = alts, deps, queued


class Queues:

    ENG = ["PE", "ACT", "DVE", "POOL", "SP"]
    LAT = {"PE": 205, "ACT": 190, "DVE": 150, "POOL": 160, "SP": 0}

    def __init__(self):
        self.items = {e: [] for e in self.ENG}
        self.count = {}
        self.known = {e: {} for e in self.ENG}
        self.free = {e: 0.0 for e in self.ENG}
        self.tset = None
        self.warm = 0.0

    def finish(self, alt, deps):
        if isinstance(alt, list):
            (a, da), (b, db) = alt
            t = self.start(a, da) + a[2] + self.LAT[a[0]]
            return max([t, self.free[b[0]]] + [d.t for d in db]) + b[2]
        return self.start(alt, deps) + alt[2]

    def start(self, alt, deps):
        if isinstance(alt, list):
            return self.start(*alt[0])
        eng, _, _, tset, _ = alt
        t = max([self.free[eng]] + [d.t for d in deps])
        if eng == "ACT" and tset and self.tset not in tset:
            t += 1300
        return t

    def emit(self, alt, deps):
        if isinstance(alt, list):
            (a, da), (b, db) = alt
            first = self.emit(a, da)
            tok = self.emit(b, db + [first])
            tok.first = first
            return tok
        eng, fn, cost, tset, dma = alt
        t = self.start(alt, deps)
        if eng == "ACT" and tset and self.tset not in tset:
            self.tset = tset[0]
        if eng == "PE":
            if t - self.free["PE"] > 2000:
                self.warm = 0.0
            slow = min(cost, max(0.0, (4000 - self.warm) / 2))
            self.warm += cost + slow
            cost += slow
        need = {}
        for d in deps:
            if self.known[eng].get(d.key, 0) < d.n:
                need[d.key] = max(need.get(d.key, 0), d.n)
        self.known[eng].update(need)
        key, by = (dma, 16) if dma else (eng, 1)
        self.count[key] = self.count.get(key, 0) + by
        self.items[eng].append((sorted(need.items()), fn, key, by))
        self.free[eng] = t + (cost if not dma else 1050 if eng == "POOL" else 50)
        return Tok(key, self.count[key], t + cost + (0 if dma else self.LAT[eng]))


class Slots:
    def __init__(self, bufs):
        self.bufs, self.promised, self.n, self.line = list(bufs), 0, len(bufs), []

    def take(self, k):
        self.bufs.sort(key=lambda b: (b.last, max([x.t for x in b.w], default=0)))
        out, self.bufs = self.bufs[:k], self.bufs[k:]
        return out

    def give(self, b, toks):
        b.w = list(toks)
        self.bufs.append(b)


class Strand:
    def __init__(self, pri, gen):
        self.pri, self.gen, self.value, self.done = pri, gen, None, False
        self.step(None)

    def step(self, val):
        try:
            self.req = self.gen.send(val)
        except StopIteration as e:
            self.done, self.value, self.req = True, e.value, None


def run(queues, streams):
    live = [Strand(pri * 0.001, g) for pri, g in enumerate(streams)]
    while True:
        live = [s for s in live if not s.done]
        if not live:
            return
        best = None
        for s in live:
            req = s.req
            if isinstance(req, Op):
                alt = min(req.alts, key=lambda a: queues.finish(a, req.deps))
                k = (queues.start(alt, req.deps), s.pri)
                if best is None or k[0] < best[0][0] - NEAR or (abs(k[0] - best[0][0]) <= NEAR and k[1] < best[0][1]):
                    best = (k, s, alt)
                continue
            got = None
            if req[0] == "take" and len(req[1].bufs) >= req[2]:
                got = req[1].take(req[2])
            elif req[0] == "reserve":
                if s not in req[1].line:
                    req[1].line.append(s)
                if req[1].line[0] is s and req[1].n - req[1].promised >= req[2]:
                    req[1].line.pop(0)
                    req[1].promised += req[2]
                    got = True
            elif req[0] == "until" and req[1]():
                got = True
            elif req[0] == "rank":
                s.pri = got = req[1]
            elif req[0] == "spawn":
                got = [Strand(s.pri, g) for g in req[1]]
                live += got
            elif req[0] == "join" and all(x.done for x in req[1]):
                got = [x.value for x in req[1]]
            if got is not None:
                best = (None, s, got)
                break
        assert best is not None, ("stuck", [(s.pri, s.req[0], s.req[2:]) for s in live])
        k, s, what = best
        if k is not None and s.req.queued:
            s.req.queued()
        s.step(what if k is None else queues.emit(what, s.req.deps))


def par(gens, wide):
    todo, out = iter(enumerate(gens)), {}

    def worker():
        for i, g in todo:
            out[i] = yield from g

    hands = yield ("spawn", [worker() for _ in range(wide)])
    yield ("join", hands)
    return [out[i] for i in sorted(out)]


SETS = {"Gelu": ("gelu",), "Tanh": ("exp", "gelu"), "Exp": ("exp", "lnexp"), "Ln": ("lnexp",), "Sqrt": ("sqrt",), "Silu": ("silu",)}


def width(ap):
    n = 1
    for k in ap.shape[1:]:
        n *= k
    return n


def build(nc, x_d, cs_d, w3_d, pk, temps, out_d):
    from contextlib import ExitStack
    ctx = ExitStack()
    with ctx:
        def sb(name, shape, dt=F32):
            return ctx.enter_context(nc.sbuf_tensor(name, shape, dt))

        Q = Queues()
        G = {g: sb("g_" + g, [128, n]) for g, n in GROUP_COLS.items()}
        V = {}
        for g, items in SPEC:
            at = 0
            for name, n in items:
                V[name] = G[g][:, at:at + n]
                at += n

        xs = sb("xs", [128, NT, D])
        early = sb("early", [128, 4 * S])
        hT0 = early[:, 0:S]
        Vp = early[:, S:2 * S].rearrange("p (n d) -> p n d", n=NT)
        S_buf = [early[:, 2 * S:3 * S], early[:, 3 * S:4 * S]]
        vext = [sb(f"vext{i}", [128, 4, 8, 17]) for i in range(2)]
        NTILE = 38
        tiles = sb("tiles", [128, NTILE * W])
        CQ = sb("CQ", [128, 16, 128])
        gate0 = sb("gate0", [128, 128])
        gate7 = sb("gate7", [128, 128])
        mc = sb("mc", [128, 24])
        pc = sb("pc", [128, 64])
        Acol = sb("Acol", [128, 16])
        brow2 = sb("brow2", [128, 128])
        identb = sb("identb", [128, 128], BF16)
        oneb = sb("oneb", [128, 128], BF16)
        zerob = sb("zerob", [128, 128], BF16)
        carry2 = sb("carry2", [128, NC, 8])
        carry3 = sb("carry3", [128, NC, 16])
        sm = [sb(f"sm{c}", [128, 620]) for c in range(NC)]
        sm0 = [sb(f"sma{i}", [128, 12]) for i in range(NT)]
        smu = [sb(f"smu{c}", [128, 32], U32) for c in range(NC)]
        pickb = sb("pickb", [96, 1024], BF16)
        eb2 = sb("eb2", [96, 768], BF16)
        threeb = sb("threeb", [96, 32], BF16)
        trib = sb("trib", [128, 128], BF16)
        edge = sb("edge", [128, 16])
        smb = [sb(f"smb{c}", [128, 64], BF16) for c in range(NC)]
        slot = [sb(f"slot{c}", [128, 24], U32) for c in range(NC)]
        sx = [nc.dram_tensor(f"sx{c}", (NJ * 128, D), F32, kind="Internal").ap() for c in range(NC)]
        so = [nc.dram_tensor(f"so{c}", (NJ * 128, D), F32, kind="Internal").ap() for c in range(NC)]

        psum = [ctx.enter_context(nc.psum_tensor(f"ps{i}", [128, W], F32)) for i in range(8)]

        PS = Slots([Buf(p[:, :]) for p in psum])
        TL = Slots([Buf(tiles[:, i * W:(i + 1) * W]) for i in range(NTILE)])
        SR = Slots([Buf(s) for s in S_buf])
        R3 = Slots([])
        VX = Slots([Buf(v[:, :, :, :]) for v in vext])

        def PEop(fn, cost, deps):
            return Op([("PE", fn, cost, None, None)], deps)

        def MM(chains, deps, passes=4, zero=True):
            cost = 0
            for out, prods in chains:
                cost += sum(max(passes * width(r) / 2.4, 27 * passes) + 3 for _, r in prods)

            def fn(e):
                for out, prods in chains:
                    for i, (l, r) in enumerate(prods):
                        last = e.matmul(out, l, r, start=(i == 0), stop=(i == len(prods) - 1))
                return last
            return PEop(fn, cost, deps)

        def MMadd(prods, deps, stop=False, start=False):
            cost = sum(4 * width(r) / 2.4 + 3 for _, _, r in prods)

            def fn(e):
                for i, (o, l, r) in enumerate(prods):
                    last = e.matmul(o, l, r, start=start and i == 0, stop=stop and i == len(prods) - 1)
                return last
            return PEop(fn, cost, deps)

        def MMsum(prods, deps, left):
            at = []

            def queued():
                at.append(left[0])
                left[0] -= 1

            def fn(e):
                for i, (o, l, r) in enumerate(prods):
                    last = e.matmul(o, l, r, start=at[0] == left[1] and i == 0, stop=at[0] == 1 and i == len(prods) - 1)
                return last
            return Op([("PE", fn, sum(4 * width(r) / 2.4 + 3 for _, _, r in prods), None, None)], deps, queued)

        def TR(pairs, deps):
            def fn(e):
                for o, i in pairs:
                    last = e.transpose(o, i, V["ident"])
                return last
            return PEop(fn, len(pairs) * 107, deps)

        def AC(out, in_, func, deps, bias=0.0, scale=1.0, accum=None):
            f = getattr_act(func)

            def fn(e):
                if accum is not None:
                    return e.activation(out, in_, f, bias=bias, scale=scale, accum_out=accum)
                return e.activation(out, in_, f, bias=bias, scale=scale)
            cost = 70 + width(out) / 1.2 + 93 * (sum(not isinstance(x, float) for x in (bias, scale)) + (accum is not None))
            return Op([("ACT", fn, cost, SETS.get(func), None)], deps)

        def vec(fn, out, deps, eng, n=None, rate=1.0, more=0):
            n = n or width(out)
            c = {"DVE": 68 + more + rate * n / 0.96, "POOL": 120 + more + n * (3.5 if rate < 1 else 2.15)}
            return Op([(g, fn, c[g], None, None) for g in eng], deps)

        def fast(*aps):
            return 0.5 if all("PSUM" not in str(x.space) for x in aps) else 1.0

        def TS(out, a, s1, s2, op0, op1, deps, eng=("DVE",), rate=1.0):
            rate, more = fast(out, a), 60 * sum(not isinstance(x, float) for x in (s1, s2) if x is not None)
            if op1 is None:
                return vec(lambda e: e.tensor_scalar(out, a, s1, None, op0), out, deps, eng, rate=rate, more=more)
            return vec(lambda e: e.tensor_scalar(out, a, s1, s2, op0, op1), out, deps, eng, rate=rate, more=more)

        def TT(out, a, b, op, deps, eng=("DVE",)):
            return vec(lambda e: e.tensor_tensor(out, a, b, op), out, deps, eng)

        def STT(out, a, s, b, op0, op1, deps):
            return vec(lambda e: e.scalar_tensor_tensor(out=out, in0=a, scalar=s, in1=b, op0=op0, op1=op1),
                       out, deps, ("DVE",), more=0 if isinstance(s, float) else 60)

        def CP(out, a, deps, eng=("DVE",)):
            return vec(lambda e: e.tensor_copy(out, a), out, deps, eng, rate=fast(out, a))

        def EV(out, a, deps):
            return Op([("ACT", lambda e: e.activation(out, a, ACT.Copy), 60 + width(out) / 1.2, None, None),
                       ("DVE", lambda e: e.tensor_copy(out, a), 68 + width(out) / 0.96, None, None)], deps)

        def MULP(out, p, a, pdeps, adeps):
            n = width(out)
            copy = ("ACT", lambda e: e.activation(out, p, ACT.Copy), 60 + n / 1.2, None, None)
            mul = ("POOL", lambda e: e.tensor_tensor(out, out, a, ALU.mult), 120 + n * 2.15, None, None)
            one = ("DVE", lambda e: e.tensor_tensor(out, p, a, ALU.mult), 68 + n / 0.96, None, None)
            return Op([one, [(copy, pdeps), (mul, adeps)]], pdeps + adeps)

        def RED(out, a, op, deps, negate=False):
            return vec(lambda e: e.tensor_reduce(out, a, AX.X, op, negate=negate), a, deps, ("DVE",))

        def many(fns, n, deps, eng=("DVE",), more=0):
            def fn(e):
                for f in fns:
                    last = f(e)
                return last
            return Op([(g, fn, len(fns) * (70 if g == "DVE" else 120) + n * (1.04 if g == "DVE" else 2.0) + more, None, None)
                       for g in eng], deps)

        def DMA(out, in_, key, deps, size):
            return Op([("SP", lambda e: e.dma_start(out, in_), 2000 + size / 180.0, None, key)], deps)

        def three(parts, src, n, deps):
            a = yield vec(lambda e: e.tensor_copy(parts[0:96, :], src[0:96, :]), parts, deps, ("DVE",))
            for k in (64, 32):
                a = yield vec(lambda e, k=k: e.tensor_tensor(src[0:k, :], src[0:k, :], parts[0:k, :], ALU.subtract), parts, [a], ("DVE",))
                a = yield vec(lambda e, k=k: e.tensor_copy(parts[0:k, :], src[0:k, :]), parts, [a], ("DVE",))
            return a

        def GATHER(out, rows, ix, key, deps, size):
            return Op([("POOL", lambda e: e.indirect_dma_start(out, None, rows, bass.IndirectOffsetOnAxis(ap=ix, axis=0)),
                        3000 + size / 250.0, None, key)], deps)

        def SCATTER(rows, ix, in_, key, deps, size):
            return Op([("POOL", lambda e: e.indirect_dma_start(rows, bass.IndirectOffsetOnAxis(ap=ix, axis=0), in_, None),
                        3000 + size / 250.0, None, key)], deps)

        BOTH = ("DVE", "POOL")
        take = lambda pool, k=1: ("take", pool, k)

        load = {}
        done = {}
        xt = [None] * NC
        hTt, Vt = [None] * NC, [None] * NC
        L0A_last, L0F_last, lent, begun = [], [], [], []
        c2t, c3t = {}, {}

        def tile4(b):
            return b.rearrange("p (t n) -> p t n", t=4)

        def tl(ap, i):
            return ap[:, i * 128:(i + 1) * 128]

        tbase = {}
        at = 0
        for name, n in TEMP:
            tbase[name] = (at, n)
            at += n
        NTEMP = -(-at // W)
        wmod = tiles[:, 0:3072].rearrange("p (l n) -> p l n", l=4)
        wqkv = tiles[0:16, 3072:6144].rearrange("p (h n) -> p h n", h=24)
        proj = tiles[0:16, 6144:7168].rearrange("p (h n) -> p h n", h=8)

        def loads():
            tmp = TL.take(NTEMP)
            xv = x_d.rearrange("a (n p) d -> p (a n) d", p=128)
            load["c0"] = yield DMA(G["c0"][:, :], pk["c0"], "d_c0", [], 128 * 4 * GROUP_COLS["c0"])
            xt[0] = [(yield DMA(xs[:, 0:4, :], xv[:, 0:4, :], "d_x0", [], 1 << 18))]
            load["wmod0"] = yield DMA(tiles[:, 0:768], temps["wmod"][:, 0:768], "d_wmod0", [], 128 * 4 * 768)
            load["a0"] = yield DMA(G["a0"][:, :], pk["a0"], "d_a0", [], 128 * 4 * GROUP_COLS["a0"])
            for c in range(1, NC):
                xt[c] = [(yield DMA(xs[:, 4 * c:4 * c + 4, :], xv[:, 4 * c:4 * c + 4, :], f"d_x{c}", [], 1 << 18))]
            load["f0"] = yield DMA(G["f0"][:, :], pk["f0"], "d_f0", [], 128 * 4 * GROUP_COLS["f0"])
            load["wmod"] = yield DMA(tiles[:, 768:3072], temps["wmod"][:, 768:3072], "d_wmod", [], 128 * 4 * 2304)
            a = yield DMA(tiles[0:16, 3072:6144], temps["wqkv"], "d_wqkv", [], 16 * 4 * 3072)
            b = yield DMA(tiles[0:16, 6144:7168], temps["proj"], "d_proj", [], 16 * 4 * 1024)
            load["qkv"] = [a, b]
            for g in ("l1", "l2", "l3"):
                load[g] = yield DMA(G[g][:, :], pk[g], "d_" + g, [], 128 * 4 * GROUP_COLS[g])
            load["tmp"] = tmp

        def prep():
            yield ("until", lambda: "wmod0" in load)
            lc, lw = load["c0"], load["wmod0"]
            a = yield CP(identb[:, :], V["ident"], [lc])
            done["identb"] = a
            a = yield vec(lambda e: e.memset(pc[:, 0:1], -0.5), pc[:, 0:1], [], ("POOL",))
            done["half"] = a
            a = yield AC(pc[:, 4:8], V["ccol"], "Tanh", [lc], scale=0.5)
            a = yield STT(pc[:, 8:12], pc[:, 4:8], 1.0, V["ccol"], ALU.add, ALU.mult, [a])
            a = yield TS(pc[:, 12:16], pc[:, 8:12], 0.5, None, ALU.mult, None, [a])
            sc = pc[:, 12:16]
            (b,) = yield take(PS)
            mc3 = mc[:, :].rearrange("p (l s) -> p l s", l=4)

            def columns(ls, deps):
                t = yield MM([(b.ap[:, 6 * l + s:6 * l + s + 1], [(wmod[:, l, 128 * s:128 * s + 128], sc[:, l:l + 1])])
                              for l in ls for s in range(6)], deps)
                t2 = yield CP(mc[:, 6 * ls[0]:6 * ls[-1] + 6], b.ap[:, 6 * ls[0]:6 * ls[-1] + 6], [t])
                m = mc3[:, ls[0]:ls[-1] + 1, 1:5:3]
                return (yield TS(m, m, 1.0, None, ALU.add, None, [t2])), t2

            t3, t2 = yield from columns([0], [a, lw] + b.w)
            done["mc0"] = t3
            t4 = yield TS(pc[:, 16:17], mc[:, 5:6], 0.0, 2.0, ALU.is_ge, ALU.mult, [t3])
            t5 = yield STT(pc[:, 17:18], pc[:, 16:17], -1.0, mc[:, 5:6], ALU.add, ALU.mult, [t4])
            t5 = yield TS(pc[:, 17:18], pc[:, 17:18], 0.25, None, ALU.max, None, [t5])
            done["gcol"] = yield STT(pc[:, 18:19], pc[:, 16:17], -1.0, pc[:, 17:18], ALU.add, ALU.mult, [t4, t5])
            g0 = b.ap[:, 128:256]
            t = yield MM([(g0, [(sc[:, 0:1].broadcast_to([128, 128]), wmod[:, 0, 256:384])])], [a, lw, t2])
            (m,) = yield take(TL)
            t5 = yield TS(gate0[:, :], g0, 0.0, 2.0, ALU.is_ge, ALU.mult, [t])
            t6 = yield STT(m.ap[:, 0:128], gate0[:, :], -1.0, g0, ALU.add, ALU.mult, [t5] + m.w)
            t6 = yield TS(m.ap[:, 0:128], m.ap[:, 0:128], 0.25, None, ALU.max, None, [t6])
            done["gate0"] = yield STT(gate0[:, :], gate0[:, :], -1.0, m.ap[:, 0:128], ALU.add, ALU.mult, [t6])
            TL.give(m, [done["gate0"]])
            yield ("rank", LATER)
            yield ("until", lambda: "wmod" in load)
            lw = load["wmod"]
            t3, t2 = yield from columns([1, 2, 3], [a, lw, t6])
            done["mc"] = t3
            PS.give(b, [t2])
            bs = yield take(PS, 2)
            GT = yield take(TL, 3)
            for k, seg in enumerate((2, 5)):
                ch = [(tl(bs[k].ap, l), [(sc[:, l:l + 1].broadcast_to([128, 128]), wmod[:, l, 128 * seg:128 * seg + 128])])
                      for l in range(4)]
                t = yield MM(ch, [a, lw, load["wmod0"]] + bs[k].w)
                ge = tile4(GT[k].ap)
                (m,) = yield take(TL)
                t2 = yield TS(ge, tile4(bs[k].ap), 0.0, 2.0, ALU.is_ge, ALU.mult, [t] + GT[k].w)
                t3 = yield STT(tile4(m.ap), ge, -1.0, tile4(bs[k].ap), ALU.add, ALU.mult, [t2] + m.w)
                t3 = yield TS(m.ap, m.ap, 0.25, None, ALU.max, None, [t3])
                t4 = yield STT(ge, ge, -1.0, tile4(m.ap), ALU.add, ALU.mult, [t3])
                TL.give(m, [t4])
                PS.give(bs[k], [t2, t3])
                done["G%d" % k] = t4
            tw = [t]
            GA = lambda l: tl(GT[0].ap, l)
            GB = lambda l: tl(GT[1].ap, l)
            ga, gb = done["G0"], done["G1"]
            used = []
            a = yield vec(lambda e: e.memset(oneb[:, :], 1.0), oneb[:, :], [], ("DVE",))
            done["oneb"] = a
            a = yield vec(lambda e: e.memset(zerob[:, :], 0.0), zerob[:, :], [], ("DVE",))
            done["zerob"] = a
            done["vones"] = []
            for v in vext:
                a = yield vec(lambda e, v=v: e.memset(v[:, :, :, 16:17], 1.0), v[:, :, :, 16], [], ("POOL",))
                done["vones"].append(a)
            yield ("until", lambda: "f0" in load)
            lf = load["f0"]
            a = yield AC(pc[:, 20:21], V["sw"], "Tanh", [lf], scale=0.5)
            t1 = yield TS(pc[:, 21:22], pc[:, 20:21], 0.5, 0.5, ALU.mult, ALU.add, [a])
            t2 = yield TS(pc[:, 22:23], pc[:, 20:21], -0.5, 0.5, ALU.mult, ALU.add, [a])
            t3 = yield TS(pc[:, 23:24], pc[:, 20:21], -0.5, -0.5, ALU.mult, ALU.add, [a])
            t4 = yield TS(pc[:, 24:25], V["bh2"], 0.5, None, ALU.mult, None, [lf])
            t5 = yield TS(pc[:, 25:26], V["iw"], 0.5, None, ALU.mult, None, [lf])
            done["f0c"] = [t1, t2, t3, t4, t5]
            a = yield CP(threeb[:, :], V["three"][0:96, :], [lc])
            at = sum(n for _, n in SPEC[2][1][:[k for k, _ in SPEC[2][1]].index("eb2a")])
            done["eb2"] = yield from three(eb2[:, :], G["f0"][0:96, at:at + 768], 768, [lf])
            done["three"] = yield CP(pickb[:, :].rearrange("p (e n) -> p e n", e=16),
                                     V["three"][0:96, 0:16].unsqueeze(2).broadcast_to([96, 16, 64]), [a])
            a = yield TS(trib[:, :], V["mask"], 0.0, None, ALU.is_lt, None, [lc])
            a = yield TT(trib[:, :], trib[:, :], V["ident"], ALU.subtract, [a])
            b = yield TS(edge[:, :], V["iota"], 128.0, None, ALU.mult, None, [lc])
            done["route"] = [a, b]
            (z,) = yield take(TL)
            a = yield vec(lambda e: e.memset(z.ap[:, 0:128], 0.0), z.ap[:, 0:128], z.w, ("DVE",))
            done["blank"] = []
            for c in range(NC):
                t = yield DMA(sx[c].rearrange("(p n) d -> p n d", n=NJ), z.ap[:, 0:128].unsqueeze(1).broadcast_to([128, NJ, 128]),
                              f"d_z{c}", [a], NJ << 16)
                done["blank"].append(t)
            TL.give(z, done["blank"])
            yield ("until", lambda: "tmp" in load)
            ts = []
            for k in range(2):
                for half in range(2):
                    (b,) = yield take(PS)
                    t = yield MM([(tl(b.ap, j), [(wqkv[:, 8 * k + 4 * half + j, :], proj[:, 4 * half + j, :])])
                                  for j in range(4)], load["qkv"] + b.w)
                    o = 8 * k + 4 * half
                    t2 = yield CP(CQ[:, o:o + 4, :], tile4(b.ap), [t])
                    PS.give(b, [t2])
                    ts.append(t2)
                    tw.append(t)
            done["CQ"] = ts
            for b in load["tmp"]:
                TL.give(b, tw)
            l1 = load["l1"]
            a = yield TT(V["wo1"], V["wo1"], GA(1), ALU.mult, [l1, ga], BOTH)
            b = yield TT(V["bo1"], V["bo1"], GA(1), ALU.mult, [l1, ga], BOTH)
            done["L1A"] = [a, b]
            used += [a, b]
            gw1, gw2 = tl(GT[2].ap, 0), tl(GT[2].ap, 1)
            h1 = yield CP(gw1, GB(1), [gb] + GT[2].w, BOTH)
            w = V["wou"].rearrange("p (k n) -> p k n", k=2)
            a = yield TT(w, w, gw1.unsqueeze(1).broadcast_to([128, 2, 128]), ALU.mult, [l1, h1], BOTH)
            w = V["w21"].rearrange("p (k n) -> p k n", k=16)
            b = yield TT(w, w, gw1.unsqueeze(1).broadcast_to([128, 16, 128]), ALU.mult, [l1, h1], ("POOL",))
            done["L1F"] = [a, b]
            used += [a, b]
            l2 = load["l2"]
            (p,) = yield take(PS)
            t = yield MM([(p.ap[:, 0:128], [(V["bet"].broadcast_to([128, 128]), V["wo2"])])], [l2] + p.w)
            t2 = yield TT(brow2[:, :], p.ap[:, 0:128], GA(2), ALU.mult, [t, ga])
            PS.give(p, [t2])
            t3 = yield STT(V["wo2"], V["wo2"], V["gam"], GA(2), ALU.mult, ALU.mult, [l2, t, ga])
            done["L2A"] = [t2, t3]
            h2 = yield TS(gw2, GB(2), 1.0 / 1.702, None, ALU.mult, None, [gb] + GT[2].w)
            w = V["dwn"].rearrange("p (k n) -> p k n", k=8)
            a = yield TT(w, w, gw2.unsqueeze(1).broadcast_to([128, 8, 128]), ALU.mult, [l2, h2], ("POOL",))
            b = yield TT(V["dbn"][64:80, :], V["dbn"][64:80, :], GB(2)[64:80, :], ALU.mult, [l2, gb])
            c = yield TS(V["ub"], V["ub"], 1.0, None, ALU.add, None, [l2], BOTH)
            done["L2F"] = [a, b, c]
            used += [t2, t3, a, b]
            l3 = load["l3"]
            t1 = yield AC(Acol[:, :], V["alog"], "Exp", [l3])
            t2 = yield TS(Acol[:, :], Acol[:, :], -1.0, None, ALU.mult, None, [t1])
            t3 = yield TS(V["wo3"], V["wo3"], 0.5, None, ALU.mult, None, [l3], BOTH)
            t3 = yield TT(V["wo3"], V["wo3"], GA(3), ALU.mult, [t3, ga], BOTH)
            t4 = yield TT(V["bo3"], V["bo3"], GA(3), ALU.mult, [l3, ga], BOTH)
            t5 = yield TS(V["bz"], V["bz"], 0.5, None, ALU.mult, None, [l3], BOTH)
            done["L3A"] = [t2, t3, t4, t5]
            t6 = yield CP(gate7[:, :], GB(3), [gb], BOTH)
            done["L3F"] = [t6, l3]
            for b in GT:
                TL.give(b, used + [t3, t4, t6])

        def norm(c, k, deps, keep=False):
            l, half = divmod(k, 2)
            st = sm[c][:, 0:24].rearrange("p (t n) -> p t n", t=4)
            mv = sm[c][:, 24:32].rearrange("p (t n) -> p t n", t=4)
            rs = sm[c][:, 32:36]
            a = yield many([lambda e, i=i: e.bn_stats(st[:, i, :], xs[:, 4 * c + i, :]) for i in range(4)], 512, xt[c])
            a = yield many([lambda e, i=i: e.bn_aggr(mv[:, i, :], st[:, i, :]) for i in range(4)], 104, [a])
            b = yield TS(rs, mv[:, :, 1], 1e-5, None, ALU.add, None, [a], ("POOL",))
            b = yield vec(lambda e: e.tensor_tensor(rs, rs, pc[:, 0:1].broadcast_to([128, 4]), ALU.pow), rs, [b, done["half"]], ("POOL",), more=830)
            (xn,) = yield take(TL)
            nm = sm[c][:, 36:40]
            b2 = yield TT(nm, mv[:, :, 0], rs, ALU.mult, [b], ("POOL",))
            b2 = yield TS(nm, nm, -1.0, None, ALU.mult, None, [b2], ("POOL",))

            def on_vector(e):
                for i in range(4):
                    last = e.tensor_scalar(tl(xn.ap, i), xs[:, 4 * c + i, :], mv[:, i, 0:1], rs[:, i:i + 1], ALU.subtract, ALU.mult)
                return last

            def on_scalar(e):
                for i in range(4):
                    last = e.activation(tl(xn.ap, i), xs[:, 4 * c + i, :], ACT.Identity, bias=nm[:, i:i + 1], scale=rs[:, i:i + 1])
                return last
            t = yield Op([("DVE", on_vector, 1030, None, None), ("ACT", on_scalar, 1460, None, None)], [b, b2] + xn.w)
            (p,) = yield take(PS)
            t2 = yield TR([(tl(p.ap, i), tl(xn.ap, i)) for i in range(4)], [t, load["c0"]] + p.w)
            if not keep:
                TL.give(xn, [t2])
            if deps is None:
                dst, w = hT0[:, c * W:(c + 1) * W], []
                h = Buf(dst)
            else:
                (h,) = yield take(TL)
                dst, w = h.ap, h.w
            o = 6 * l + 3 * half
            mod = "mc" if l else "mc0"
            yield ("until", lambda: mod in done)
            t3 = yield AC(dst, p.ap, "Identity", [t2, done[mod]] + w, bias=mc[:, o:o + 1], scale=mc[:, o + 1:o + 2])
            PS.give(p, [t3])
            return (h, t3, t, xn, t2) if keep else (h, t3, t)

        def topk(c, E, lg, t):
            s = sm[c]
            mx = s[:, 100:132].rearrange("p (t n) -> p t n", t=4)
            ix = smu[c][:, :].rearrange("p (t n) -> p t n", t=4)
            ixf = s[:, 132:140].rearrange("p (t n) -> p t n", t=4)
            w = s[:, 140:148].rearrange("p (s t) -> p s t", s=2)
            oh = s[:, 160:160 + 8 * E].rearrange("p (t s n) -> p t s n", t=4, s=2)
            a = yield many([lambda e, i=i: e.max(mx[:, i, :], lg[:, i, :]) for i in range(4)], 4 * E, [t])
            b = yield many([lambda e, i=i: e.max_index(ix[:, i, :], mx[:, i, :], lg[:, i, :]) for i in range(4)], 8 * E, [a])
            b = yield CP(ixf, ix[:, :, 0:2], [b])
            io = V["iota"][:, 0:E].unsqueeze(1).broadcast_to([128, 4, E])
            o0 = yield TT(oh[:, :, 0, :], io, ixf[:, :, 0:1].broadcast_to([128, 4, E]), ALU.is_equal, [b])
            o1 = yield TT(oh[:, :, 1, :], io, ixf[:, :, 1:2].broadcast_to([128, 4, E]), ALU.is_equal, [b])
            a = yield TT(w[:, 1, :], mx[:, :, 1], mx[:, :, 0], ALU.subtract, [a])
            a = yield AC(w[:, 1, :], w[:, 1, :], "Exp", [a])
            d = yield TS(w[:, 0, :], w[:, 1, :], 1.0, None, ALU.add, None, [a])
            d = yield vec(lambda e: e.reciprocal(w[:, 0, :], w[:, 0, :]), w[:, 0, :], [d], ("DVE",))
            d = yield TT(w[:, 1, :], w[:, 1, :], w[:, 0, :], ALU.mult, [d])
            return oh, w, [o0, o1, d]

        def weights(c, E, oh, w, ts):
            s = sm[c]
            se = s[:, 300:300 + 4 * E].rearrange("p (t n) -> p t n", t=4)
            s2 = s[:, 364:364 + 4 * E].rearrange("p (t n) -> p t n", t=4)
            a = yield TT(se, oh[:, :, 0, :], w[:, 0, :].unsqueeze(2).broadcast_to([128, 4, E]), ALU.mult, ts)
            b = yield TT(s2, oh[:, :, 1, :], w[:, 1, :].unsqueeze(2).broadcast_to([128, 4, E]), ALU.mult, ts)
            a = yield TT(se, se, s2, ALU.add, [a, b])
            return se, a

        def project_out(c, a, t, w, ws):
            (p,) = yield take(PS)
            t2 = yield MM([(tl(p.ap, i), [(tl(a, i), w)]) for i in range(4)], t + ws + p.w)
            xc = xs[:, 4 * c:4 * c + 4, :]
            t3 = yield TT(xc, tile4(p.ap), xc, ALU.add, [t2] + xt[c])
            PS.give(p, [t3])
            xt[c] = [t3]
            return t2

        def turned(src, t):
            (p,) = yield take(PS)
            t2 = yield TR([(tl(p.ap, i), tl(src.ap, i)) for i in range(4)], t + p.w)
            TL.give(src, [t2])
            (o,) = yield take(TL)
            t3 = yield EV(o.ap, p.ap, [t2] + o.w)
            PS.give(p, [t3])
            return o, t3

        def bias_rows(c, row, t):
            xc = xs[:, 4 * c:4 * c + 4, :]
            a = yield TT(xc, xc, row.unsqueeze(1).broadcast_to([128, 4, 128]), ALU.add, t + xt[c], ("POOL",))
            xt[c] = [a]

        def L0A(c):
            yield ("reserve", TL, ROOM["L0A"])
            yield ("until", lambda: xt[c] is not None and "a0" in load and "half" in done)
            h, th, _ = yield from norm(c, 0, None)
            hTt[c] = th
            h = h.ap
            wd = load["a0"]
            p = yield take(PS, 3)
            t1 = yield MM([(p[0].ap, [(V["wdec"], h)])], [th, wd] + p[0].w)
            (qT,) = yield take(TL)
            tq = yield EV(qT.ap, p[0].ap, [t1] + qT.w)
            t2 = yield MM([(tl(p[1].ap, i), [(tl(h, i), V["w2o"])]) for i in range(4)], p[1].w + [th, wd])
            Vt[c] = yield EV(Vp[:, 4 * c:4 * c + 4, :], tile4(p[1].ap), [t2])
            t3 = yield MM([(tl(p[2].ap, i), [(tl(h, i), V["w1o"])]) for i in range(4)], p[2].w + [th, wd])
            (Bt,) = yield take(TL)
            tB = yield TT(tile4(Bt.ap), tile4(p[2].ap), V["brow0"].unsqueeze(1).broadcast_to([128, 4, 128]), ALU.add, [t3] + Bt.w)
            PS.give(p[0], [tq])
            PS.give(p[1], [Vt[c]])
            PS.give(p[2], [tB])
            yield ("until", lambda: all(Vt[k] is not None for k in range(c)))
            outs, last_pe = [], []

            def qtile(i):
                s = sm0[4 * c + i]
                (R,) = yield take(SR)
                rw = R.w
                mx = s[:, 0:8]
                parts = []
                for kb in range(c + 1):
                    n = W if kb < c else (i + 1) * 128
                    (p,) = yield take(PS)
                    t = yield MM([(p.ap[:, 0:n], [(tl(qT.ap, i), hT0[:, kb * W:kb * W + n])])], [tq, hTt[kb]] + p.w)
                    free = []
                    m = n if kb < c else n - 128
                    if m:
                        a = yield vec(lambda e, o=R.ap[:, kb * W:kb * W + m], q=p.ap[:, 0:m], z=mx[:, kb:kb + 1]:
                                      e.tensor_scalar(o, q, 0.0, -3.0e38, ALU.add, ALU.max, accum_out=z),
                                      p.ap[:, 0:m], [t] + rw, ("DVE",))
                        free.append(a)
                        parts.append(a)
                    if kb == c:
                        dg = R.ap[:, kb * W + m:kb * W + n]
                        a = yield TT(dg, p.ap[:, m:n], V["mask0" if c == 0 and i == 0 else "mask"], ALU.add, [t] + rw)
                        free.append(a)
                        a = yield RED(mx[:, 5:6], dg, ALU.max, [a])
                        parts.append(a)
                        if not m:
                            a = yield CP(mx[:, kb:kb + 1], mx[:, 5:6], [a])
                            parts.append(a)
                    PS.give(p, free)
                n = c * W + (i + 1) * 128
                nk = n // 128
                a = yield CP(mx[:, c + 1:c + 2], mx[:, 5:6], parts) if c < 4 else None
                a = yield RED(s[:, 8:9], mx[:, 0:c + 2], ALU.max, parts + [a], negate=True)
                te = yield AC(R.ap[:, 0:n], R.ap[:, 0:n], "Exp", parts + [a], bias=s[:, 8:9], accum=s[:, 9:10])
                tr = yield vec(lambda e: e.reciprocal(s[:, 10:11], s[:, 9:10]), s[:, 10:11], [te], ("DVE",))
                last = []
                (O,) = yield take(PS)
                tw = O.w
                o = O.ap[:, 0:128]
                for j0 in range(0, nk, 4):
                    js = range(j0, min(j0 + 4, nk))
                    (p,) = yield take(PS)
                    t = yield TR([(tl(p.ap, j - j0), tl(R.ap, j)) for j in js], [te] + p.w)
                    (PT,) = yield take(TL)
                    t2 = yield EV(PT.ap[:, 0:128 * len(js)], p.ap[:, 0:128 * len(js)], [t] + PT.w)
                    PS.give(p, [t2])
                    pr = [(tl(PT.ap, j - j0), Vp[:, j, :]) for j in js]

                    def fn(e, pr=pr, first=j0 == 0, fin=js[-1] == nk - 1, o=o):
                        for q, (a, b) in enumerate(pr):
                            x = e.matmul(o, a, b, start=first and q == 0, stop=fin and q == len(pr) - 1)
                        return x
                    t3 = yield PEop(fn, len(pr) * 216, [t2] + [Vt[j // 4] for j in js] + tw)
                    TL.give(PT, [t3])
                    last = [t3]
                SR.give(R, [t, te])
                a = yield STT(tl(Bt.ap, i), o, s[:, 10:11], tl(Bt.ap, i), ALU.mult, ALU.add, last + [tr, tB])
                outs.append(a)
                last_pe.extend(last)
                PS.give(O, [a])

            yield from par([qtile(i) for i in range(4)], WIDE["L0A"])
            last = last_pe
            TL.give(qT, last)
            a = yield AC(Bt.ap, Bt.ap, "Tanh", outs)
            yield ("until", lambda: "gate0" in done)
            a = yield TT(tile4(Bt.ap), tile4(Bt.ap), gate0[:, :].unsqueeze(1).broadcast_to([128, 4, 128]), ALU.mult,
                         [a, done["gate0"]], BOTH)
            xc = xs[:, 4 * c:4 * c + 4, :]
            a = yield TT(xc, xc, tile4(Bt.ap), ALU.add, [a] + xt[c], BOTH)
            TL.give(Bt, [a])
            xt[c] = [a]
            TL.promised -= ROOM["L0A"]
            L0A_last.append(last + outs)
            if len(L0A_last) == NC:
                after = [t for ts in L0A_last for t in ts]
                for i in range(16):
                    b = Buf(early[:, i * W:(i + 1) * W])
                    if i < 12:
                        lent.append(b)
                    TL.give(b, after)
                TL.n += 16

        def L0F(c):
            yield ("reserve", TL, ROOM["L0F"])
            yield ("until", lambda: "f0c" in done and "identb" in done and "gcol" in done and "eb2" in done)
            lf = load["f0"]
            fc = done["f0c"]
            I, tI, _ = yield from norm(c, 1, [])
            s = sm[c]
            (p,) = yield take(PS)
            t = yield MM([(p.ap[0:32, :], [(V["wr1"], I.ap)])], [tI, lf] + p.w)
            (g,) = yield take(TL)
            t = yield AC(g.ap[0:32, :], p.ap[0:32, :], "Gelu", [t] + g.w, bias=V["br1"][0:32, :])
            PS.give(p, [t])
            (p,) = yield take(PS)
            t = yield MM([(p.ap[:, 8 * i:8 * i + 8], [(tl(g.ap[0:32, :], i), V["wr2"][0:32, :])]) for i in range(4)], [t] + p.w)
            TL.give(g, [t])
            lg = s[:, 52:84].rearrange("p (t n) -> p t n", t=4)
            t = yield TT(lg, p.ap[:, 0:32].rearrange("p (t n) -> p t n", t=4),
                         V["br2"].unsqueeze(1).broadcast_to([128, 4, 8]), ALU.add, [t])
            PS.give(p, [t])
            oh, w, ts = yield from topk(c, 8, lg, t)
            uw = s[:, 148:156].rearrange("p (s t) -> p s t", s=2)
            tu = yield TS(uw, w, pc[:, 22:23], None, ALU.mult, None, ts + fc)
            (p,) = yield take(PS)
            (X,) = yield take(TL)
            t = yield vec(lambda e: e.memset(X.ap, 0.0), X.ap, X.w, BOTH, rate=0.5)
            t = yield CP(tile4(X.ap).rearrange("p t (r n) -> p t r n", n=32)[:, :, 0:3, 0:16],
                         s[:, 160:224].rearrange("p (t n) -> p t n", t=4).unsqueeze(2).broadcast_to([128, 4, 3, 16]), ts + [t])
            t = yield TR([(tl(p.ap, i), tl(X.ap, i)) for i in range(4)], [t] + p.w)
            TL.give(X, [t])
            mk = yield take(TL, 5)
            halves = [b.ap.bitcast(BF16)[:, 512 * q:512 * q + 512] for b in mk for q in range(2)]
            ohb = halves[8]
            tob = yield EV(ohb, p.ap, [t] + mk[4].w)
            PS.give(p, [tob])
            tm = {}

            def mask(k, m):
                if True:
                    (p,) = yield take(PS)
                    sel = [identb[0:96, 8 * k + 2 * m + q:8 * k + 2 * m + q + 1].broadcast_to([96, 64]) for q in range(2)]
                    t = yield MM([(p.ap[64 * q:64 * q + 64, :], [(sel[q], ohb[0:96, :])]) for q in range(2)],
                                 [tob, done["identb"]] + p.w, passes=1)
                    tm[k, m] = yield EV(halves[4 * k + m], p.ap, [t] + mk[2 * k + m // 2].w)
                    PS.give(p, [tm[k, m]])
                    return t
            tohb = yield from par([mask(k, m) for k in range(2) for m in range(4)], WIDE["mask"])
            U, tU = [], []
            for k in range(2):
                (p,) = yield take(PS)
                t = yield TR([(tl(p.ap, i), uw[:, k, i:i + 1].broadcast_to([128, 128])) for i in range(4)], [tu] + p.w)
                (u,) = yield take(TL)
                t = yield EV(u.ap, p.ap, [t] + u.w)
                PS.give(p, [t])
                U.append(u)
                tU.append(t)
            v, tv = None, []
            ew1 = V["ew1"].rearrange("p (k m n) -> p k m n", k=2, m=4)
            ew2 = V["ew2"].rearrange("p (m n) -> p m n", m=4)
            ws1 = V["ws1"].rearrange("p (k n) -> p k n", k=2)
            wf1 = V["wf1"].rearrange("p (k n) -> p k n", k=2)
            wf2 = V["wf2"].rearrange("p (k n) -> p k n", k=2)
            lastmask = []
            for it in range(2):
                def hidden(m, it=it, v=v, tv=tv, tI=tI):
                    (p,) = yield take(PS)
                    t = yield MM([(p.ap, [(ew1[:, 0, m, :], I.ap)] + ([(ew1[:, 1, m, :], v.ap)] if it else []))],
                                 [tI, lf] + tv + p.w)
                    (b,) = yield take(TL)
                    t = yield AC(b.ap, p.ap, "Gelu", [t] + b.w, bias=V["eb1"][:, m:m + 1])
                    PS.give(p, [t])
                    return b, t
                gg = yield from par([hidden(m) for m in range(4)], 4)
                g, tg = [x[0] for x in gg], [x[1] for x in gg]
                (p,) = yield take(PS)
                t = yield MM([(p.ap[0:64, :], [(ws1[:, 0, :], I.ap)] + ([(ws1[:, 1, :], v.ap)] if it else []))],
                             [tI, lf] + tv + p.w)
                (gs,) = yield take(TL)
                t1 = yield AC(gs.ap[0:64, :], p.ap[0:64, :], "Gelu", [t] + gs.w, bias=V["bs1"][0:64, :])
                PS.give(p, [t1])
                t2 = yield vec(lambda e, gs=gs: e.memset(gs.ap[64:65, :], 1.0), gs.ap, gs.w, ("DVE",), rate=0.5)
                tgs = [t1, t2]
                (err,) = yield take(TL)
                terr = yield TS(err.ap, I.ap, V["mu"], None, ALU.subtract, None, [tI, lf] + err.w, BOTH, rate=0.5)
                gfree = [[] for _ in range(4)]
                def variant(k, it=it, v=v, tv=tv, g=g, tg=tg, gs=gs, tgs=tgs, err=err, terr=terr, gfree=gfree):
                    ps = yield take(PS, 3 if it else 2)
                    cols = (0, 1, 2) if it else (1, 2)
                    if k < 0:
                        tp = []
                        for q, cc in zip(ps, cols):
                            t = yield MM([(q.ap, [(V["ws2"][0:65, 128 * cc:128 * cc + 128], gs.ap[0:65, :])])], tgs + [lf] + q.w)
                            tp.append(t)
                        TL.give(gs, tp)
                    else:
                        for q, cc in zip(ps, cols):
                            at = 384 * k + 128 * cc
                            t = yield PEop(lambda e, q=q, at=at: e.matmul(q.ap, eb2[:, at:at + 128], ohb[0:96, :], start=True, stop=False),
                                           216, [tob, done["eb2"]] + q.w)
                            lastmask.append(t)
                        for m in range(4):
                            (gm,) = yield take(TL)
                            t = yield TT(gm.ap, g[m].ap, halves[4 * k + m], ALU.mult, [tg[m], tm[k, m]] + gm.w, BOTH)
                            gfree[m].append(t)
                            lastmask.append(t)
                            t = yield MMadd([(q.ap, ew2[:, m, 128 * cc:128 * cc + 128], gm.ap) for q, cc in zip(ps, cols)], [t, lf], stop=False) \
                                if m < 3 else PEop(
                                    lambda e, ps=ps, cols=cols, gm=gm: [e.matmul(q.ap, ew2[:, 3, 128 * cc:128 * cc + 128], gm.ap, start=False, stop=True)
                                                                        for q, cc in zip(ps, cols)][-1], 2560, [t, lf])
                            TL.give(gm, [t])
                        tp = [t] * len(ps)
                    pb, pg = ps[-2], ps[-1]
                    tpb, tpg = tp[-2], tp[-1]
                    if it:
                        (T,) = yield take(TL)
                        ta = yield AC(T.ap, ps[0].ap, "Tanh", [tp[0]] + T.w, scale=0.5)
                        PS.give(ps[0], [ta])
                    (Gt,) = yield take(TL)
                    tgt = yield AC(Gt.ap, pg.ap, "Tanh", [tpg] + Gt.w, scale=0.5)
                    PS.give(pg, [tgt])
                    (A,) = yield take(TL)
                    t = yield AC(A.ap, pb.ap, "Abs", [tpb] + A.w)
                    t = yield AC(A.ap, A.ap, "Exp", [t], scale=-1.0)
                    t = yield AC(A.ap, A.ap, "Ln", [t], bias=1.0)
                    t = yield STT(A.ap, pb.ap, 0.0, A.ap, ALU.max, ALU.add, [t])
                    PS.give(pb, [t])
                    t = yield TT(A.ap, A.ap, err.ap, ALU.mult, [t, terr], BOTH)
                    ter, tvr = t, None
                    if it:
                        ta = yield STT(T.ap, T.ap, 1.0, v.ap, ALU.add, ALU.mult, [ta] + tv)
                        tvr = ta
                        t = yield STT(A.ap, T.ap, 0.5, A.ap, ALU.mult, ALU.subtract, [ta, t])
                        TL.give(T, [t])
                        if k < 0:
                            t = yield TS(A.ap, A.ap, pc[:, 21:22], None, ALU.mult, None, [t] + fc, BOTH, rate=0.5)
                        else:
                            t = yield TT(A.ap, A.ap, U[k].ap, ALU.mult, [t, tU[k]], BOTH)
                    elif k < 0:
                        t = yield TS(A.ap, A.ap, pc[:, 23:24], None, ALU.mult, None, [t] + fc, BOTH, rate=0.5)
                    else:
                        t = yield STT(A.ap, A.ap, -1.0, U[k].ap, ALU.mult, ALU.mult, [t, tU[k]])
                    tA = t
                    t = yield STT(Gt.ap, Gt.ap, 1.0, A.ap, ALU.add, ALU.mult, [tgt, tA])
                    return A, tA, Gt, t, ter, tvr, tp[-1]

                vs = yield from par([variant(k) for k in (-1, 0, 1)], WIDE["L0F"])
                for m in range(4):
                    TL.give(g[m], gfree[m])
                vacc, tva, xacc, txa = vs[0][0], [vs[0][1], vs[0][3]], vs[0][2], [vs[0][3]]
                for A, tA, Gt, t, *_ in vs[1:]:
                    tva = [(yield TT(vacc.ap, vacc.ap, A.ap, ALU.add, [tA, t] + tva, BOTH))]
                    txa = [(yield TT(xacc.ap, xacc.ap, Gt.ap, ALU.add, [t] + txa, BOTH))]
                    TL.give(A, tva)
                    TL.give(Gt, txa)
                tA = vs[1][1], vs[2][1]
                ter, tvr, tpl = ([x[j] for x in vs] for j in (4, 5, 6))
                TL.give(err, ter)
                if it:
                    TL.give(v, tvr)
                    TL.give(vacc, tva)
                v, tv = vacc, tva
                t = yield STT(xacc.ap, xacc.ap, 0.05, I.ap, ALU.mult, ALU.add, txa + [tI])
                xn, tx = xacc, t
                (p,) = yield take(PS)
                t = yield MM([(p.ap[0:32, :], [(V["wh1"], xn.ap)])], [tx, lf] + p.w)
                (gh,) = yield take(TL)
                t = yield AC(gh.ap[0:32, :], p.ap[0:32, :], "Gelu", [t] + gh.w, bias=V["bh1"][0:32, :])
                PS.give(p, [t])
                f, tf = [], []
                for m in range(2):
                    (p,) = yield take(PS)
                    a = yield MM([(p.ap, [(wf1[:, m, :], xn.ap)])], [tx, lf] + p.w)
                    (b,) = yield take(TL)
                    a2 = yield AC(b.ap, p.ap, "Gelu", [a] + b.w, bias=V["bf1"][:, m:m + 1])
                    PS.give(p, [a2])
                    f.append(b)
                    tf.append(a2)
                TL.give(xn, [a])
                ps = yield take(PS, 2)
                t = yield MM([(ps[0].ap, [(V["wh2"][0:32, :].broadcast_to([32, 128]), gh.ap[0:32, :])])], [t] + ps[0].w)
                (th_,) = yield take(TL)
                t2 = yield AC(th_.ap, ps[0].ap, "Tanh", [t] + th_.w + fc, bias=pc[:, 24:25], scale=0.5)
                TL.give(gh, [t])
                t = yield MM([(ps[1].ap, [(wf2[:, m, :], f[m].ap) for m in range(2)])], tf + ps[1].w)
                for b in f:
                    TL.give(b, [t])
                (r,) = yield take(TL)
                t3 = yield TS(r.ap, ps[1].ap, V["bf2"], pc[:, 25:26], ALU.add, ALU.mult, [t] + r.w + fc)
                PS.give(ps[0], [t2])
                PS.give(ps[1], [t3])
                t = yield STT(r.ap, th_.ap, 1.0, r.ap, ALU.add, ALU.mult, [t2, t3])
                TL.give(th_, [t])
                tI = yield TT(I.ap, I.ap, r.ap, ALU.add, [t, tI, a, tx], BOTH)
                TL.give(r, [tI])
            for b in mk:
                TL.give(b, lastmask + tohb)
            for u in U:
                TL.give(u, list(tA))
            t = yield TS(I.ap, I.ap, pc[:, 18:19], None, ALU.mult, None, [tI, done["gcol"]], BOTH, rate=0.5)
            (p,) = yield take(PS)
            t = yield TR([(tl(p.ap, i), tl(I.ap, i)) for i in range(4)], [t] + p.w)
            TL.give(I, [t])
            xc = xs[:, 4 * c:4 * c + 4, :]
            t = yield TT(xc, tile4(p.ap), xc, ALU.add, [t] + xt[c])
            PS.give(p, [t])
            xt[c] = [t]
            TL.promised -= ROOM["L0F"]
            L0F_last.append(t)
            if len(L0F_last) == NC:
                for i in range(8):
                    TL.give(Buf(G["f0"][:, i * W:(i + 1) * W]), L0F_last)
                TL.n += 8

        def L1A(c):
            yield ("reserve", TL, ROOM["L1A"])
            yield ("until", lambda: "L1A" in done and "CQ" in done)
            l1 = load["l1"]
            h, th, tx = yield from norm(c, 2, [])
            yield from bias_rows(c, V["bo1"], done["L1A"] + [tx])
            (vx,) = yield take(VX)
            (p,) = yield take(PS)
            t = yield MM([(tl(p.ap, i), [(tl(h.ap, i), V["wv1"])]) for i in range(4)], [th, l1] + p.w)
            tv = [(yield EV(vx.ap[:, :, :, 0:16], p.ap.rearrange("p (t h n) -> p t h n", t=4, h=8), [t] + vx.w))]
            PS.give(p, tv)
            nd = yield take(PS, 2)
            tnd = []
            def head(hd):
                maps = []
                for k in range(2):
                    (p,) = yield take(PS)

                    t = yield MM([(p.ap, [(CQ[:, 8 * k + hd, :], h.ap)])], [th] + done["CQ"] + p.w)
                    (E,) = yield take(TL)
                    t2 = yield Op([("ACT", lambda e, E=E, p=p: e.activation(E.ap, p.ap, ACT.Relu, scale=-1.0), 60 + W / 1.2, None, None),
                                   ("DVE", lambda e, E=E, p=p: e.tensor_scalar(E.ap, p.ap, -1.0, 0.0, ALU.mult, ALU.max), 68 + W / 0.96, None, None)],
                                  [t] + E.w)
                    t2 = yield AC(E.ap, E.ap, "Exp", [t2], scale=-1.0)
                    t2 = yield STT(E.ap, p.ap, 1.0, E.ap, ALU.add, ALU.max, [t2])
                    PS.give(p, [t2])
                    maps.append((E, t2))
                (qf, tq), (kf, tk) = maps
                (p,) = yield take(PS)
                t = yield MM([(tl(p.ap, i), [(tl(kf.ap, i), tl(qf.ap, i))]) for i in range(4)], [tq, tk] + p.w)
                TL.give(qf, [t])
                TL.give(kf, [t])
                (B,) = yield take(TL)
                t = yield MULP(tile4(B.ap), tile4(p.ap), V["block"].unsqueeze(1).broadcast_to([128, 4, 128]), [t] + B.w, [])
                PS.give(p, [t.first])
                t = yield MM([(nd[i // 2].ap[:, (i % 2) * 136 + 17 * hd:(i % 2) * 136 + 17 * hd + 17],
                               [(tl(B.ap, i), vx.ap[:, i, hd, :])]) for i in range(4)],
                             [t] + tv + done["vones"] + nd[0].w + nd[1].w)
                TL.give(B, [t])
                return t

            tnd = yield from par([head(i) for i in range(8)], WIDE["L1A"])
            TL.give(h, tnd)
            VX.give(vx, tnd)
            (o,) = yield take(TL)
            to = []
            for j in range(2):
                z = sm[c][:, 500 + 16 * j:516 + 16 * j].rearrange("p (t n) -> p t n", t=2)
                v4 = nd[j].ap[:, 0:272].rearrange("p (t n k) -> p t n k", t=2, n=8)
                a = yield TS(z, v4[:, :, :, 16], 1e-8, None, ALU.add, None, tnd)
                a = yield vec(lambda e, z=z: e.reciprocal(z, z), z, [a], ("DVE",))
                for i in range(2):
                    b = yield TT(tl(o.ap, 2 * j + i).rearrange("p (n k) -> p n k", n=8), v4[:, i, :, 0:16],
                                 z[:, i, :].unsqueeze(2).broadcast_to([128, 8, 16]), ALU.mult, [a] + o.w)
                    to.append(b)
                PS.give(nd[j], to[-2:])
            oT, t = yield from turned(o, to)
            t = yield from project_out(c, oT.ap, [t], V["wo1"], done["L1A"])
            TL.give(oT, [t])
            TL.promised -= ROOM["L1A"]

        def L1F(c):
            yield ("reserve", TL, ROOM["L1F"])
            yield ("until", lambda: "L1F" in done)
            l1 = load["l1"]
            h, th, tx = yield from norm(c, 3, [])
            s = sm[c]
            (p,) = yield take(PS)
            t = yield MM([(p.ap[:, 10 * i:10 * i + 10], [(tl(h.ap, i), V["wge"])]) for i in range(4)], [th, l1] + p.w)
            lg = s[:, 52:92].rearrange("p (t n) -> p t n", t=4)
            t = yield TT(lg, p.ap[:, 0:40].rearrange("p (t n) -> p t n", t=4),
                         V["bge"].unsqueeze(1).broadcast_to([128, 4, 10]), ALU.add, [t])
            PS.give(p, [t])
            pen = s[:, 92:100].rearrange("p (t n) -> p t n", t=4)
            gd = s[:, 440:444]
            a = yield TT(gd, lg[:, :, 1], lg[:, :, 0], ALU.subtract, [t])
            b0 = yield TT(pen[:, :, 0], lg[:, :, 1], lg[:, :, 0], ALU.is_gt, [t])
            b1 = yield TS(pen[:, :, 1], pen[:, :, 0], 1.0e30, -1.0e30, ALU.mult, ALU.add, [b0])
            b0 = yield TS(pen[:, :, 0], pen[:, :, 0], -1.0e30, None, ALU.mult, None, [b0, b1])
            gp = s[:, 444:448]
            a = yield AC(gd, gd, "Abs", [a])
            a = yield AC(gd, gd, "Exp", [a], scale=-1.0)
            em = s[:, 448:480].rearrange("p (t n) -> p t n", t=4)
            te = yield TT(s[:, 448:480].rearrange("p (t a n) -> p t a n", t=4, a=2),
                          lg[:, :, 2:10].rearrange("p t (a n) -> p t a n", a=2),
                          pen.unsqueeze(3).broadcast_to([128, 4, 2, 4]), ALU.add, [t, b0, b1])
            oh, w, ts = yield from topk(c, 8, em, te)
            mx = s[:, 100:132].rearrange("p (t n) -> p t n", t=4)
            pe = s[:, 300:332].rearrange("p (t n) -> p t n", t=4)
            t = yield TT(pe, em, mx[:, :, 0:1].broadcast_to([128, 4, 8]), ALU.subtract, ts)
            t = yield AC(s[:, 300:332], s[:, 300:332], "Exp", [t])
            den = s[:, 484:488]
            d = yield RED(den, pe, ALU.add, [t])
            d = yield STT(den, gd, 1.0, den, ALU.add, ALU.mult, [d, a])
            d = yield vec(lambda e: e.reciprocal(den, den), den, [d], ("DVE",))
            b = yield TT(oh[:, :, 0, :], oh[:, :, 0, :], oh[:, :, 1, :], ALU.add, ts)
            t = yield TT(pe, pe, oh[:, :, 0, :], ALU.mult, [t, b, d])
            tse = yield TT(pe, pe, den.unsqueeze(2).broadcast_to([128, 4, 8]), ALU.mult, [t, d])

            def swiglu(wt, j):
                ps = yield take(PS, 2)
                t1 = yield MM([(ps[0].ap, [(wt[:, 128 * j:128 * j + 128], h.ap)])], [th, l1] + ps[0].w)
                t2 = yield MM([(ps[1].ap, [(wt[:, 256 + 128 * j:384 + 128 * j], h.ap)])], [th, l1] + ps[1].w)
                (T, u) = yield take(TL, 2)
                a = yield AC(T.ap, ps[0].ap, "Silu", [t1] + T.w)
                PS.give(ps[0], [a])
                a = yield MULP(u.ap, ps[1].ap, T.ap, [t2] + u.w, [a])
                PS.give(ps[1], [a.first])
                TL.give(T, [a])
                return u, a, t2

            both = yield from par([swiglu(V[n], j) for n in ("win", "w11") for j in range(2)], WIDE["swiglu"])
            sh, hh = both[:2], both[2:]
            t2 = [x[2] for x in both]
            TL.give(h, t2)
            wou = V["wou"].rearrange("p (k n) -> p k n", k=2)
            w21 = V["w21"].rearrange("p (k n) -> p k n", k=2)
            wt = done["L1F"]
            (p,) = yield take(PS)
            t = yield MM([(tl(p.ap, i), [(tl(sh[k][0].ap, i), wou[:, k, :]) for k in range(2)]) for i in range(4)],
                         [sh[0][1], sh[1][1]] + wt + p.w)
            TL.give(sh[0][0], [t])
            TL.give(sh[1][0], [t])
            xc = xs[:, 4 * c:4 * c + 4, :]
            t = yield TT(xc, tile4(p.ap), xc, ALU.add, [t] + xt[c])
            PS.give(p, [t])
            def routed(i, tx=t):
                xi = xs[:, 4 * c + i, :]
                for half in range(2):
                    (p,) = yield take(PS)
                    t3 = yield MM([(p.ap, [(tl(hh[k][0].ap, i), w21[:, k, 512 * half:512 * half + 512]) for k in range(2)])],
                                  [hh[0][1], hh[1][1]] + wt + p.w)
                    for e in range(4):
                        tx = yield STT(xi, tl(p.ap, e), pe[:, i, 4 * half + e:4 * half + e + 1], xi, ALU.mult, ALU.add,
                                       [t3, tse, tx])
                    PS.give(p, [tx])
                return tx, t3

            rr = yield from par([routed(i) for i in range(4)], WIDE["routed"])
            fin, t3 = [x[0] for x in rr], [x[1] for x in rr]
            TL.give(hh[0][0], t3)
            TL.give(hh[1][0], t3)
            xt[c] = fin
            TL.promised -= ROOM["L1F"]

        def L2A(c):
            yield ("reserve", TL, ROOM["L2A"])
            yield ("until", lambda: "L2A" in done)
            l2 = load["l2"]
            cs = yield take(TL, 2)
            tc = []
            for k in range(2):
                a = yield DMA(cs[k].ap, cs_d[k, :, c * W:(c + 1) * W], f"d_cs{c}{k}", cs[k].w, 1 << 18)
                tc.append(a)
            h, th, tx = yield from norm(c, 4, [])
            yield from bias_rows(c, brow2[:, :], done["L2A"] + [tx])
            qk = []
            for a, b in (("wk", "wks"), ("wq", "wqs")):
                ps = yield take(PS, 2)
                t1 = yield MM([(ps[0].ap, [(V[a], h.ap)])], [th, l2] + ps[0].w)
                t2 = yield MM([(ps[1].ap, [(V[b], h.ap)])], [th, l2] + ps[1].w)
                (r, r2) = yield take(TL, 2)
                t1 = yield TT(r.ap, ps[0].ap, cs[0].ap, ALU.mult, [t1, tc[0]] + r.w)
                t2 = yield TT(r2.ap, ps[1].ap, cs[1].ap, ALU.mult, [t2, tc[1]] + r2.w)
                PS.give(ps[0], [t1])
                PS.give(ps[1], [t2])
                t = yield TT(r.ap, r.ap, r2.ap, ALU.add, [t1, t2], BOTH)
                TL.give(r2, [t])
                qk.append((r, t))
            TL.give(cs[0], [t1])
            TL.give(cs[1], [t2])
            (kT, tk), (qT, tq) = qk
            (R,) = yield take(PS)
            def state(e):
                (p,) = yield take(PS)
                t = yield MM([(p.ap, [(V["wvr"][:, 128 * e:128 * e + 128], h.ap)])], [th, l2] + p.w)
                tvv = t
                (kv,) = yield take(TL)
                t = yield MULP(kv.ap, p.ap, kT.ap, [t] + kv.w, [tk])
                tkl = t
                PS.give(p, [t.first])
                if c:
                    yield ("until", lambda: (c - 1, e) in c2t)
                init, wi = (carry2[:, c - 1, e:e + 1], [c2t[c - 1, e]]) if c else (0.0, [])
                st = kv
                t = yield vec(lambda en, st=st, kv=kv, init=init: en.tensor_tensor_scan(
                    st.ap, decay.broadcast_to([128, W]), kv.ap, init, ALU.mult, ALU.add),
                    st.ap, [t, l2] + wi, ("DVE",), more=60)
                c2t[c, e] = yield CP(carry2[:, c, e:e + 1], st.ap[:, W - 1:W], [t], ("POOL",))
                t = yield TT(st.ap, st.ap, qT.ap, ALU.mult, [t, tq, c2t[c, e]], BOTH)
                tql = t
                t = yield MM([(tl(R.ap, i).rearrange("p (h e) -> p h e", e=8)[:, :, e], [(tl(st.ap, i), V["ind"])])
                              for i in range(4)], [t] + R.w)
                TL.give(st, [t])
                return tvv, tkl, tql, t

            rr = yield from par([state(e) for e in range(8)], WIDE["L2A"])
            TL.give(h, [x[0] for x in rr])
            TL.give(kT, [x[1] for x in rr])
            TL.give(qT, [x[2] for x in rr])
            t = [x[3] for x in rr]
            s = sm[c]
            nm, vs = s[:, 490:554], s[:, 554:618]
            R3d = R.ap.rearrange("p (g n) -> p g n", n=8)
            a = yield RED(nm, R3d, ALU.add, t)
            a = yield TS(nm, nm, -0.125, None, ALU.mult, None, [a])
            (xc, sq) = yield take(TL, 2)
            x3 = xc.ap.rearrange("p (g n) -> p g n", n=8)
            t = yield TT(x3, R3d, nm.unsqueeze(2).broadcast_to([128, 64, 8]), ALU.add, [a] + xc.w)
            PS.give(R, [t])
            b = yield TT(sq.ap, xc.ap, xc.ap, ALU.mult, [t] + sq.w, BOTH)
            b = yield RED(vs, sq.ap.rearrange("p (g n) -> p g n", n=8), ALU.add, [b])
            TL.give(sq, [b])
            b = yield TS(vs, vs, 0.125, 1e-5, ALU.mult, ALU.add, [b])
            b = yield AC(vs, vs, "Sqrt", [b])
            b = yield vec(lambda e: e.reciprocal(vs, vs), vs, [b], ("DVE",), rate=8)
            t = yield TT(x3, x3, vs.unsqueeze(2).broadcast_to([128, 64, 8]), ALU.mult, [t, b], BOTH)
            oT, t = yield from turned(xc, [t])
            t = yield from project_out(c, oT.ap, [t], V["wo2"], done["L2A"])
            TL.give(oT, [t])
            TL.promised -= ROOM["L2A"]

        def L2F(c):
            yield ("reserve", TL, ROOM["L2F"])
            yield ("until", lambda: "L2F" in done)
            l2 = load["l2"]
            h, th, tx = yield from norm(c, 5, [])
            s = sm[c]
            (p,) = yield take(PS)
            t = yield MM([(p.ap[:, 16 * i:16 * i + 16], [(tl(h.ap, i), V["rw"])]) for i in range(4)], [th, l2] + p.w)
            lg = s[:, 500:564].rearrange("p (t n) -> p t n", t=4)
            t = yield CP(lg, p.ap[:, 0:64].rearrange("p (t n) -> p t n", t=4), [t])
            PS.give(p, [t])
            oh, w, ts = yield from topk(c, 16, lg, t)
            se, tse = yield from weights(c, 16, oh, w, ts)
            (X, SP) = yield take(TL, 2)
            t = yield CP(tile4(X.ap)[:, :, 0:96].rearrange("p t (r n) -> p t r n", n=16),
                         se.unsqueeze(2).broadcast_to([128, 4, 6, 16]), [tse] + X.w)
            (p,) = yield take(PS)
            t = yield TR([(tl(p.ap[0:96, :], i), tl(X.ap, i)[:, 0:96]) for i in range(4)], [t] + p.w)
            t = yield EV(X.ap[0:96, :], p.ap[0:96, :], [t])
            PS.give(p, [t])
            parts = SP.ap.bitcast(BF16)[:, 0:W]
            tsp = yield from three(parts, X.ap, W, [t] + SP.w)
            parts = parts[0:96, :]
            wt = done["L2F"]
            (Y,) = yield take(PS)

            def fn(e):
                e.matmul(Y.ap, zerob[64:80, :], zerob[64:80, 0:1].broadcast_to([16, W]), start=True, stop=False)
                for i in range(4):
                    x = e.matmul(tl(Y.ap, i), tl(X.ap[64:80, :], i), V["dbn"][64:80, :], start=False, stop=False)
                return x
            t = yield PEop(fn, 1100, [tsp, done["zerob"]] + wt + Y.w)
            TL.give(X, [t])
            tpick = []
            gu = V["gup"].rearrange("p (e f a) -> p e f a", e=16, a=2)
            dw = V["dwn"].rearrange("p (k n) -> p k n", k=8)
            tY = t

            def expert(m):
                ps = yield take(PS, 3)
                t1 = yield MM([(ps[0].ap, [(gu[:, 2 * m:2 * m + 2, :, 0], h.ap)])], [th, l2] + ps[0].w)
                t2 = yield MM([(ps[1].ap, [(gu[:, 2 * m:2 * m + 2, :, 1], h.ap)])], [th, l2] + ps[1].w)
                (g, T, u) = yield take(TL, 3)
                t3 = yield MM([(ps[2].ap, [(pickb[:, 128 * m:128 * m + 128], parts)])], [tsp, done["three"]] + ps[2].w, passes=1)
                tpick.append(t3)
                a = yield TS(g.ap, ps[0].ap, V["gb"][:, m:m + 1], 7.0, ALU.add, ALU.min, [t1, l2] + g.w)
                PS.give(ps[0], [a])
                b = yield AC(u.ap, ps[1].ap, "Identity", [t2] + wt + u.w, bias=V["ub"][:, m:m + 1])
                PS.give(ps[1], [b])
                b = yield TS(u.ap, u.ap, -6.0, 8.0, ALU.max, ALU.min, [b], BOTH, rate=0.5)
                a = yield AC(T.ap, g.ap, "Silu", [a] + T.w, scale=1.702)
                b = yield MULP(g.ap, ps[2].ap, u.ap, [t3, a], [b])
                PS.give(ps[2], [b.first])
                TL.give(u, [b])
                a = yield TT(g.ap, g.ap, T.ap, ALU.mult, [a, b], BOTH)
                TL.give(T, [a])
                t = yield MMsum([(tl(Y.ap, i), tl(g.ap, i), dw[:, m, :]) for i in range(4)], [a, tY] + wt, left)
                TL.give(g, [t])
                return t2, t

            left = [8, 0]
            rr = yield from par([expert(m) for m in range(8)], WIDE["L2F"])
            TL.give(SP, tpick)
            TL.give(h, [x[0] for x in rr])
            t = max((x[1] for x in rr), key=lambda x: x.n)
            xc = xs[:, 4 * c:4 * c + 4, :]
            t = yield TT(xc, tile4(Y.ap), xc, ALU.add, [t] + xt[c])
            PS.give(Y, [t])
            xt[c] = [t]
            TL.promised -= ROOM["L2F"]

        def L3A(c):
            yield ("reserve", TL, ROOM["L3A"])
            yield ("until", lambda: "L3A" in done)
            l3 = load["l3"]
            wt = done["L3A"]
            h, th, tx = yield from norm(c, 6, [])
            yield from bias_rows(c, V["bo3"], wt + [tx])
            s = sm[c]
            (p,) = yield take(PS)
            t = yield MM([(p.ap[:, 32 * i:32 * i + 32], [(tl(h.ap, i), V["wbc"])]) for i in range(4)], [th, l3] + p.w)
            bc = s[:, 160:288].rearrange("p (t n) -> p t n", t=4)
            tbc = yield TT(bc, p.ap[:, 0:128].rearrange("p (t n) -> p t n", t=4),
                           V["bbc"].unsqueeze(1).broadcast_to([128, 4, 32]), ALU.add, [t])
            (X, BC) = yield take(TL, 2)
            t = yield CP(tile4(X.ap)[:, :, 0:96].rearrange("p t (r n) -> p t r n", n=32),
                         bc.unsqueeze(2).broadcast_to([128, 4, 3, 32]), [tbc] + X.w)
            t = yield TR([(tl(p.ap[0:96, :], i), tl(X.ap, i)[:, 0:96]) for i in range(4)], [t, tbc])
            t = yield EV(X.ap[0:96, :], p.ap[0:96, :], [t])
            PS.give(p, [t])
            bc3 = BC.ap.bitcast(BF16)[:, 0:W]
            tbc = yield from three(bc3, X.ap, W, [t, done["three"]] + BC.w)
            TL.give(X, [tbc])
            bc3 = bc3[0:96, :]
            ps = yield take(PS, 3)
            t1 = yield MM([(ps[0].ap, [(V["wz"], h.ap)])], [th, l3] + ps[0].w)
            t2 = yield MM([(ps[1].ap, [(V["wdt"], h.ap)])], [th, l3] + ps[1].w)
            t3 = yield MM([(ps[2].ap, [(V["wx"], h.ap)])], [th, l3] + ps[2].w)
            TL.give(h, [t3])
            (tz, dt, dx) = yield take(TL, 3)
            tzt = yield AC(tz.ap, ps[0].ap, "Tanh", [t1] + wt + tz.w, bias=V["bz"], scale=0.5)
            PS.give(ps[0], [tzt])
            ab = yield AC(dt.ap, ps[1].ap, "Abs", [t2] + dt.w, bias=V["bdt"])
            a = yield AC(dt.ap, dt.ap, "Exp", [ab], scale=-1.0)
            a = yield AC(dt.ap, dt.ap, "Ln", [a], bias=1.0)
            b = yield TS(dx.ap, ps[1].ap, V["bdt"], 0.0, ALU.add, ALU.max, [ab] + dx.w)
            PS.give(ps[1], [b])
            tdt = yield TT(dt.ap, dt.ap, dx.ap, ALU.add, [a, b])
            tdx = yield STT(dx.ap, ps[2].ap, V["bx"], dt.ap, ALU.add, ALU.mult, [t3, tdt])
            PS.give(ps[2], [tdx])
            (Y,) = yield take(PS)
            tbl = []

            def state(n):
                (A, db) = yield take(TL, 2)
                ta = yield AC(A.ap, dt.ap, "Exp", [tdt] + wt + A.w, scale=Acol[:, n:n + 1])
                (p,) = yield take(PS)
                t = yield MM([(p.ap, [(threeb[:, n:n + 1].broadcast_to([96, 128]), bc3)])], [tbc] + p.w, passes=1)
                t = yield MULP(db.ap, p.ap, dx.ap, [t] + db.w, [tdx])
                tdl = t
                PS.give(p, [t.first])
                if c:
                    yield ("until", lambda: (c - 1, n) in c3t)
                init, wi = (carry3[:, c - 1, n:n + 1], [c3t[c - 1, n]]) if c else (0.0, [])
                H = db
                t = yield vec(lambda e, A=A, db=db, H=H, init=init: e.tensor_tensor_scan(H.ap, A.ap, db.ap, init, ALU.mult, ALU.add),
                              H.ap, [ta, t] + wi, ("DVE",), more=60)
                ts = t
                c3t[c, n] = yield CP(carry3[:, c, n:n + 1], H.ap[:, W - 1:W], [t], ("POOL",))
                (p,) = yield take(PS)
                t2 = yield MM([(p.ap, [(threeb[:, 16 + n:17 + n].broadcast_to([96, 128]), bc3)])], [tbc] + p.w, passes=1)
                tbl.append(t2)
                t = yield MULP(A.ap, p.ap, H.ap, [t2, ts], [ts])
                PS.give(p, [t.first])
                TL.give(H, [t, c3t[c, n]])
                return ta, tdl, A, t

            def pair(n):
                ta, td, H, t = yield from state(n)
                ta2, td2, H2, t2 = yield from state(n + 1)
                t = yield TT(H.ap, H.ap, H2.ap, ALU.add, [t, t2], BOTH)
                TL.give(H2, [t])
                t = yield MMsum([(Y.ap, V["ident"], H.ap)], [t] + Y.w, left)
                TL.give(H, [t])
                return ta, ta2, td, td2, t

            left = [8, 8]
            rr = yield from par([pair(n) for n in range(0, 16, 2)], WIDE["L3A"])
            TL.give(dt, [y for x in rr for y in x[0:2]])
            TL.give(dx, [y for x in rr for y in x[2:4]])
            TL.give(BC, tbl)
            t = max((x[4] for x in rr), key=lambda x: x.n)
            t = yield STT(tz.ap, tz.ap, 1.0, Y.ap, ALU.add, ALU.mult, [t, tzt])
            PS.give(Y, [t])
            t = yield from project_out(c, tz.ap, [t], V["wo3"], wt)
            TL.give(tz, [t])
            TL.promised -= ROOM["L3A"]

        def places(c, oh, ts):
            s = sm[c]
            ohf = s[:, 160:224]
            a = yield CP(smb[c][:, :], ohf, ts)
            (p,) = yield take(PS)

            def fn(e):
                b = smb[c]
                e.matmul(p.ap[:, 0:64], trib[:, :], b[:, :], start=True, stop=False)
                for k in range(1, 8):
                    e.matmul(p.ap[:, 8 * k:64], oneb[:, 0:128], b[:, 0:64 - 8 * k], start=False, stop=k == 7)
                for k in range(8):
                    x = e.matmul(p.ap[:, 64:72], oneb[:, 0:128], b[:, 8 * k:8 * k + 8], start=k == 0, stop=k == 7)
                return x
            t = yield PEop(fn, 16 * 64, [a, done["oneb"]] + done["route"] + p.w)
            more = s[:, 300:332].rearrange("p (e n) -> p e n", e=8)
            rows, end, first = s[:, 332:340], s[:, 340:348], s[:, 348:356]
            a = yield TT(more, p.ap[:, 64:72].unsqueeze(2).broadcast_to([128, 8, 4]),
                         edge[:, 0:4].unsqueeze(1).broadcast_to([128, 8, 4]), ALU.is_gt, [t])
            a = yield RED(rows, more, ALU.add, [a])
            a = yield TS(rows, rows, 128.0, None, ALU.mult, None, [a])
            a = yield vec(lambda e: e.tensor_tensor_scan(end, oneb[:, 0:8], rows, 0.0, ALU.mult, ALU.add), end, [a], ("DVE",))
            b = yield TT(first, end, rows, ALU.subtract, [a])
            at = s[:, 364:428].rearrange("p (g n) -> p g n", g=8)
            b = yield TT(at, p.ap[:, 0:64].rearrange("p (g n) -> p g n", g=8), first.unsqueeze(1).broadcast_to([128, 8, 8]),
                         ALU.add, [b])
            PS.give(p, [b])
            b = yield TT(at, at, ohf.rearrange("p (g n) -> p g n", g=8), ALU.mult, [b])
            b = yield RED(s[:, 356:364], at, ALU.add, [b])
            b = yield CP(slot[c][:, 0:8], s[:, 356:364], [b])
            over = s[:, 490:490 + 8 * NJ].rearrange("p (j n) -> p j n", j=NJ)
            a = yield TT(over, end.unsqueeze(1).broadcast_to([128, NJ, 8]), edge[:, 0:NJ].unsqueeze(2).broadcast_to([128, NJ, 8]),
                         ALU.is_le, [a])
            a = yield RED(s[:, 428:428 + NJ], over, ALU.add, [a])
            a = yield TS(s[:, 428:428 + NJ], s[:, 428:428 + NJ], 7.0, 128.0, ALU.min, ALU.mult, [a])
            a = yield TS(slot[c][:, 8:8 + NJ], s[:, 428:428 + NJ], V["pio"], None, ALU.add, None, [a])
            return b, a

        def L3F(c):
            yield ("reserve", TL, ROOM["L3F"])
            yield ("until", lambda: "L3F" in done)
            wt = done["L3F"]
            h, th, tx, xn, txn = yield from norm(c, 7, [], keep=True)
            s = sm[c]
            (p,) = yield take(PS)
            t = yield MM([(p.ap[:, 8 * i:8 * i + 8], [(tl(h.ap, i), V["gw"])]) for i in range(4)], [th] + wt + p.w)
            TL.give(h, [t])
            lg = s[:, 52:84].rearrange("p (t n) -> p t n", t=4)
            t = yield CP(lg, p.ap[:, 0:32].rearrange("p (t n) -> p t n", t=4), [t])
            PS.give(p, [t])
            oh, w, ts = yield from topk(c, 8, lg, t)
            tpl, twx = yield from places(c, oh, ts)
            ring = {}

            def stream():
                yield ("until", lambda: sent)
                for j in range(NJ):
                    (b,) = yield take(R3)
                    t = yield GATHER(b.ap, w3_d.rearrange("e p n -> (e p) n"), slot[c][:, 8 + j:9 + j], b.sem, [twx] + b.w, 128 * 4 * 1536)
                    ring[j] = (b, t)

            land = yield take(TL, 4)
            XT, tXT, out, sent = {}, {}, {}, []

            def rows():
                for g in range(8):
                    t = yield SCATTER(sx[c], slot[c][:, g:g + 1], tl(xn.ap, g // 2), f"d_s{c}", [tpl, tx, done["blank"][c]], 1 << 16)
                sent.append(t)
                TL.give(xn, [t, txn])
                for q in range(4):
                    n = min(4, NJ - 4 * q)
                    ld = land[q].ap[:, 0:128 * n]
                    t2 = yield DMA(ld.rearrange("p (j d) -> p j d", j=n),
                                   sx[c][512 * q:512 * q + 128 * n].rearrange("(j p) d -> p j d", p=128), f"d_l{c}{q}", [t] + land[q].w, n << 16)
                    land[q].t = t2
                o = 6 * 3 + 3
                for q in range(4):
                    n = min(4, NJ - 4 * q)
                    (p,) = yield take(PS)
                    t = yield TR([(tl(p.ap, i), tl(land[q].ap, i)) for i in range(n)], [land[q].t] + p.w)
                    TL.give(land[q], [t])
                    (x,) = yield take(TL)
                    t = yield AC(x.ap[:, 0:128 * n], p.ap[:, 0:128 * n], "Identity", [t, done["mc"]] + x.w,
                                 bias=mc[:, o:o + 1], scale=mc[:, o + 1:o + 2])
                    PS.give(p, [t])
                    XT[q], tXT[q] = x, t

            left = {q: min(4, NJ - 4 * q) for q in range(4)}
            hold = {q: [] for q in range(4)}
            tout = {q: [] for q in range(4)}
            back = []

            def expert(j):
                q, i = divmod(j, 4)
                yield ("until", lambda: j in ring and q in XT)
                rb, tr = ring[j]
                w1, w3 = rb.ap[:, 0:512], rb.ap[:, 512:1024]
                w2 = rb.ap[:, 1024:1536].rearrange("p (f n) -> p f n", f=4)
                x = tl(XT[q].ap, i)
                ps = yield take(PS, 2)
                t1 = yield MM([(tl(ps[0].ap, f), [(tl(w1, f), x)]) for f in range(4)], [tXT[q], tr] + ps[0].w)
                t2 = yield MM([(tl(ps[1].ap, f), [(tl(w3, f), x)]) for f in range(4)], [tXT[q], tr] + ps[1].w)
                hold[q].append(t2)
                if len(hold[q]) == left[q]:
                    TL.give(XT[q], hold[q])
                (z, T) = yield take(TL, 2)
                a = yield AC(z.ap, ps[0].ap, "Silu", [t1] + z.w)
                PS.give(ps[0], [a])
                a = yield MULP(T.ap, ps[1].ap, z.ap, [t2] + T.w, [a])
                PS.give(ps[1], [a.first])
                TL.give(z, [a])
                (p,) = yield take(PS)
                t = yield MM([(p.ap[:, 0:128], [(tl(T.ap, f), w2[:, f, :]) for f in range(4)])], [a, tr] + p.w)
                R3.give(rb, [t])
                TL.give(T, [t])
                if q not in out:
                    out[q] = None
                    (out[q],) = yield take(TL)
                yield ("until", lambda: out[q] is not None)
                a = yield TT(tl(out[q].ap, i), p.ap[:, 0:128], gate7[:, :], ALU.mult, [t] + wt + out[q].w)
                PS.give(p, [a])
                tout[q].append(a)
                if len(tout[q]) == left[q]:
                    n = left[q]
                    t = yield DMA(so[c][512 * q:512 * q + 128 * n].rearrange("(j p) d -> p j d", p=128),
                                  out[q].ap[:, 0:128 * n].rearrange("p (j d) -> p j d", j=n), f"d_o{c}{q}", tout[q], n << 16)
                    TL.give(out[q], [t])
                    back.append(t)

            feed = yield ("spawn", [stream(), rows()])
            yield from par([expert(j) for j in range(NJ)], WIDE["L3F"])
            yield ("join", feed)
            r = yield take(TL, 2)
            got = []
            for i in range(4):
                tt = []
                for k in range(2):
                    tt.append((yield GATHER(tl(r[k].ap, i), so[c], slot[c][:, 2 * i + k:2 * i + k + 1], f"d_g{c}{i}{k}", back + r[k].w, 1 << 16)))
                got.append(tt)
            fin = []
            for i in range(4):
                xi = xs[:, 4 * c + i, :]
                a = xt[c]
                for k in range(2):
                    a = [(yield STT(xi, tl(r[k].ap, i), w[:, k, i:i + 1], xi, ALU.mult, ALU.add, [got[i][k]] + a))]
                fin += a
            for k in range(2):
                TL.give(r[k], fin)
            ov = out_d.rearrange("a (n p) d -> p (a n) d", p=128)
            yield DMA(ov[:, 4 * c:4 * c + 4, :], xs[:, 4 * c:4 * c + 4, :], "d_out", fin, 1 << 18)
            TL.promised -= ROOM["L3F"]

        def ring3():
            yield ("until", lambda: begun)
            yield ("reserve", TL, 12)
            for b in lent:
                b.last = True
            yield ("until", lambda: all(b in TL.bufs for b in lent))
            for b in lent:
                TL.bufs.remove(b)
            for i in range(4):
                R3.give(Buf(early[:, 3 * i * W:3 * (i + 1) * W]), [t for b in lent[3 * i:3 * i + 3] for t in b.w])
                R3.bufs[-1].sem = f"r3_{i}"

        decay = sb("decay_sb", [128, 1])

        def consts():
            load["decay"] = yield DMA(decay[:, :], pk["decay"], "d_decay", [], 512)

        def chunk(c):
            layers = (L0A, L0F, L1A, L1F, L2A, L2F, L3A, L3F)
            for layer in layers:
                yield ("rank", RANK[layers.index(layer)] + AGE * c)
                if layer is L3A:
                    begun.append(c)
                if layer is L2A:
                    yield ("until", lambda: "decay" in load)
                yield from layer(c)

        run(Q, [chunk(c) for c in range(NC)] + [loads(), prep(), consts(), ring3()])

        sems = {k: ctx.enter_context(nc.semaphore("s_" + k)) for k in Q.count}
        block = ctx.enter_context(nc.Block())

        def play(name, eng):
            for waits, fn, key, by in Q.items[name]:
                for k, n in waits:
                    eng.wait_ge(sems[k], n)
                fn(eng).then_inc(sems[key], by)

        @block.sync
        def _(eng):
            play("SP", eng)
            eng.wait_ge(sems["d_out"], Q.count["d_out"])

        @block.tensor
        def _(eng):
            play("PE", eng)

        @block.scalar
        def _(eng):
            play("ACT", eng)

        @block.vector
        def _(eng):
            play("DVE", eng)

        @block.gpsimd
        def _(eng):
            play("POOL", eng)


FUNCS = {"Silu": ACT.Silu, "Sqrt": ACT.Sqrt, "Relu": ACT.Relu, "Gelu": ACT.Gelu, "Tanh": ACT.Tanh, "Exp": ACT.Exp, "Ln": ACT.Ln, "Abs": ACT.Abs, "Identity": ACT.Identity}


def getattr_act(name):
    return FUNCS[name]


def _laid_out(d):
    f = np.float32
    col = lambda a: np.asarray(a, f).reshape(-1, 1)
    rows = lambda a: np.broadcast_to(np.asarray(a, f).reshape(1, -1), (128, np.asarray(a).size))
    A = {k: np.asarray(v) for k, v in d.items()}
    p = np.arange(128)
    out = {}
    out["ident"] = np.eye(128, dtype=f)
    out["mask"] = np.where(p[None, :] < p[:, None], 0.0, -1e30).astype(f)
    m0 = out["mask"].copy()
    m0[0, 0] = 0.0
    out["mask0"] = m0
    out["block"] = (p[None, :] // 32 == p[:, None] // 32).astype(f)
    out["iota"] = np.broadcast_to(np.arange(16, dtype=f), (128, 16))
    out["ind"] = (p[:, None] // 8 == np.arange(16)[None, :]).astype(f)
    out["ccol"] = np.concatenate([col(A[f"L{l}_c"]) for l in range(4)], 1)
    out["pio"] = col(p)
    out["three"] = ((p[:, None] % 32 == np.arange(32)[None, :]) & (p[:, None] < 96)).astype(f)
    out["wdec"] = A["L0_attn_w_dec_attn"]
    out["w1o"] = A["L0_attn_w_out"][:, :128].T
    out["w2o"] = A["L0_attn_w_out"][:, 128:].T
    out["brow0"] = rows(A["L0_attn_b_out"])
    F = lambda n: A["L0_ffn_" + n]
    out["wr1"], out["br1"], out["wr2"], out["br2"] = F("w_r1"), col(F("b_r1")), F("w_r2"), rows(F("b_r2"))
    out["wh1"], out["bh1"], out["wh2"], out["bh2"] = F("w_h1"), col(F("b_h1")), F("w_h2"), np.broadcast_to(col(F("b_h2")), (128, 1))
    w = F("expert_w1").reshape(8, 2, 128, 64)
    out["ew1"] = w.transpose(2, 1, 0, 3).reshape(128, 1024)
    out["eb1"] = F("expert_b1").reshape(4, 128).T
    out["ew2"] = F("expert_w2").reshape(4, 128, 384).transpose(1, 0, 2).reshape(128, 1536)
    b2 = F("expert_b2")
    z = np.zeros((8, 384), f)
    thrice = lambda a: np.concatenate([a, np.zeros((16, 384), f)] * 3)
    out["eb2a"], out["eb2b"] = thrice(np.concatenate([b2, z])), thrice(np.concatenate([z, b2]))
    out["ws1"] = F("w_s1").reshape(2, 128, 64).transpose(1, 0, 2).reshape(128, 128)
    out["bs1"] = col(F("b_s1"))
    out["ws2"] = np.concatenate([F("w_s2"), F("b_s2").reshape(1, 384)])
    out["sw"] = np.broadcast_to(col(F("shared_weight")), (128, 1))
    out["wf1"] = F("w_f1")
    out["bf1"] = F("b_f1").reshape(2, 128).T
    out["wf2"] = F("w_f2").reshape(2, 128, 128).transpose(1, 0, 2).reshape(128, 256)
    out["bf2"], out["iw"], out["mu"] = col(F("b_f2")), col(F("integration_weight")), col(F("mu"))
    wq = A["L1_attn_w_qkv"]
    out["wv1"] = wq[256:].T
    out["wo1"], out["bo1"] = A["L1_attn_w_out"].T, rows(A["L1_attn_b_out"])
    F = lambda n: A["L1_ffn_" + n]
    out["win"], out["w11"] = F("w_in").T, F("w1").T
    out["wou"] = F("w_out").T.reshape(2, 128, 128).transpose(1, 0, 2).reshape(128, 256)
    out["w21"] = F("w2").transpose(2, 0, 1).reshape(2, 128, 8, 128).transpose(1, 0, 2, 3).reshape(128, 2048)
    out["wge"] = np.concatenate([F("wg"), F("we")]).T
    out["bge"] = np.concatenate([rows(F("gb")), rows(F("eb"))], 1)
    F = lambda n: A["L2_attn_" + n]
    swap = p ^ 1
    for n, k in (("wq", "WQ"), ("wk", "WK")):
        m = F(k).reshape(128, 128)
        out[n], out[n + "s"] = m.T, m[swap].T
    out["wvr"] = np.repeat(F("WV").transpose(2, 1, 0).reshape(128, 128), 8, axis=1)
    out["wo2"] = F("WO")
    out["gam"], out["bet"] = col(F("gamma")), col(F("beta"))
    F = lambda n: A["L2_ffn_" + n]
    out["rw"] = F("router_weight")
    out["gup"] = F("gate_up_proj").transpose(1, 0, 2).reshape(128, 2048)
    gub = F("gate_up_proj_bias")
    out["gb"], out["ub"] = gub[:, 0::2].reshape(8, 128).T, gub[:, 1::2].reshape(8, 128).T
    out["dwn"] = F("down_proj").reshape(8, 128, 128).transpose(1, 0, 2).reshape(128, 1024)
    out["dbn"] = np.concatenate([np.zeros((64, 128), f), F("down_proj_bias")])
    F = lambda n: A["L3_attn_" + n]
    out["wz"], out["bz"], out["wx"], out["bx"] = F("Wz"), col(F("bz")), F("Wx"), col(F("bx"))
    out["wbc"] = np.concatenate([F("WB"), F("WC")], 1)
    out["bbc"] = np.concatenate([rows(F("bB")), rows(F("bC"))], 1)
    out["wdt"], out["bdt"], out["alog"] = F("Wdt"), col(F("bdt")), F("A_log")
    out["wo3"], out["bo3"] = F("Wout"), rows(F("bout"))
    out["gw"] = A["L3_ffn_gate_w"]

    packs = {}
    for g, items in SPEC:
        cols = []
        for name, n in items:
            a = np.asarray(out[name], f)
            assert a.shape[1] == n, (name, a.shape, n)
            if a.shape[0] < 128:
                a = np.concatenate([a, np.zeros((128 - a.shape[0], n), f)])
            cols.append(a)
        packs["p_" + g] = np.ascontiguousarray(np.concatenate(cols, 1))
    packs["t_wmod"] = np.ascontiguousarray(np.concatenate([A[f"L{l}_wmod"] for l in range(4)], 1))
    packs["t_wqkv"] = np.ascontiguousarray(wq.reshape(24, 16, 128).transpose(1, 0, 2).reshape(16, 3072))
    packs["t_proj"] = np.ascontiguousarray(A["L1_attn_proj"].transpose(1, 0, 2).reshape(16, 1024))
    F = lambda n: A["L3_ffn_" + n]
    packs["w3"] = np.ascontiguousarray(np.concatenate(
        [F("w1"), F("w3"), F("w2").reshape(8, 4, 128, 128).transpose(0, 2, 1, 3).reshape(8, 128, 512)], 2))
    packs["x"] = np.ascontiguousarray(A["L0_attn_hidden_states"])
    ex = np.arange(0, 8, 2, dtype=f) / f(8)
    angle = (f(10.0) ** (f(-4.0) * ex)).astype(f)
    pos = np.arange(S, dtype=f)
    na = (pos[:, None] * angle[None, :]).astype(f)
    pair = (p % 8) // 2
    cosT = np.cos(na.astype(np.float64)).astype(f).T[pair]
    sinT = np.sin(na.astype(np.float64)).astype(f).T[pair]
    sinT = np.where((p % 2 == 0)[:, None], -sinT, sinT).astype(f)
    packs["cs"] = np.ascontiguousarray(np.stack([cosT, sinT]))
    packs["decay"] = np.ascontiguousarray((1.0 - 2.0 ** (-5.0 - (p // 8))).astype(f).reshape(128, 1))
    return packs


def kernel(**inputs):
    import concourse.bacc as _bacc
    from concourse.bass_utils import run_bass_kernel_spmd as _run

    nc = _bacc.Bacc("TRN2", target_bir_lowering=False, num_devices=1)
    arrays = _laid_out(inputs)
    ap = {k: nc.dram_tensor(k, a.shape, F32, kind="ExternalInput").ap() for k, a in arrays.items()}
    out = nc.dram_tensor("out", (1, S, D), F32, kind="ExternalOutput").ap()
    pk = {g: ap["p_" + g] for g, _ in SPEC}
    pk["decay"] = ap["decay"]
    build(nc, ap["x"], ap["cs"], ap["w3"], pk, {k: ap["t_" + k] for k in ("wmod", "wqkv", "proj")}, out)
    r = _run(nc, [arrays], core_ids=[0])
    return r.results[0]["out"]
```
